# Optimizing a Trainium2 kernel written in Bass

```python
import numpy as np
import jax
import jax.numpy as jnp

def _softmax(x, axis=-1):
    return jax.nn.softmax(x, axis=axis)

def _gelu(x):
    return jax.nn.gelu(x, approximate=True)

def _silu(x):
    return jax.nn.silu(x)

def _sigmoid(x):
    return jax.nn.sigmoid(x)

def _layernorm(x, axis=-1, eps=1e-05):
    m = jnp.mean(x, axis=axis, keepdims=True)
    v = jnp.var(x, axis=axis, keepdims=True)
    return (x - m) / jnp.sqrt(v + eps)

def _scatter_add(tgt, idx, src, axis=0):
    return tgt.at[idx].add(src)

def _segment_sum(src, seg, n):
    return jax.ops.segment_sum(src, seg, n)
kernel_name = 'mk_flamingo_gated_d4_seqx_r8_cb185d'

def setup_inputs(seed: int=0):
    np.random.seed(seed)
    _w = jnp.asarray

    def _rec_inputs():
        import jax
        import jax.numpy as jnp
        _rk = jax.random.key(seed)
        x = -0.000125 + 0.9999 * jax.random.normal(jax.random.fold_in(_rk, 1), (4, 256, 256), jnp.float32)
        _lenS = 256 - jax.random.randint(jax.random.fold_in(_rk, 7), (4,), 0, max(1, 256 // 4) + 1, jnp.int32)
        _lenS2 = 64 - jax.random.randint(jax.random.fold_in(_rk, 8), (4,), 0, max(1, 64 // 4) + 1, jnp.int32)
        _ctx_2048P = jax.random.normal(jax.random.fold_in(_rk, 11), (4, 16, 256), jnp.float32)
        _ctx_2048c = jax.random.dirichlet(jax.random.fold_in(_rk, 511), 0.3 * jnp.ones((16,), jnp.float32), (4, 64))
        _ctx_2048t = jnp.einsum('bsk,bkd->bsd', _ctx_2048c, _ctx_2048P)
        _ctx_2048t = _ctx_2048t * jax.lax.rsqrt(jnp.mean(jnp.square(_ctx_2048t)) + 1e-12) * 0.953939
        ctx_2048 = -0.000540021 + 0.99982 * (_ctx_2048t + 0.3 * jax.random.normal(jax.random.fold_in(_rk, 611), (4, 64, 256), jnp.float32))
        itok_BxS_0_1023 = jax.random.randint(jax.random.fold_in(_rk, 12), (4, 256), 0, 128, jnp.int32)
        _validS = jnp.arange(256)[None, :] < _lenS[:, None]
        _validS2 = jnp.arange(64)[None, :] < _lenS2[:, None]
        _causal = jnp.tril(jnp.ones((256, 256), dtype=bool))
        mask_Bx1xSxS_fk0 = jnp.where(jnp.broadcast_to(_validS[:, None, None, :], (4, 1, 256, 256)), -1000000000.0, 0.0).astype(jnp.float32)
        _g = jax.random.normal(jax.random.fold_in(_rk, 9001), (2, 4), jnp.float32)
        _g = jnp.sign(_g) * jnp.maximum(jnp.abs(_g), 1.0) + (_g == 0) * 1.0
        g_xattn = _g[0]
        g_ffn = _g[1]
        return (x, ctx_2048, itok_BxS_0_1023, mask_Bx1xSxS_fk0, g_xattn, g_ffn)
    x, ctx_2048, itok_BxS_0_1023, mask_Bx1xSxS_fk0, g_xattn, g_ffn = _rec_inputs()

    def _L0_xattn_setup():
        import jax, jax.numpy as jnp
        import numpy as np
        DIM = 256
        N_HEADS = 16
        HEAD_DIM = DIM // N_HEADS
        EPS = 1e-06
        IMG_LEN = 257

        def rms_norm(x, g, eps=EPS):
            var = jnp.mean(x * x, axis=-1, keepdims=True)
            return x * jax.lax.rsqrt(var + eps) * g

        def _attend(q, k, v, k_mask=None):
            scale = 1.0 / jnp.sqrt(jnp.asarray(HEAD_DIM, q.dtype))
            scores = jnp.einsum('bqnd,bknd->bnqk', q, k) * scale
            if k_mask is not None:
                neg = jnp.asarray(jnp.finfo(scores.dtype).min, scores.dtype)
                scores = jnp.where(k_mask[:, None, None, :], scores, neg)
            probs = jax.nn.softmax(scores, axis=-1)
            return jnp.einsum('bnqk,bknd->bqnd', probs, v)
        key = jax.random.key(seed)
        ks = jax.random.split(key, 16)
        B, L1, L2 = (1, 2048, 769)
        std = 0.02
        inp = {'x': jax.random.normal(ks[0], (B, L1, DIM), jnp.float32), 'context': jax.random.normal(ks[1], (B, L2, DIM), jnp.float32), 'context_lens': jax.random.randint(ks[2], (B,), 32, 513, jnp.int32), 'Wq': jax.random.normal(ks[3], (DIM, DIM), jnp.float32) * std, 'bq': jnp.zeros((DIM,), jnp.float32), 'gq': jnp.ones((DIM,), jnp.float32), 'Wk': jax.random.normal(ks[4], (DIM, DIM), jnp.float32) * std, 'bk': jnp.zeros((DIM,), jnp.float32), 'gk': jnp.ones((DIM,), jnp.float32), 'Wv': jax.random.normal(ks[5], (DIM, DIM), jnp.float32) * std, 'bv': jnp.zeros((DIM,), jnp.float32), 'Wk_img': jax.random.normal(ks[6], (DIM, DIM), jnp.float32) * std, 'bk_img': jnp.zeros((DIM,), jnp.float32), 'gk_img': jnp.ones((DIM,), jnp.float32), 'Wv_img': jax.random.normal(ks[7], (DIM, DIM), jnp.float32) * std, 'bv_img': jnp.zeros((DIM,), jnp.float32), 'Wo': jax.random.normal(ks[8], (DIM, DIM), jnp.float32) * std, 'bo': jnp.zeros((DIM,), jnp.float32)}
        return inp
    _L0_xattn_all = _L0_xattn_setup()
    _L0_xattn_in = {k: v for k, v in _L0_xattn_all.items() if k in ('context_lens', 'Wq', 'bq', 'gq', 'Wk', 'bk', 'gk', 'Wv', 'bv', 'Wk_img', 'bk_img', 'gk_img', 'Wv_img', 'bv_img', 'Wo', 'bo')}
    del _L0_xattn_all

    def _L0_ffn_setup():
        import jax, jax.numpy as jnp
        import numpy as np

        def _sparsify_2to4(h):
            B, S, I = h.shape
            g = h.reshape(B, S, I // 4, 4)
            a = jnp.abs(g)
            _, idx = jax.lax.top_k(a, 2)
            pos = jnp.arange(4)
            mask = (pos == idx[..., 0:1]) | (pos == idx[..., 1:2])
            return (g * mask.astype(g.dtype)).reshape(B, S, I)
        key = jax.random.key(seed)
        k1, k2, k3, k4 = jax.random.split(key, 4)
        B, S, H, I = (4, 256, 256, 1024)
        x = jax.random.normal(k1, (B, S, H), dtype=jnp.float32)
        w_gate = jax.random.normal(k2, (H, I), dtype=jnp.float32) / np.sqrt(H)
        w_up = jax.random.normal(k3, (H, I), dtype=jnp.float32) / np.sqrt(H)
        w_down = jax.random.normal(k4, (I, H), dtype=jnp.float32) / np.sqrt(I)
        return {'x': x, 'w_gate': w_gate, 'w_up': w_up, 'w_down': w_down}
    _L0_ffn_all = _L0_ffn_setup()
    _L0_ffn_in = {k: v for k, v in _L0_ffn_all.items() if k in ('w_gate', 'w_up', 'w_down')}
    del _L0_ffn_all

    def _L1_xattn_setup():
        import jax, jax.numpy as jnp
        import numpy as np
        B, Lq, Lk = (2, 512, 128)
        Q_DIM, KV_DIM = (256, 256)
        H, HD = (16, 128)
        KVC, QC, R = (64, 96, 64)
        LOOKBACK = 8
        NEG = -1e+30

        def _rope(x, L):
            half = x.shape[-1] // 2
            inv_freq = 1.0 / 10000.0 ** (jnp.arange(half, dtype=jnp.float32) / half)
            ang = jnp.arange(L, dtype=jnp.float32)[:, None] * inv_freq
            cos, sin = (jnp.cos(ang), jnp.sin(ang))
            x1, x2 = (x[..., :half], x[..., half:])
            return jnp.concatenate([x1 * cos - x2 * sin, x1 * sin + x2 * cos], axis=-1)
        key = jax.random.key(seed)
        ks = jax.random.split(key, 11)

        def w(k, shape, fan_in):
            return jax.random.normal(k, shape, jnp.float32) / np.sqrt(fan_in).astype(np.float32)
        return {'q': jax.random.normal(ks[0], (B, Lq, Q_DIM), jnp.float32), 'kv': jax.random.normal(ks[1], (B, Lk, KV_DIM), jnp.float32), 'seg_id': jnp.sort(jax.random.randint(ks[2], (B, Lq), 0, Lk), axis=-1), 'W_kvc': w(ks[3], (KV_DIM, KVC), KV_DIM), 'W_dq': w(ks[4], (Q_DIM, QC), Q_DIM), 'W_uq': w(ks[5], (QC, H * HD), QC), 'W_qr': w(ks[6], (QC, H * R), QC), 'W_uk': w(ks[7], (KVC, H * HD), KVC), 'W_kr': w(ks[8], (KVC, R), KVC), 'W_uv': w(ks[9], (KVC, H * HD), KVC), 'W_o': w(ks[10], (H * HD, Q_DIM), H * HD)}
    _L1_xattn_all = _L1_xattn_setup()
    _L1_xattn_in = {k: v for k, v in _L1_xattn_all.items() if k in ('W_kvc', 'W_dq', 'W_uq', 'W_qr', 'W_uk', 'W_kr', 'W_uv', 'W_o')}
    del _L1_xattn_all

    def _L1_ffn_setup():
        import jax, jax.numpy as jnp
        import numpy as np
        TOPK = 2
        NORM_TOPK = True
        SCALE = 1.0
        EPS = 1e-09
        key = jax.random.key(seed)
        ks = jax.random.split(key, 9)
        h, i, E = (256, 128, 16)
        std = 0.02
        return {'x': jax.random.normal(ks[0], (1, 256, h), jnp.float32), 'Wr': jax.random.normal(ks[1], (E, h), jnp.float32) * std, 'bias': jnp.zeros((E,), jnp.float32), 'Wg': jax.random.normal(ks[2], (E, h, i), jnp.float32) * std, 'Wu': jax.random.normal(ks[3], (E, h, i), jnp.float32) * std, 'Wd': jax.random.normal(ks[4], (E, i, h), jnp.float32) * std, 'sWg': jax.random.normal(ks[5], (h, i), jnp.float32) * std, 'sWu': jax.random.normal(ks[6], (h, i), jnp.float32) * std, 'sWd': jax.random.normal(ks[7], (i, h), jnp.float32) * std}
    _L1_ffn_all = _L1_ffn_setup()
    _L1_ffn_in = {k: v for k, v in _L1_ffn_all.items() if k in ('Wr', 'bias', 'Wg', 'Wu', 'Wd', 'sWg', 'sWu', 'sWd')}
    del _L1_ffn_all

    def _L2_xattn_setup():
        import jax, jax.numpy as jnp
        import numpy as np
        import math
        B, S, HID, H = (2, 256, 256, 32)
        D = HID // H
        AL = 10

        def _rope_tables(seq_len, dim, dtype):
            inv_freq = 1.0 / 10000.0 ** (np.arange(0, dim, 2, dtype=np.float32) / dim)
            t = np.arange(seq_len, dtype=np.float32)
            freqs = np.outer(t, inv_freq)
            emb = np.concatenate([freqs, freqs], -1)
            return (jnp.asarray(np.cos(emb), dtype), jnp.asarray(np.sin(emb), dtype))

        def _rotate_half(x):
            x1, x2 = jnp.split(x, 2, axis=-1)
            return jnp.concatenate([-x2, x1], axis=-1)
        key = jax.random.key(seed)
        ks = jax.random.split(key, 8)
        hidden_states = jax.random.normal(ks[0], (B, S, HID), dtype=jnp.float32)
        adapter = jax.random.normal(ks[1], (B, AL, HID), dtype=jnp.float32)
        causal = jnp.tril(jnp.ones((S, S), dtype=bool))
        attention_mask = jnp.broadcast_to(jnp.where(causal, 0.0, -1000000000.0).astype(jnp.float32)[None, None], (B, 1, S, S))
        scale = 0.02
        Wq = jax.random.normal(ks[2], (HID, HID), dtype=jnp.float32) * scale
        Wk = jax.random.normal(ks[3], (HID, HID), dtype=jnp.float32) * scale
        Wv = jax.random.normal(ks[4], (HID, HID), dtype=jnp.float32) * scale
        Wo = jax.random.normal(ks[5], (HID, HID), dtype=jnp.float32) * scale
        gate = jax.random.normal(ks[6], (1, H, 1, 1), dtype=jnp.float32) * 0.1
        return {'hidden_states': hidden_states, 'attention_mask': attention_mask, 'adapter': adapter, 'Wq': Wq, 'Wk': Wk, 'Wv': Wv, 'Wo': Wo, 'gate': gate}
    _L2_xattn_all = _L2_xattn_setup()
    _L2_xattn_in = {k: v for k, v in _L2_xattn_all.items() if k in ('Wq', 'Wk', 'Wv', 'Wo', 'gate')}
    del _L2_xattn_all

    def _L2_ffn_setup():
        import jax, jax.numpy as jnp
        import numpy as np
        HIDDEN = 256
        INTER = 704
        EPS = 1e-05

        def rms_norm(x, g):
            var = jnp.mean(x * x, axis=-1, keepdims=True)
            return x * jax.lax.rsqrt(var + EPS) * g

        def activation_quant(x):
            scale = 127.0 / jnp.clip(jnp.max(jnp.abs(x), axis=-1, keepdims=True), 1e-05, None)
            return jnp.clip(jnp.round(x * scale), -128, 127) / scale

        def weight_quant(w):
            scale = 1.0 / jnp.clip(jnp.mean(jnp.abs(w)), 1e-05, None)
            return jnp.clip(jnp.round(w * scale), -1, 1) / scale

        def ste(x, q):
            return x + jax.lax.stop_gradient(q - x)

        def bit_linear(x, w, g):
            xn = rms_norm(x, g)
            xq = ste(xn, activation_quant(xn))
            wq = ste(w, weight_quant(w))
            return xq @ wq.T
        key = jax.random.key(seed)
        k1, k2, k3 = jax.random.split(key, 3)
        x = jax.random.normal(k1, (4, 256, HIDDEN), dtype=jnp.float32)
        gate_w = jax.random.normal(k2, (2 * INTER, HIDDEN), dtype=jnp.float32) * HIDDEN ** (-0.5)
        down_w = jax.random.normal(k3, (HIDDEN, INTER), dtype=jnp.float32) * INTER ** (-0.5)
        gate_norm_w = jnp.ones((HIDDEN,), dtype=jnp.float32)
        down_norm_w = jnp.ones((INTER,), dtype=jnp.float32)
        return {'x': x, 'gate_w': gate_w, 'down_w': down_w, 'gate_norm_w': gate_norm_w, 'down_norm_w': down_norm_w}
    _L2_ffn_all = _L2_ffn_setup()
    _L2_ffn_in = {k: v for k, v in _L2_ffn_all.items() if k in ('gate_w', 'down_w', 'gate_norm_w', 'down_norm_w')}
    del _L2_ffn_all

    def _L3_xattn_setup():
        import jax, jax.numpy as jnp
        import numpy as np
        from jax import lax
        LN_EPS = 1e-05
        key = jax.random.key(seed)
        ks = jax.random.split(key, 8)
        B, S, T, D = (4, 128, 256, 256)
        scale = 0.02
        return {'Z': jax.random.normal(ks[0], (B, S, D), dtype=jnp.float32), 'kv': jax.random.normal(ks[1], (B, T, D), dtype=jnp.float32), 'decay': jnp.float32(0.9), 'W_in': jax.random.normal(ks[2], (D, D), dtype=jnp.float32) * scale, 'b_in': jnp.zeros((D,), dtype=jnp.float32), 'W_out': jax.random.normal(ks[3], (D, D), dtype=jnp.float32) * scale, 'b_out': jnp.zeros((D,), dtype=jnp.float32), 'gamma': jnp.ones((D,), dtype=jnp.float32), 'beta': jnp.zeros((D,), dtype=jnp.float32)}
    _L3_xattn_all = _L3_xattn_setup()
    _L3_xattn_in = {k: v for k, v in _L3_xattn_all.items() if k in ('decay', 'W_in', 'b_in', 'W_out', 'b_out', 'gamma', 'beta')}
    del _L3_xattn_all

    def _L3_ffn_setup():
        import jax, jax.numpy as jnp
        import numpy as np
        B, S, H = (2, 128, 256)
        I = 128
        E = 32
        Z = 32
        K = 8
        SCALE = 1.5
        CAP = 128
        EPS = 1e-20

        def _moe_forward(x, w_cls, bias, w_gate_up, w_down):
            T = x.shape[0] * x.shape[1]
            xf = x.reshape(T, H)
            logits = xf.astype(jnp.float32) @ w_cls.T
            scores = jax.nn.softmax(logits, axis=-1)
            _, topk_idx = jax.lax.top_k(scores + bias[None, :], K)
            w = jnp.take_along_axis(scores, topk_idx, axis=-1)
            w = w / (w.sum(-1, keepdims=True) + EPS) * SCALE
            routed = topk_idx < E
            w_r = jnp.where(routed, w, 0.0)
            w_z = jnp.where(routed, 0.0, w)
            N = T * K
            flat_ids = jnp.where(routed, topk_idx, E).reshape(-1)
            x_exp = jnp.repeat(xf, K, axis=0)
            order = jnp.argsort(flat_ids)
            ids_s = flat_ids[order]
            counts = jax.ops.segment_sum(jnp.ones(N, jnp.int32), flat_ids, num_segments=E + 1)
            starts = jnp.cumsum(counts) - counts
            pos = jnp.arange(N) - starts[ids_s]
            buf = jnp.zeros((E, CAP, H), xf.dtype).at[ids_s, pos].set(x_exp[order], mode='drop')
            gu = jnp.einsum('ech,ehf->ecf', buf, w_gate_up)
            g, u = jnp.split(gu, 2, axis=-1)
            act = jax.nn.silu(g) * u
            y = jnp.einsum('eci,eih->ech', act, w_down)
            valid = (ids_s < E) & (pos < CAP)
            y_tok = jnp.where(valid[:, None], y[jnp.clip(ids_s, 0, E - 1), jnp.clip(pos, 0, CAP - 1)], 0.0)
            y_exp = jnp.zeros((N, H), xf.dtype).at[order].set(y_tok).reshape(T, K, H)
            routed_out = jnp.einsum('tk,tkh->th', w_r, y_exp)
            out = routed_out * (1.0 + w_z.sum(-1, keepdims=True))
            return out.reshape(x.shape)
        key = jax.random.key(seed)
        ks = jax.random.split(key, 5)
        x = jax.random.normal(ks[0], (B, S, H), jnp.float32)
        w_cls = jax.random.normal(ks[1], (E + Z, H), jnp.float32) / np.float32(np.sqrt(H))
        bias = jax.random.normal(ks[2], (E + Z,), jnp.float32) * 0.02
        w_gate_up = jax.random.normal(ks[3], (E, H, 2 * I), jnp.float32) * 0.02
        w_down = jax.random.normal(ks[4], (E, I, H), jnp.float32) * 0.02
        return {'x': x, 'w_cls': w_cls, 'bias': bias, 'w_gate_up': w_gate_up, 'w_down': w_down}
    _L3_ffn_all = _L3_ffn_setup()
    _L3_ffn_in = {k: v for k, v in _L3_ffn_all.items() if k in ('w_cls', 'bias', 'w_gate_up', 'w_down')}
    del _L3_ffn_all
    return {'x': x, 'ctx_2048': ctx_2048, 'itok_BxS_0_1023': itok_BxS_0_1023, 'mask_Bx1xSxS_fk0': mask_Bx1xSxS_fk0, 'g_xattn': g_xattn, 'g_ffn': g_ffn, 'L0_xattn_context_lens': _L0_xattn_in['context_lens'], 'L0_xattn_Wq': _L0_xattn_in['Wq'], 'L0_xattn_bq': _L0_xattn_in['bq'], 'L0_xattn_gq': _L0_xattn_in['gq'], 'L0_xattn_Wk': _L0_xattn_in['Wk'], 'L0_xattn_bk': _L0_xattn_in['bk'], 'L0_xattn_gk': _L0_xattn_in['gk'], 'L0_xattn_Wv': _L0_xattn_in['Wv'], 'L0_xattn_bv': _L0_xattn_in['bv'], 'L0_xattn_Wk_img': _L0_xattn_in['Wk_img'], 'L0_xattn_bk_img': _L0_xattn_in['bk_img'], 'L0_xattn_gk_img': _L0_xattn_in['gk_img'], 'L0_xattn_Wv_img': _L0_xattn_in['Wv_img'], 'L0_xattn_bv_img': _L0_xattn_in['bv_img'], 'L0_xattn_Wo': _L0_xattn_in['Wo'], 'L0_xattn_bo': _L0_xattn_in['bo'], 'L0_ffn_w_gate': _L0_ffn_in['w_gate'], 'L0_ffn_w_up': _L0_ffn_in['w_up'], 'L0_ffn_w_down': _L0_ffn_in['w_down'], 'L1_xattn_W_kvc': _L1_xattn_in['W_kvc'], 'L1_xattn_W_dq': _L1_xattn_in['W_dq'], 'L1_xattn_W_uq': _L1_xattn_in['W_uq'], 'L1_xattn_W_qr': _L1_xattn_in['W_qr'], 'L1_xattn_W_uk': _L1_xattn_in['W_uk'], 'L1_xattn_W_kr': _L1_xattn_in['W_kr'], 'L1_xattn_W_uv': _L1_xattn_in['W_uv'], 'L1_xattn_W_o': _L1_xattn_in['W_o'], 'L1_ffn_Wr': _L1_ffn_in['Wr'], 'L1_ffn_bias': _L1_ffn_in['bias'], 'L1_ffn_Wg': _L1_ffn_in['Wg'], 'L1_ffn_Wu': _L1_ffn_in['Wu'], 'L1_ffn_Wd': _L1_ffn_in['Wd'], 'L1_ffn_sWg': _L1_ffn_in['sWg'], 'L1_ffn_sWu': _L1_ffn_in['sWu'], 'L1_ffn_sWd': _L1_ffn_in['sWd'], 'L2_xattn_Wq': _L2_xattn_in['Wq'], 'L2_xattn_Wk': _L2_xattn_in['Wk'], 'L2_xattn_Wv': _L2_xattn_in['Wv'], 'L2_xattn_Wo': _L2_xattn_in['Wo'], 'L2_xattn_gate': _L2_xattn_in['gate'], 'L2_ffn_gate_w': _L2_ffn_in['gate_w'], 'L2_ffn_down_w': _L2_ffn_in['down_w'], 'L2_ffn_gate_norm_w': _L2_ffn_in['gate_norm_w'], 'L2_ffn_down_norm_w': _L2_ffn_in['down_norm_w'], 'L3_xattn_decay': _L3_xattn_in['decay'], 'L3_xattn_W_in': _L3_xattn_in['W_in'], 'L3_xattn_b_in': _L3_xattn_in['b_in'], 'L3_xattn_W_out': _L3_xattn_in['W_out'], 'L3_xattn_b_out': _L3_xattn_in['b_out'], 'L3_xattn_gamma': _L3_xattn_in['gamma'], 'L3_xattn_beta': _L3_xattn_in['beta'], 'L3_ffn_w_cls': _L3_ffn_in['w_cls'], 'L3_ffn_bias': _L3_ffn_in['bias'], 'L3_ffn_w_gate_up': _L3_ffn_in['w_gate_up'], 'L3_ffn_w_down': _L3_ffn_in['w_down']}

def reference(x, ctx_2048, itok_BxS_0_1023, mask_Bx1xSxS_fk0, g_xattn, g_ffn, L0_xattn_context_lens, L0_xattn_Wq, L0_xattn_bq, L0_xattn_gq, L0_xattn_Wk, L0_xattn_bk, L0_xattn_gk, L0_xattn_Wv, L0_xattn_bv, L0_xattn_Wk_img, L0_xattn_bk_img, L0_xattn_gk_img, L0_xattn_Wv_img, L0_xattn_bv_img, L0_xattn_Wo, L0_xattn_bo, L0_ffn_w_gate, L0_ffn_w_up, L0_ffn_w_down, L1_xattn_W_kvc, L1_xattn_W_dq, L1_xattn_W_uq, L1_xattn_W_qr, L1_xattn_W_uk, L1_xattn_W_kr, L1_xattn_W_uv, L1_xattn_W_o, L1_ffn_Wr, L1_ffn_bias, L1_ffn_Wg, L1_ffn_Wu, L1_ffn_Wd, L1_ffn_sWg, L1_ffn_sWu, L1_ffn_sWd, L2_xattn_Wq, L2_xattn_Wk, L2_xattn_Wv, L2_xattn_Wo, L2_xattn_gate, L2_ffn_gate_w, L2_ffn_down_w, L2_ffn_gate_norm_w, L2_ffn_down_norm_w, L3_xattn_decay, L3_xattn_W_in, L3_xattn_b_in, L3_xattn_W_out, L3_xattn_b_out, L3_xattn_gamma, L3_xattn_beta, L3_ffn_w_cls, L3_ffn_bias, L3_ffn_w_gate_up, L3_ffn_w_down):
    import jax
    import jax.numpy as jnp

    def _L0_xattn_ref(x, context, context_lens, Wq, bq, gq, Wk, bk, gk, Wv, bv, Wk_img, bk_img, gk_img, Wv_img, bv_img, Wo, bo):
        import jax, jax.numpy as jnp
        import numpy as np
        DIM = 256
        N_HEADS = 16
        HEAD_DIM = DIM // N_HEADS
        EPS = 1e-06
        IMG_LEN = 257

        def rms_norm(x, g, eps=EPS):
            var = jnp.mean(x * x, axis=-1, keepdims=True)
            return x * jax.lax.rsqrt(var + eps) * g

        def _attend(q, k, v, k_mask=None):
            scale = 1.0 / jnp.sqrt(jnp.asarray(HEAD_DIM, q.dtype))
            scores = jnp.einsum('bqnd,bknd->bnqk', q, k) * scale
            if k_mask is not None:
                neg = jnp.asarray(jnp.finfo(scores.dtype).min, scores.dtype)
                scores = jnp.where(k_mask[:, None, None, :], scores, neg)
            probs = jax.nn.softmax(scores, axis=-1)
            return jnp.einsum('bnqk,bknd->bqnd', probs, v)
        b = x.shape[0]
        n, d = (N_HEADS, HEAD_DIM)
        ctx_img = context[:, :IMG_LEN]
        ctx_txt = context[:, IMG_LEN:]
        q = rms_norm(x @ Wq + bq, gq).reshape(b, -1, n, d)
        k = rms_norm(ctx_txt @ Wk + bk, gk).reshape(b, -1, n, d)
        v = (ctx_txt @ Wv + bv).reshape(b, -1, n, d)
        k_img = rms_norm(ctx_img @ Wk_img + bk_img, gk_img).reshape(b, -1, n, d)
        v_img = (ctx_img @ Wv_img + bv_img).reshape(b, -1, n, d)
        img_x = _attend(q, k_img, v_img)
        k_mask = jnp.arange(k.shape[1])[None, :] < context_lens[:, None]
        txt_x = _attend(q, k, v, k_mask)
        out = (txt_x + img_x).reshape(b, -1, n * d)
        return out @ Wo + bo

    def _L0_ffn_ref(x, w_gate, w_up, w_down):
        import jax, jax.numpy as jnp
        import numpy as np

        def _sparsify_2to4(h):
            B, S, I = h.shape
            g = h.reshape(B, S, I // 4, 4)
            a = jnp.abs(g)
            _, idx = jax.lax.top_k(a, 2)
            pos = jnp.arange(4)
            mask = (pos == idx[..., 0:1]) | (pos == idx[..., 1:2])
            return (g * mask.astype(g.dtype)).reshape(B, S, I)
        h = jax.nn.silu(jnp.einsum('bsh,hi->bsi', x, w_gate)) * jnp.einsum('bsh,hi->bsi', x, w_up)
        h_sparse = _sparsify_2to4(h)
        return jnp.einsum('bsi,ih->bsh', h_sparse, w_down)

    def _L1_xattn_ref(q, kv, seg_id, W_kvc, W_dq, W_uq, W_qr, W_uk, W_kr, W_uv, W_o):
        import jax, jax.numpy as jnp
        import numpy as np
        B, Lq, Lk = (2, 512, 128)
        Q_DIM, KV_DIM = (256, 256)
        H, HD = (16, 128)
        KVC, QC, R = (64, 96, 64)
        LOOKBACK = 8
        NEG = -1e+30

        def _rope(x, L):
            half = x.shape[-1] // 2
            inv_freq = 1.0 / 10000.0 ** (jnp.arange(half, dtype=jnp.float32) / half)
            ang = jnp.arange(L, dtype=jnp.float32)[:, None] * inv_freq
            cos, sin = (jnp.cos(ang), jnp.sin(ang))
            x1, x2 = (x[..., :half], x[..., half:])
            return jnp.concatenate([x1 * cos - x2 * sin, x1 * sin + x2 * cos], axis=-1)
        b, lq, _ = q.shape
        lk = kv.shape[1]
        kv_c = kv @ W_kvc
        q_c = q @ W_dq
        q_nope = (q_c @ W_uq).reshape(b, lq, H, HD).transpose(0, 2, 1, 3)
        q_rope = (q_c @ W_qr).reshape(b, lq, H, R).transpose(0, 2, 1, 3)
        k_nope = (kv_c @ W_uk).reshape(b, lk, H, HD)
        v = (kv_c @ W_uv).reshape(b, lk, H, HD)
        k_rope = kv_c @ W_kr
        q_rope = _rope(q_rope, lq)
        k_rope = _rope(k_rope, lk)
        scale = 1.0 / np.sqrt(HD + R).astype(np.float32)
        scores = (jnp.einsum('bhqd,bkhd->bhqk', q_nope, k_nope) + jnp.einsum('bhqr,bkr->bhqk', q_rope, k_rope)) * scale
        k_ids = jnp.arange(lk)[None, None, :]
        qs = seg_id[:, :, None]
        good = (k_ids <= qs) & (k_ids >= qs - LOOKBACK)
        scores = jnp.where(good[:, None, :, :], scores, NEG)
        attn = jax.nn.softmax(scores, axis=-1)
        out = jnp.einsum('bhqk,bkhd->bqhd', attn, v).reshape(b, lq, H * HD)
        return out @ W_o

    def _L1_ffn_ref(x, Wr, bias, Wg, Wu, Wd, sWg, sWu, sWd):
        import jax, jax.numpy as jnp
        import numpy as np
        TOPK = 2
        NORM_TOPK = True
        SCALE = 1.0
        EPS = 1e-09
        b, s, h = x.shape
        E = Wr.shape[0]
        xt = x.reshape(b * s, h)
        logits = xt @ Wr.T + bias
        probs = jax.nn.softmax(logits, axis=-1)
        topk_val, topk_idx = jax.lax.top_k(probs, TOPK)
        if NORM_TOPK:
            w = topk_val / (jnp.sum(topk_val, axis=-1, keepdims=True) + EPS)
        else:
            w = topk_val
        w = w * SCALE
        g = jnp.einsum('th,ehi->tei', xt, Wg)
        u = jnp.einsum('th,ehi->tei', xt, Wu)
        y = jnp.einsum('tei,eih->teh', jax.nn.silu(g) * u, Wd)
        oh = jax.nn.one_hot(topk_idx, E, dtype=x.dtype)
        routed = jnp.einsum('tke,tk,teh->th', oh, w, y)
        shared = jax.nn.silu(xt @ sWg) * (xt @ sWu) @ sWd
        return (routed + shared).reshape(b, s, h)

    def _L2_xattn_ref(hidden_states, attention_mask, adapter, Wq, Wk, Wv, Wo, gate):
        import jax, jax.numpy as jnp
        import numpy as np
        import math
        B, S, HID, H = (2, 256, 256, 32)
        D = HID // H
        AL = 10

        def _rope_tables(seq_len, dim, dtype):
            inv_freq = 1.0 / 10000.0 ** (np.arange(0, dim, 2, dtype=np.float32) / dim)
            t = np.arange(seq_len, dtype=np.float32)
            freqs = np.outer(t, inv_freq)
            emb = np.concatenate([freqs, freqs], -1)
            return (jnp.asarray(np.cos(emb), dtype), jnp.asarray(np.sin(emb), dtype))

        def _rotate_half(x):
            x1, x2 = jnp.split(x, 2, axis=-1)
            return jnp.concatenate([-x2, x1], axis=-1)
        bsz, q_len, hid = hidden_states.shape
        n_heads = gate.shape[1]
        head_dim = hid // n_heads
        inv_sqrt_d = 1.0 / math.sqrt(head_dim)

        def split_heads(x, length):
            return x.reshape(bsz, length, n_heads, head_dim).transpose(0, 2, 1, 3)
        q = split_heads(hidden_states @ Wq, q_len)
        k = split_heads(hidden_states @ Wk, q_len)
        v = split_heads(hidden_states @ Wv, q_len)
        cos, sin = _rope_tables(q_len, head_dim, q.dtype)
        q = q * cos + _rotate_half(q) * sin
        k = k * cos + _rotate_half(k) * sin
        scores = jnp.einsum('bhqd,bhkd->bhqk', q, k) * inv_sqrt_d
        scores = scores + attention_mask
        scores = jnp.maximum(scores, jnp.finfo(scores.dtype).min)
        w = jax.nn.softmax(scores.astype(jnp.float32), axis=-1).astype(q.dtype)
        attn_output = jnp.einsum('bhqk,bhkd->bhqd', w, v)
        adapter_len = adapter.shape[1]
        a_k = split_heads(adapter @ Wk, adapter_len)
        a_v = split_heads(adapter @ Wv, adapter_len)
        a_scores = jnp.einsum('bhqd,bhkd->bhqk', q, a_k) * inv_sqrt_d
        a_scores = jnp.tanh(gate) * jax.nn.softmax(a_scores.astype(jnp.float32), axis=-1).astype(q.dtype)
        attn_output = attn_output + jnp.einsum('bhqk,bhkd->bhqd', a_scores, a_v)
        attn_output = attn_output.transpose(0, 2, 1, 3).reshape(bsz, q_len, hid)
        return attn_output @ Wo

    def _L2_ffn_ref(x, gate_w, down_w, gate_norm_w, down_norm_w):
        import jax, jax.numpy as jnp
        import numpy as np
        HIDDEN = 256
        INTER = 704
        EPS = 1e-05

        def rms_norm(x, g):
            var = jnp.mean(x * x, axis=-1, keepdims=True)
            return x * jax.lax.rsqrt(var + EPS) * g

        def activation_quant(x):
            scale = 127.0 / jnp.clip(jnp.max(jnp.abs(x), axis=-1, keepdims=True), 1e-05, None)
            return jnp.clip(jnp.round(x * scale), -128, 127) / scale

        def weight_quant(w):
            scale = 1.0 / jnp.clip(jnp.mean(jnp.abs(w)), 1e-05, None)
            return jnp.clip(jnp.round(w * scale), -1, 1) / scale

        def ste(x, q):
            return x + jax.lax.stop_gradient(q - x)

        def bit_linear(x, w, g):
            xn = rms_norm(x, g)
            xq = ste(xn, activation_quant(xn))
            wq = ste(w, weight_quant(w))
            return xq @ wq.T
        y = bit_linear(x, gate_w, gate_norm_w)
        gate, up = jnp.split(y, 2, axis=-1)
        h = gate * jax.nn.sigmoid(gate) * up
        return bit_linear(h, down_w, down_norm_w)

    def _L3_xattn_ref(Z, kv, decay, W_in, b_in, W_out, b_out, gamma, beta):
        import jax, jax.numpy as jnp
        import numpy as np
        from jax import lax
        LN_EPS = 1e-05
        B, T, D = kv.shape
        K = jax.nn.sigmoid(decay)
        x = jnp.einsum('btd,ed->bte', kv, W_in) + b_in

        def scan_fn(s, xt):
            s = K * s + xt
            return (s, s)
        s0 = jnp.zeros((B, D), dtype=kv.dtype)
        _, states = lax.scan(scan_fn, s0, jnp.swapaxes(x, 0, 1))
        states = jnp.swapaxes(states, 0, 1)
        proj = jnp.einsum('btd,ed->bte', states, W_out) + b_out
        summary = jnp.mean(proj, axis=1, keepdims=True)
        y = Z + summary
        mu = jnp.mean(y, axis=-1, keepdims=True)
        var = jnp.mean((y - mu) ** 2, axis=-1, keepdims=True)
        return (y - mu) / jnp.sqrt(var + LN_EPS) * gamma + beta

    def _L3_ffn_ref(x, w_cls, bias, w_gate_up, w_down):
        import jax, jax.numpy as jnp
        import numpy as np
        B, S, H = (2, 128, 256)
        I = 128
        E = 32
        Z = 32
        K = 8
        SCALE = 1.5
        CAP = 128
        EPS = 1e-20

        def _moe_forward(x, w_cls, bias, w_gate_up, w_down):
            T = x.shape[0] * x.shape[1]
            xf = x.reshape(T, H)
            logits = xf.astype(jnp.float32) @ w_cls.T
            scores = jax.nn.softmax(logits, axis=-1)
            _, topk_idx = jax.lax.top_k(scores + bias[None, :], K)
            w = jnp.take_along_axis(scores, topk_idx, axis=-1)
            w = w / (w.sum(-1, keepdims=True) + EPS) * SCALE
            routed = topk_idx < E
            w_r = jnp.where(routed, w, 0.0)
            w_z = jnp.where(routed, 0.0, w)
            N = T * K
            flat_ids = jnp.where(routed, topk_idx, E).reshape(-1)
            x_exp = jnp.repeat(xf, K, axis=0)
            order = jnp.argsort(flat_ids)
            ids_s = flat_ids[order]
            counts = jax.ops.segment_sum(jnp.ones(N, jnp.int32), flat_ids, num_segments=E + 1)
            starts = jnp.cumsum(counts) - counts
            pos = jnp.arange(N) - starts[ids_s]
            buf = jnp.zeros((E, CAP, H), xf.dtype).at[ids_s, pos].set(x_exp[order], mode='drop')
            gu = jnp.einsum('ech,ehf->ecf', buf, w_gate_up)
            g, u = jnp.split(gu, 2, axis=-1)
            act = jax.nn.silu(g) * u
            y = jnp.einsum('eci,eih->ech', act, w_down)
            valid = (ids_s < E) & (pos < CAP)
            y_tok = jnp.where(valid[:, None], y[jnp.clip(ids_s, 0, E - 1), jnp.clip(pos, 0, CAP - 1)], 0.0)
            y_exp = jnp.zeros((N, H), xf.dtype).at[order].set(y_tok).reshape(T, K, H)
            routed_out = jnp.einsum('tk,tkh->th', w_r, y_exp)
            out = routed_out * (1.0 + w_z.sum(-1, keepdims=True))
            return out.reshape(x.shape)
        return _moe_forward(x, w_cls, bias, w_gate_up, w_down)
    x = x + jnp.tanh(g_xattn[0]) * _L0_xattn_ref(_layernorm(x, axis=-1), ctx_2048, L0_xattn_context_lens, L0_xattn_Wq, L0_xattn_bq, L0_xattn_gq, L0_xattn_Wk, L0_xattn_bk, L0_xattn_gk, L0_xattn_Wv, L0_xattn_bv, L0_xattn_Wk_img, L0_xattn_bk_img, L0_xattn_gk_img, L0_xattn_Wv_img, L0_xattn_bv_img, L0_xattn_Wo, L0_xattn_bo)
    x = x + jnp.tanh(g_ffn[0]) * _L0_ffn_ref(_layernorm(x, axis=-1), L0_ffn_w_gate, L0_ffn_w_up, L0_ffn_w_down)
    x = x + jnp.tanh(g_xattn[1]) * _L1_xattn_ref(_layernorm(x, axis=-1), ctx_2048, itok_BxS_0_1023, L1_xattn_W_kvc, L1_xattn_W_dq, L1_xattn_W_uq, L1_xattn_W_qr, L1_xattn_W_uk, L1_xattn_W_kr, L1_xattn_W_uv, L1_xattn_W_o)
    x = x + jnp.tanh(g_ffn[1]) * _L1_ffn_ref(_layernorm(x, axis=-1), L1_ffn_Wr, L1_ffn_bias, L1_ffn_Wg, L1_ffn_Wu, L1_ffn_Wd, L1_ffn_sWg, L1_ffn_sWu, L1_ffn_sWd)
    x = x + jnp.tanh(g_xattn[2]) * _L2_xattn_ref(_layernorm(x, axis=-1), mask_Bx1xSxS_fk0, ctx_2048, L2_xattn_Wq, L2_xattn_Wk, L2_xattn_Wv, L2_xattn_Wo, L2_xattn_gate)
    x = x + jnp.tanh(g_ffn[2]) * _L2_ffn_ref(_layernorm(x, axis=-1), L2_ffn_gate_w, L2_ffn_down_w, L2_ffn_gate_norm_w, L2_ffn_down_norm_w)
    x = x + jnp.tanh(g_xattn[3]) * _L3_xattn_ref(_layernorm(x, axis=-1), ctx_2048, L3_xattn_decay, L3_xattn_W_in, L3_xattn_b_in, L3_xattn_W_out, L3_xattn_b_out, L3_xattn_gamma, L3_xattn_beta)
    x = x + jnp.tanh(g_ffn[3]) * _L3_ffn_ref(_layernorm(x, axis=-1), L3_ffn_w_cls, L3_ffn_bias, L3_ffn_w_gate_up, L3_ffn_w_down)
    return x

_drawn_inputs = setup_inputs


def setup_inputs(seed=0):
    import zlib

    import numpy as np

    out = dict(_drawn_inputs(seed))
    spreads = {'L0_xattn_bq': (0.0, 0.527),
     'L0_xattn_gq': (1.0, 0.6),
     'L0_xattn_bk': (0.0, 0.1),
     'L0_xattn_gk': (1.0, 0.2),
     'L0_xattn_bv': (0.0, 0.1),
     'L0_xattn_bk_img': (0.0, 0.8),
     'L0_xattn_gk_img': (1.0, 0.6),
     'L0_xattn_bv_img': (0.0, 0.1),
     'L0_xattn_bo': (0.0, 0.1),
     'L1_ffn_bias': (0.0, 0.8),
     'L2_ffn_gate_norm_w': (1.0, 0.2),
     'L2_ffn_down_norm_w': (1.0, 0.2),
     'L3_xattn_b_in': (0.0, 0.1),
     'L3_xattn_b_out': (0.0, 0.1),
     'L3_xattn_gamma': (1.0, 0.2),
     'L3_xattn_beta': (0.0, 0.1)}
    factors = {'g_ffn': 8.0,
     'L0_xattn_Wq': 2.681,
     'L1_ffn_Wr': 5.759,
     'L1_ffn_Wg': 5.564,
     'L1_ffn_Wu': 5.564,
     'L1_ffn_Wd': 5.566,
     'L1_ffn_sWg': 4.622,
     'L1_ffn_sWu': 4.574,
     'L1_ffn_sWd': 4.562,
     'L2_xattn_Wq': 8.0,
     'L2_xattn_Wk': 8.0,
     'L2_xattn_gate': 6.761,
     'L3_ffn_w_cls': 5.631,
     'L3_ffn_bias': 8.0,
     'L3_ffn_w_gate_up': 5.451,
     'L3_ffn_w_down': 5.469}
    for name, (base, spread) in spreads.items():
        noise = np.random.default_rng([zlib.crc32(name.encode()), seed]).standard_normal(out[name].shape)
        drawn = base * np.exp(spread * noise) if base else spread * noise
        out[name] = jnp.asarray(drawn.astype(out[name].dtype))
    for name, factor in factors.items():
        out[name] = (out[name] * factor).astype(out[name].dtype)
    return out
```

```python
from contextlib import ExitStack

import numpy as np

import concourse.bass as bass
from concourse import mybir

F32 = mybir.dt.float32
BF16 = mybir.dt.bfloat16
I32 = mybir.dt.int32
ALU = mybir.AluOpType
ACT = mybir.ActivationFunctionType
AX = mybir.AxisListType.X

P = 128
D = 256
C = D // P
B = 4
S = 256
TB = S // P
NT = B * TB
T = B * S
SK = 64
CT = B * SK
BANK = 512

H0, HD0 = 16, 16
HB0 = P // HD0
I0 = 1024
H1, HD1, R1, QC1, KC1 = 16, 128, 64, 96, 64
LOOKBACK = 8
I1, E1 = 128, 16
H2, HD2 = 32, 8
I2 = 704
I3, E3, Z3, TOP3, CAP3 = 128, 32, 32, 8, 128


class Tally:

    def __init__(self, sem):
        self.sem, self.base, self.k, self.i, self.per = sem, 0, 0, 0, 0

    def loop(self, i, per):
        self.base += self.k
        self.k, self.i, self.per = 0, i, per

    def end_loop(self, trips):
        assert self.k == self.per, (self.sem, self.k, self.per)
        self.base += trips * self.per
        self.k, self.i, self.per = 0, 0, 0

    def now(self):
        return self.i * self.per + (self.base + self.k)


class Steps(Tally):

    def __init__(self, eng, sem):
        super().__init__(sem)
        self.eng = eng

    def mark(self, ins):
        self.k += 1
        return ins.then_inc(self.sem, 1)

    def wait(self):
        self.eng.wait_ge(self.sem, self.now())

    def done(self, ins):
        self.mark(ins)
        self.wait()


def tile_of(x, t):
    return x[:, bass.ds(t, 1), :].rearrange("p a n -> p (a n)")


def flat(x):
    return x.rearrange("p a n -> p (a n)")


class Region:

    def __init__(self, tensor):
        self.tensor, self.at = tensor, 0

    def restart(self):
        self.at = 0

    def take(self, shape, dt=F32):
        n = int(np.prod(shape[1:]))
        words = n if dt != BF16 else (n + 1) // 2
        v = self.tensor[0:shape[0], self.at:self.at + words]
        self.at += words
        assert self.at <= self.tensor.shape[1], (self.at, self.tensor.shape)
        if dt != F32:
            v = v.bitcast(dt)
        if len(shape) == 2:
            return v
        axes = [f"d{k}" for k in range(len(shape) - 1)]
        return v.rearrange(f"p ({' '.join(axes)}) -> p {' '.join(axes)}", **dict(zip(axes[1:], shape[2:])))


def flamingo(nc, A, out, stages=8):
    ctx = ExitStack()
    with ctx:
        def sb(name, shape, dt=F32):
            return ctx.enter_context(nc.sbuf_tensor(name, shape, dt))

        def sem(name):
            return ctx.enter_context(nc.semaphore(name))

        psum = ctx.enter_context(nc.psum_tensor("psum", [P, 8, BANK], F32))

        def bank(i, n=1):
            return psum[:, i:i + n, :].rearrange("p a n -> p (a n)")

        x = sb("x", [P, NT, D])
        xn = sb("xn", [P, TB, D])
        xT = sb("xT", [P, C, S])
        ident = sb("ident", [P, P])
        ones = sb("ones", [1, P])
        gates = sb("gates", [P, 8])
        minus_half = sb("minus_half", [P, 8])
        ln_stats = sb("ln_stats", [P, TB, 6])
        ln_mv = sb("ln_mv", [P, TB, 2])
        ln_rstd = sb("ln_rstd", [P, TB, 1])
        ctxT = sb("ctxT", [P, C, CT])

        prob = sb("prob", [P, 1024])
        probT = sb("probT", [P, 8, P])
        scratch = Region(sb("scratch", [P, 11264]))
        attn_region = Region(sb("attn_region", [P, 24704]))
        ffn_region = Region(sb("ffn_region", [P, 6912]))

        turn = bank(0).rearrange("p (c s) -> p c s", c=C)

        s_load = sem("load_x")
        s_const = sem("const_set")
        s_gates = sem("gates_set")
        s_dve = sem("vector_step")
        s_pool = sem("gpsimd_step")
        s_act = sem("scalar_step")
        s_ln_var = sem("ln_var_ready")
        s_ln_rstd = sem("ln_rstd_ready")
        s_ln_norm = sem("ln_norm_ready")
        s_turned = sem("turned")
        s_turn_out = sem("turn_out")
        s_store = sem("store_out")

        def settle(eng):
            eng.sem_inc(s_settled, 1)

        s_settled = sem("settled")

        def ln_vector(dve, st, i, n):
            for j in range(TB):
                st.mark(dve.bn_stats(ln_stats[:, j, :], tile_of(x, i * TB + j)))
            st.wait()
            settle(dve)
            for j in range(TB):
                st.mark(dve.bn_aggr(ln_mv[:, j, :], ln_stats[:, j, :]))
            st.wait()
            dve.tensor_scalar(ln_mv[:, :, 1:2], ln_mv[:, :, 1:2], 1e-5, None, ALU.add).then_inc(s_ln_var, 1)
            dve.wait_ge(s_ln_rstd, n + 1)
            return n

        def ln_apply(dve, i, turned_before):
            dve.wait_ge(s_turned, turned_before)
            for j in range(TB):
                ins = dve.tensor_scalar(xn[:, j, :], tile_of(x, i * TB + j), ln_mv[:, j, 0:1],
                                        ln_rstd[:, j, :], ALU.subtract, ALU.mult)
            ins.then_inc(s_ln_norm, 1)

        def ln_gpsimd(pool, n):
            pool.wait_ge(s_ln_var, n + 1)
            pool.tensor_tensor(ln_rstd[:, :, 0], ln_mv[:, :, 1], minus_half[:, 0:TB],
                               ALU.pow).then_inc(s_ln_rstd, 1)

        def turn_batch(pe, turns, src):
            pe.wait_ge(s_turn_out, turns.now())
            for c in range(C):
                for j in range(TB):
                    ins = pe.transpose(turn[:, c, j * P:(j + 1) * P], src[:, j, c * P:(c + 1) * P],
                                       ident[:, :])
            ins.then_inc(s_turned, 1)
            turns.k += 1

        def turn_evac(act, turns, dst):
            act.wait_ge(s_turned, turns.now() + 1)
            act.activation(flat(dst[:, :, :]), bank(0), ACT.Copy).then_inc(s_turn_out, 1)
            turns.k += 1

        l0_w = attn_region.take([P, 4, C, D])
        l0_rows = attn_region.take([1, 4, D])
        l0_gain = attn_region.take([P, 2, D])
        ctxT2 = attn_region.take([P, C, B, P])
        head_of = sb("head_of", [P, HB0])
        half_of = sb("half_of", [P, 2])
        l0_kT = attn_region.take([P, C, CT])
        l0_v = attn_region.take([P, B, D])
        l0_kdiag = scratch.take([P, C, HB0, SK])
        l0_vdiag = scratch.take([P, H0 // 2, 2, HD0])
        junk = scratch.take([P, TB, D])
        ssq = scratch.take([P, TB])
        rms = scratch.take([P, TB])
        qn = scratch.take([P, TB, D])
        qT = scratch.take([P, C, S])
        top = sb("top", [P, H2])
        total = sb("total", [P, H2])
        oT = scratch.take([P, C, S])

        s_l0_load = sem("l0_load")
        s_proj = sem("rows_projected")
        s_ssq = sem("squares_summed")
        s_ms = sem("mean_square_ready")
        s_rms = sem("rms_ready")
        s_scaled = sem("rows_scaled")
        s_v = sem("l0_v_projected")
        s_vout = sem("l0_v_ready")
        s_diag = sem("l0_diag_ready")
        s_score = sem("scores_ready")
        s_shift = sem("scores_shifted")
        s_exp = sem("exp_ready")
        s_ptT = sem("probs_turned")
        s_pt = sem("probs_turn_out")
        s_pv = sem("pv_ready")
        s_o = sem("heads_ready")
        s_y = sem("attn_out_ready")
        s_res = sem("residual_added")

        q_ps = bank(1).rearrange("p (j d) -> p j d", j=TB)
        sc_ps = bank(2, 2)
        pt_ps = bank(4, 2)
        pv_ps = bank(6)[:, 0:D]
        y_ps = bank(7)[:, 0:D]

        def l0_attn_sync(sp):
            for dst, name in ((ctxT[:, :, :], "ctxT"), (l0_w[:, :, :, :], "l0_w"), (l0_rows[:, :, :], "l0_rows"),
                              (l0_gain[:, :, :], "l0_gain"), (ctxT2[:, :, :, :], "ctxT2"),
                              (head_of[:, :], "head_of"), (half_of[:, :], "half_of")):
                sp.dma_start(dst, A[name]).then_inc(s_l0_load, 16)

        def rms_scalar(act, n):
            act.wait_ge(s_proj, n + 1)
            for j in range(TB):
                ins = act.activation(junk[:, j, :], q_ps[:, j, :], ACT.Square, accum_out=ssq[:, j:j + 1])
            ins.then_inc(s_ssq, 1)

        def rms_vector(dve, n, gain, turned_before):
            dve.wait_ge(s_ssq, n + 1)
            dve.tensor_scalar(rms[:, :], ssq[:, :], 1.0 / D, 1e-6, ALU.mult, ALU.add).then_inc(s_ms, 1)
            dve.wait_ge(s_rms, n + 1)
            dve.wait_ge(s_turned, turned_before)
            for j in range(TB):
                ins = dve.scalar_tensor_tensor(out=qn[:, j, :], in0=q_ps[:, j, :], scalar=rms[:, j:j + 1],
                                               in1=gain, op0=ALU.mult, op1=ALU.mult)
            ins.then_inc(s_scaled, 1)

        def rms_gpsimd(pool, n):
            pool.wait_ge(s_ms, n + 1)
            pool.tensor_tensor(rms[:, :], rms[:, :], minus_half[:, 0:TB], ALU.pow).then_inc(s_rms, 1)

        def l0_attn_tensor(pe, turns):
            pe.wait_ge(s_l0_load, 16 * 7)
            pe.wait_ge(s_const, 3)
            for m in range(TB):
                pe.matmul(q_ps[:, m, :], ones[:, :], l0_rows[:, 1, :], start=True, stop=False)
                for c in range(C):
                    ins = pe.matmul(q_ps[:, m, :], ctxT[:, c, m * P:(m + 1) * P], l0_w[:, 1, c, :],
                                    start=False, stop=(c == C - 1))
            ins.then_inc(s_proj, 1)
            for b in range(B):
                v_ps = sc_ps[:, b * D:(b + 1) * D]
                pe.matmul(v_ps, ones[:, :], l0_rows[:, 2, :], start=True, stop=False)
                for c in range(C):
                    ins = pe.matmul(v_ps, ctxT2[:, c, b, :], l0_w[:, 2, c, :], start=False, stop=(c == C - 1))
            ins.then_inc(s_v, 1)
            pe.wait_ge(s_scaled, 1)
            turn_batch(pe, turns, qn)
            pe.wait_ge(s_vout, 1)
            with pe.Fori(0, B) as i:
                turns.loop(i, 3)
                pe.wait_ge(s_ln_norm, i + 1)
                turn_batch(pe, turns, xn)
                pe.wait_ge(s_turn_out, turns.now())
                for j in range(TB):
                    pe.matmul(q_ps[:, j, :], ones[:, :], l0_rows[:, 0, :], start=True, stop=False)
                    for c in range(C):
                        ins = pe.matmul(q_ps[:, j, :], xT[:, c, j * P:(j + 1) * P], l0_w[:, 0, c, :],
                                        start=False, stop=(c == C - 1))
                ins.then_inc(s_proj, 1)
                pe.wait_ge(s_scaled, i + 2)
                turn_batch(pe, turns, qn)
                pe.wait_ge(s_turn_out, turns.now())
                pe.wait_ge(s_diag, i + 1)

                def scores(j):
                    pe.wait_ge(s_shift, i * TB + j)
                    for c in range(C):
                        ins = pe.matmul(sc_ps[:, c * BANK:(c + 1) * BANK], qT[:, c, j * P:(j + 1) * P],
                                        l0_kdiag[:, c, :, :].rearrange("p h k -> p (h k)"),
                                        start=True, stop=True)
                    ins.then_inc(s_score, 1)

                def weigh(j):
                    pe.wait_ge(s_exp, i * TB + j + 1)
                    pe.wait_ge(s_pt, i * TB + j)
                    for g in range(8):
                        ins = pe.transpose(pt_ps[:, g * P:(g + 1) * P], prob[:, g * P:(g + 1) * P], ident[:, :])
                    ins.then_inc(s_ptT, 1)
                    pe.wait_ge(s_pt, i * TB + j + 1)
                    pe.wait_ge(s_o, i * TB + j)
                    for g in range(8):
                        ins = pe.matmul(pv_ps[:, g * 32:(g + 1) * 32], probT[:, g, :],
                                        l0_vdiag[:, g, :, :].rearrange("p a d -> p (a d)"), start=True, stop=True)
                    ins.then_inc(s_pv, 1)

                scores(0)
                scores(1)
                weigh(0)
                weigh(1)
                pe.wait_ge(s_o, i * TB + TB)
                turn_batch(pe, turns, qn)
                pe.wait_ge(s_turn_out, turns.now())
                for j in range(TB):
                    pe.wait_ge(s_res, i * TB + j)
                    pe.matmul(y_ps, ones[:, :], l0_rows[:, 3, :], start=True, stop=False)
                    for c in range(C):
                        ins = pe.matmul(y_ps, oT[:, c, j * P:(j + 1) * P], l0_w[:, 3, c, :],
                                        start=False, stop=(c == C - 1))
                    ins.then_inc(s_y, 1)
            turns.end_loop(B)

        def l0_attn_scalar(act, turns):
            rms_scalar(act, 0)
            act.wait_ge(s_v, 1)
            act.activation(l0_v[:, :, :].rearrange("p b d -> p (b d)"), sc_ps, ACT.Copy).then_inc(s_vout, 1)
            turn_evac(act, turns, l0_kT)
            with act.Fori(0, B) as i:
                turns.loop(i, 3)
                turn_evac(act, turns, xT)
                rms_scalar(act, i + 1)
                turn_evac(act, turns, qT)
                for j in range(TB):
                    act.wait_ge(s_shift, i * TB + j + 1)
                    act.activation(prob[:, :], prob[:, :], ACT.Exp, scale=HD0 ** -0.5).then_inc(s_exp, 1)
                    act.wait_ge(s_ptT, i * TB + j + 1)
                    act.wait_ge(s_pv, i * TB + j)
                    act.activation(probT[:, :, :].rearrange("p g q -> p (g q)"), pt_ps, ACT.Copy).then_inc(s_pt, 1)
                turn_evac(act, turns, oT)
            turns.end_loop(B)

        def l0_attn_gpsimd(pool):
            rms_gpsimd(pool, 0)
            pool.wait_ge(s_l0_load, 16 * 7)
            pool.wait_ge(s_turn_out, 1)
            pool.wait_ge(s_vout, 1)
            with pool.Fori(0, B) as i:
                ln_gpsimd(pool, i)
                pool.wait_ge(s_score, i * TB)
                pool.wait_ge(s_pv, i * TB)
                for c in range(C):
                    pool.tensor_tensor(l0_kdiag[:, c, :, :],
                                       l0_kT[:, c:c + 1, bass.ds(i * SK, SK)].to_broadcast([P, HB0, SK]),
                                       head_of[:, :].unsqueeze(2).to_broadcast([P, HB0, SK]), ALU.mult)
                pool.tensor_tensor(l0_vdiag[:, :, :, :],
                                   tile_of(l0_v, i).rearrange("p (g a d) -> p g a d", a=2, d=HD0),
                                   half_of[:, :].unsqueeze(1).unsqueeze(3).to_broadcast([P, H0 // 2, 2, HD0]),
                                   ALU.mult).then_inc(s_diag, 1)
                rms_gpsimd(pool, i + 1)

        def l0_attn_vector(dve, st):
            dve.wait_ge(s_l0_load, 16 * 7)
            rms_vector(dve, 0, l0_gain[:, 1, :], 0)
            with dve.Fori(0, B) as i:
                st.loop(i, 4 + TB * 3)
                ln_vector(dve, st, i, i)
                ln_apply(dve, i, i * 3 + 1)
                rms_vector(dve, i + 1, l0_gain[:, 0, :], i * 3 + 1)

                def shift(j):
                    dve.wait_ge(s_score, i * TB + j + 1)
                    st.done(dve.tensor_reduce(top[:, 0:H0], sc_ps.rearrange("p (h k) -> p h k", h=H0), AX, ALU.max))
                    dve.wait_ge(s_ptT, i * TB + j)
                    dve.tensor_tensor(prob[:, :].rearrange("p (h k) -> p h k", h=H0),
                                      sc_ps.rearrange("p (h k) -> p h k", h=H0),
                                      top[:, 0:H0].unsqueeze(2).to_broadcast([P, H0, SK]),
                                      ALU.subtract).then_inc(s_shift, 1)

                def norm(j):
                    dve.wait_ge(s_exp, i * TB + j + 1)
                    st.done(dve.tensor_reduce(total[:, 0:H0], prob[:, :].rearrange("p (h k) -> p h k", h=H0), AX, ALU.add))
                    st.done(dve.reciprocal(total[:, 0:H0], total[:, 0:H0]))

                def heads(j):
                    dve.wait_ge(s_pv, i * TB + j + 1)
                    dve.tensor_tensor(qn[:, j, :].rearrange("p (h d) -> p h d", h=H0),
                                      pv_ps.rearrange("p (h d) -> p h d", h=H0),
                                      total[:, 0:H0].unsqueeze(2).to_broadcast([P, H0, HD0]),
                                      ALU.mult).then_inc(s_o, 1)

                for j in range(TB):
                    shift(j)
                    norm(j)
                    heads(j)
                for j in range(TB):
                    dve.wait_ge(s_y, i * TB + j + 1)
                    dve.scalar_tensor_tensor(out=tile_of(x, i * TB + j), in0=y_ps, scalar=gates[:, 0:1],
                                             in1=tile_of(x, i * TB + j), op0=ALU.mult, op1=ALU.add).then_inc(s_res, 1)
            st.end_loop(B)

        scratch.restart()
        f0_w = ffn_region.take([P, 2, C, I0])
        f0_down = ffn_region.take([P, I0 // P, D])
        act_f = scratch.take([P, I0])
        hid = scratch.take([P, I0])
        mag = scratch.take([P, I0])
        beats = scratch.take([P, 6, I0 // 4], BF16)
        wins = scratch.take([P, 4, I0 // 4], BF16)
        hidT = scratch.take([P, I0 // P, P])

        s_f0_load = sem("f0_load")
        s_gate = sem("gate_ready")
        s_up = sem("up_ready")
        s_act = sem("act_ready")
        s_hid = sem("hidden_ready")
        s_mag = sem("magnitude_ready")
        s_kept = sem("hidden_kept")
        s_htT = sem("hidden_turned")
        s_ht = sem("hidden_turn_out")
        s_fy = sem("ffn_out_ready")

        gate_ps = bank(1, 2)
        up_ps = bank(3, 2)
        ht_ps = bank(5, 2)

        def l0_ffn_sync(sp):
            sp.dma_start(f0_w[:, :, :, :], A["f0_w"]).then_inc(s_f0_load, 16)
            sp.dma_start(f0_down[:, :, :], A["f0_down"]).then_inc(s_f0_load, 16)

        def l0_ffn_gpsimd(pool):
            with pool.Fori(0, B) as i:
                ln_gpsimd(pool, i + B)

        def l0_ffn_tensor(pe, turns):
            pe.wait_ge(s_f0_load, 32)
            pe.wait_ge(s_res, NT)
            with pe.Fori(0, B) as i:
                turns.loop(i, 1)
                pe.wait_ge(s_ln_norm, i + B + 1)
                turn_batch(pe, turns, xn)
                pe.wait_ge(s_turn_out, turns.now())
                for j in range(TB):
                    pe.wait_ge(s_hid, i * TB + j)
                    for w, ps, ready in ((0, gate_ps, s_gate), (1, up_ps, s_up)):
                        for n in range(I0 // BANK):
                            for c in range(C):
                                ins = pe.matmul(ps[:, n * BANK:(n + 1) * BANK], xT[:, c, j * P:(j + 1) * P],
                                                f0_w[:, w, c, n * BANK:(n + 1) * BANK],
                                                start=(c == 0), stop=(c == C - 1))
                        ins.then_inc(ready, 1)
                for j in range(TB):
                    pe.wait_ge(s_kept, i * TB + j + 1)
                    pe.wait_ge(s_ht, i * TB + j)
                    for g in range(I0 // P):
                        ins = pe.transpose(ht_ps[:, g * P:(g + 1) * P], hid[:, g * P:(g + 1) * P], ident[:, :])
                    ins.then_inc(s_htT, 1)
                    pe.wait_ge(s_ht, i * TB + j + 1)
                    pe.wait_ge(s_res, i * TB + j + NT)
                    for g in range(I0 // P):
                        ins = pe.matmul(y_ps, hidT[:, g, :], f0_down[:, g, :], start=(g == 0), stop=(g == I0 // P - 1))
                    ins.then_inc(s_fy, 1)
            turns.end_loop(B)

        def l0_ffn_scalar(act, turns):
            with act.Fori(0, B) as i:
                turns.loop(i, 1)
                turn_evac(act, turns, xT)
                for j in range(TB):
                    act.wait_ge(s_gate, i * TB + j + 1)
                    act.wait_ge(s_hid, i * TB + j)
                    act.activation(act_f[:, :], gate_ps, ACT.Tanh, scale=0.5).then_inc(s_act, 1)
                    act.wait_ge(s_hid, i * TB + j + 1)
                    act.wait_ge(s_kept, i * TB + j)
                    act.activation(mag[:, :], hid[:, :], ACT.Abs).then_inc(s_mag, 1)
                    act.wait_ge(s_htT, i * TB + j + 1)
                    act.wait_ge(s_fy, i * TB + j)
                    act.activation(hidT[:, :, :].rearrange("p g q -> p (g q)"), ht_ps, ACT.Copy).then_inc(s_ht, 1)
            turns.end_loop(B)

        def l0_ffn_vector(dve, st):
            quad = lambda v: v.rearrange("p (n f) -> p f n", f=4)
            with dve.Fori(0, B) as i:
                st.loop(i, 4 + TB * 12)
                ln_vector(dve, st, i, i + B)
                ln_apply(dve, i, i + 13)
                for j in range(TB):
                    dve.wait_ge(s_act, i * TB + j + 1)
                    st.done(dve.scalar_tensor_tensor(out=act_f[:, :], in0=act_f[:, :], scalar=1.0, in1=gate_ps,
                                                     op0=ALU.add, op1=ALU.mult))
                    dve.wait_ge(s_up, i * TB + j + 1)
                    dve.wait_ge(s_htT, i * TB + j)
                    dve.scalar_tensor_tensor(out=hid[:, :], in0=act_f[:, :], scalar=0.5, in1=up_ps,
                                             op0=ALU.mult, op1=ALU.mult).then_inc(s_hid, 1)
                    dve.wait_ge(s_mag, i * TB + j + 1)
                    m = quad(mag[:, :])
                    for first, n, at in ((0, 3, 0), (1, 2, 3), (2, 1, 5)):
                        st.mark(dve.tensor_tensor(beats[:, at:at + n, :],
                                                  m[:, first:first + 1, :].to_broadcast([P, n, I0 // 4]),
                                                  m[:, first + 1:4, :], ALU.is_ge))
                    st.wait()
                    for v, (a, b, op) in enumerate(((0, 1, ALU.add), (3, 4, ALU.add), (5, 1, ALU.subtract), (2, 4, ALU.add))):
                        st.mark(dve.tensor_tensor(wins[:, v, :], beats[:, a, :], beats[:, b, :], op))
                    st.wait()
                    for v, (c, op) in enumerate(((2, ALU.add), (0, ALU.subtract), (3, ALU.subtract), (5, ALU.add))):
                        st.mark(dve.tensor_tensor(wins[:, v, :], wins[:, v, :], beats[:, c, :], op))
                    st.wait()
                    h = quad(hid[:, :])
                    for v, (bound, op) in enumerate(((2.0, ALU.is_ge), (1.0, ALU.is_ge), (0.0, ALU.is_ge), (1.0, ALU.is_le))):
                        ins = dve.scalar_tensor_tensor(out=h[:, v, :], in0=wins[:, v, :], scalar=bound, in1=h[:, v, :],
                                                       op0=op, op1=ALU.mult)
                    ins.then_inc(s_kept, 1)
                add_residual(dve, i, 1, s_fy)
            st.end_loop(B)

        def add_residual(dve, i, gate, ready):
            for j in range(TB):
                dve.wait_ge(ready, i * TB + j + 1)
                dve.scalar_tensor_tensor(out=tile_of(x, i * TB + j), in0=y_ps, scalar=gates[:, gate:gate + 1],
                                         in1=tile_of(x, i * TB + j), op0=ALU.mult, op1=ALU.add).then_inc(s_res, 1)

        scratch.restart()
        attn_region.restart()
        l1_kvc = attn_region.take([P, C, KC1])
        l1_dq = attn_region.take([P, C, QC1])
        l1_uqT = attn_region.take([P, H1, QC1])
        l1_qr = attn_region.take([QC1, 2, H1 * R1])
        l1_uk = attn_region.take([KC1, H1 * HD1])
        l1_kr = attn_region.take([KC1, 2, P])
        l1_uv = attn_region.take([KC1, H1 * HD1])
        l1_wo = attn_region.take([P, H1, D])
        l1_keys = attn_region.take([QC1, B, H1, SK])
        l1_vals = attn_region.take([P, B, H1 // 2, D])
        l1_cos = scratch.take([P, S])
        l1_sin = scratch.take([P, S])
        kvT = scratch.take([KC1, CT])
        kv_h = scratch.take([P, 2, 2, CT])
        krot = scratch.take([P, 2, CT])
        krdiag = scratch.take([P, B, 2, SK])
        qcT = scratch.take([QC1, S])
        qrot = scratch.take([P, 2, 2, S])
        qrT = scratch.take([P, H1 // 2, S])
        seg_i = sb("seg_i", [P, NT], I32)
        seg = scratch.take([P, NT])
        key_at = scratch.take([P, SK])
        key_last = scratch.take([P, SK])
        seen = scratch.take([P, NT, SK])
        unseen = scratch.take([P, NT, SK])

        s_l1_load = sem("l1_load")
        s_kvT = sem("kv_compressed")
        s_kvT_out = sem("kv_compressed_out")
        s_kr = sem("keys_to_rotate")
        s_krdiag = sem("rotated_keys_ready")
        s_kvh = sem("head_kv_ready")
        s_kvh_out = sem("head_kv_out")
        s_keys = sem("head_keys_ready")
        s_keys_out = sem("head_keys_out")
        s_vals = sem("pair_values_ready")
        s_vals_out = sem("pair_values_out")
        s_qc = sem("queries_compressed")
        s_qc_out = sem("queries_compressed_out")
        s_qr = sem("queries_to_rotate")
        s_qrot = sem("queries_multiplied")
        s_qrT = sem("queries_rotated")
        s_prob = sem("probs_ready")

        L1_LOADS = 13
        l1_names = ("l1_kvc", "l1_dq", "l1_uqT", "l1_qr", "l1_uk", "l1_kr", "l1_uv", "l1_wo")

        def l1_attn_sync(sp):
            sp.wait_ge(s_res, NT)
            for dst, name in zip((l1_kvc, l1_dq, l1_uqT, l1_qr, l1_uk, l1_kr, l1_uv, l1_wo), l1_names):
                sp.dma_start(dst, A[name]).then_inc(s_l1_load, 16)
            sp.dma_start(seg_i[:, :], A["seg"]).then_inc(s_l1_load, 16)
            sp.wait_ge(s_res, 2 * NT)
            for dst, name in ((l1_cos, "l1_cos"), (l1_sin, "l1_sin"), (key_at, "key_at"), (key_last, "key_last")):
                sp.dma_start(dst, A[name]).then_inc(s_l1_load, 16)

        def l1_attn_gpsimd(pool):
            with pool.Fori(0, B) as i:
                ln_gpsimd(pool, i + 2 * B)
                for g in range(4):
                    pool.wait_ge(s_qrot, i * 4 + g + 1)
                    pool.wait_ge(s_score, i * TB + NT)
                    pool.tensor_tensor(qrT[:, 2 * g:2 * g + 2, :], qrot[:, 0, :, :], qrot[:, 1, :, :],
                                       ALU.add).then_inc(s_qrT, 1)

        kvh_ps = [bank(1 + k).rearrange("p (a n) -> p a n", a=2) for k in range(2)]
        keys_ps = bank(3).rearrange("p (a n) -> p a n", a=2)
        vals_ps = [bank(4, 2), bank(6, 2)]
        qr_ps = [[bank(1), bank(2)], [bank(4), bank(5)]]
        sc1_ps = bank(2, 2)

        def l1_attn_tensor(pe, turns):
            pe.wait_ge(s_l1_load, 16 * L1_LOADS)
            pe.wait_ge(s_res, 2 * NT)
            for c in range(C):
                ins = pe.matmul(kvh_ps[0][0:KC1, 0, :], l1_kvc[:, c, :], ctxT[:, c, :], start=(c == 0), stop=(c == C - 1))
            ins.then_inc(s_kvT, 1)
            pe.wait_ge(s_kvT_out, 1)
            for a in range(2):
                ins = pe.matmul(keys_ps[:, a, :], l1_kr[:, a, :], kvT, start=True, stop=True)
            ins.then_inc(s_kr, 1)

            def head_kv(h):
                if h >= 2:
                    pe.wait_ge(s_kvh_out, h - 1)
                pe.matmul(kvh_ps[h % 2][:, 0, :], l1_uk[:, h * HD1:(h + 1) * HD1], kvT, start=True, stop=True)
                pe.matmul(kvh_ps[h % 2][:, 1, :], l1_uv[:, h * HD1:(h + 1) * HD1], kvT, start=True, stop=True)\
                  .then_inc(s_kvh, 1)

            head_kv(0)
            pe.wait_ge(s_krdiag, 1)
            for h in range(H1):
                if h + 1 < H1:
                    head_kv(h + 1)
                pe.wait_ge(s_kvh_out, h + 1)
                if h >= 2:
                    pe.wait_ge(s_keys_out, h - 1)
                pe.matmul(keys_ps[0:QC1, h % 2, :], l1_uqT[:, h, :], kv_h[:, h % 2, 0, :],
                          start=True, stop=True).then_inc(s_keys, 1)
                if h % 2 == 0 and h >= 4:
                    pe.wait_ge(s_vals_out, h // 2 - 1)
                for b in range(B):
                    ins = pe.matmul(vals_ps[h // 2 % 2][SK * (h % 2):SK * (h % 2) + SK, b * D:(b + 1) * D],
                                    kv_h[:, h % 2, 1, b * SK:(b + 1) * SK], l1_wo[:, h, :], start=True, stop=True)
                ins.then_inc(s_vals, 1)
            pe.wait_ge(s_vals_out, H1 // 2)
            pe.wait_ge(s_keys_out, H1)
            with pe.Fori(0, B) as i:
                turns.loop(i, 1)
                pe.wait_ge(s_ln_norm, i + 2 * B + 1)
                turn_batch(pe, turns, xn)
                pe.wait_ge(s_turn_out, turns.now())
                for c in range(C):
                    ins = pe.matmul(pv_ps[0:QC1, :], l1_dq[:, c, :], xT[:, c, :], start=(c == 0), stop=(c == C - 1))
                ins.then_inc(s_qc, 1)
                pe.wait_ge(s_qc_out, i + 1)
                pe.wait_ge(s_shift, i * TB + NT)
                for g in range(4):
                    if g >= 2:
                        pe.wait_ge(s_qrot, i * 4 + g - 1)
                    for a in range(2):
                        for k in range(2):
                            h = 2 * (2 * g + k)
                            ins = pe.matmul(qr_ps[g % 2][a][:, k * S:(k + 1) * S], l1_qr[:, a, h * R1:(h + 2) * R1], qcT,
                                            start=True, stop=True)
                    ins.then_inc(s_qr, 1)
                pe.wait_ge(s_qrT, i * 4 + 4)
                for j in range(TB):
                    pe.wait_ge(s_shift, i * TB + j + NT)
                    for n in range(2):
                        keys = l1_keys[:, bass.ds(i, 1), 8 * n:8 * n + 8, :].rearrange("p a h k -> p (a h k)")
                        pe.matmul(sc1_ps[:, n * BANK:(n + 1) * BANK], qcT[:, j * P:(j + 1) * P], keys,
                                  start=True, stop=False)
                        for g in range(4 * n, 4 * n + 4):
                            ins = pe.matmul(sc1_ps[:, g * P:(g + 1) * P], qrT[:, g, j * P:(j + 1) * P],
                                            krdiag[:, bass.ds(i, 1), :, :].rearrange("p b a k -> p (b a k)"),
                                            start=False, stop=(g % 4 == 3))
                    ins.then_inc(s_score, 1)
                    pe.wait_ge(s_prob, i * TB + j + 1)
                    pe.wait_ge(s_pt, i * TB + j + NT)
                    for g in range(8):
                        ins = pe.transpose(pt_ps[:, g * P:(g + 1) * P], prob[:, g * P:(g + 1) * P], ident[:, :])
                    ins.then_inc(s_ptT, 1)
                    pe.wait_ge(s_pt, i * TB + j + NT + 1)
                    pe.wait_ge(s_res, i * TB + j + 2 * NT)
                    for g in range(8):
                        ins = pe.matmul(y_ps, probT[:, g, :],
                                        l1_vals[:, bass.ds(i, 1), g, :].rearrange("p b n -> p (b n)"),
                                        start=(g == 0), stop=(g == 7))
                    ins.then_inc(s_y, 1)
            turns.end_loop(B)

        def l1_attn_scalar(act, turns):
            act.wait_ge(s_kvT, 1)
            act.activation(kvT, kvh_ps[0][0:KC1, 0, :], ACT.Copy).then_inc(s_kvT_out, 1)
            for h in range(H1):
                act.wait_ge(s_kvh, h + 1)
                if h >= 2:
                    act.wait_ge(s_vals, h - 1)
                act.activation(kv_h[:, h % 2, :, :], kvh_ps[h % 2], ACT.Copy).then_inc(s_kvh_out, 1)
                act.wait_ge(s_keys, h + 1)
                act.activation(l1_keys[:, :, h, :], keys_ps[0:QC1, h % 2, :].rearrange("p (b k) -> p b k", b=B),
                               ACT.Copy).then_inc(s_keys_out, 1)
            with act.Fori(0, B) as i:
                turns.loop(i, 1)
                turn_evac(act, turns, xT)
                act.wait_ge(s_qc, i + 1)
                act.wait_ge(s_score, i * TB + NT)
                act.activation(qcT, pv_ps[0:QC1, :], ACT.Copy).then_inc(s_qc_out, 1)
                for j in range(TB):
                    act.wait_ge(s_shift, i * TB + j + NT + 1)
                    act.activation(prob[:, :], prob[:, :], ACT.Exp, scale=(HD1 + R1) ** -0.5).then_inc(s_exp, 1)
                    act.wait_ge(s_ptT, i * TB + j + NT + 1)
                    act.wait_ge(s_y, i * TB + j + NT)
                    act.activation(probT[:, :, :].rearrange("p g q -> p (g q)"), pt_ps, ACT.Copy).then_inc(s_pt, 1)
            turns.end_loop(B)

        def l1_attn_vector(dve, st):
            dve.wait_ge(s_l1_load, 16 * L1_LOADS)
            st.done(dve.tensor_copy(seg, seg_i[:, :]))
            wide = lambda v, axis: v.unsqueeze(axis).to_broadcast([P, NT, SK])
            st.mark(dve.tensor_tensor(seen, wide(key_at, 1), wide(seg, 2), ALU.is_le))
            st.done(dve.tensor_tensor(unseen, wide(key_last, 1), wide(seg, 2), ALU.is_ge))
            st.done(dve.tensor_tensor(unseen, unseen, seen, ALU.mult))
            st.done(dve.tensor_scalar(unseen, unseen, -1.0, 1e30, ALU.add, ALU.mult))
            dve.wait_ge(s_kr, 1)
            for a, table in enumerate((l1_cos, l1_sin)):
                st.mark(dve.tensor_tensor(krot[:, a, :].rearrange("p (b k) -> p b k", b=B),
                                          keys_ps[:, a, :].rearrange("p (b k) -> p b k", b=B),
                                          table[:, 0:SK].unsqueeze(1).to_broadcast([P, B, SK]), ALU.mult))
            st.wait()
            st.done(dve.tensor_tensor(krot[:, 0, :], krot[:, 0, :], krot[:, 1, :], ALU.add))
            for b in range(B):
                ins = st.mark(dve.tensor_tensor(krdiag[:, b, :, :],
                                                krot[:, 0:1, b * SK:(b + 1) * SK].to_broadcast([P, 2, SK]),
                                                half_of[:, :].unsqueeze(2).to_broadcast([P, 2, SK]), ALU.mult))
            st.wait()
            dve.engine_nop().then_inc(s_krdiag, 1)
            for g in range(H1 // 2):
                dve.wait_ge(s_vals, 2 * g + 2)
                dve.tensor_copy(l1_vals[:, :, g, :], vals_ps[g % 2].rearrange("p (b n) -> p b n", b=B)).then_inc(s_vals_out, 1)
            with dve.Fori(0, B) as i:
                st.loop(i, 4 + TB * 4)
                ln_vector(dve, st, i, i + 2 * B)
                ln_apply(dve, i, i + 17)
                for g in range(4):
                    dve.wait_ge(s_qr, i * 4 + g + 1)
                    dve.wait_ge(s_qrT, i * 4 + g)
                    for a, table in enumerate((l1_cos, l1_sin)):
                        ins = dve.tensor_tensor(qrot[:, a, :, :], qr_ps[g % 2][a].rearrange("p (k s) -> p k s", k=2),
                                                table.unsqueeze(1).to_broadcast([P, 2, S]), ALU.mult)
                    ins.then_inc(s_qrot, 1)
                for j in range(TB):
                    heads = lambda v: v.rearrange("p (h k) -> p h k", h=H1)
                    per_head = lambda v: v[:, 0:H1].unsqueeze(2).to_broadcast([P, H1, SK])
                    dve.wait_ge(s_score, i * TB + j + NT + 1)
                    dve.wait_ge(s_ptT, i * TB + j + NT)
                    st.done(dve.tensor_tensor(heads(prob[:, :]), heads(sc1_ps),
                                              unseen[:, bass.ds(i * TB + j, 1), :].to_broadcast([P, H1, SK]), ALU.add))
                    st.done(dve.tensor_reduce(top[:, 0:H1], heads(prob[:, :]), AX, ALU.max))
                    dve.tensor_tensor(heads(prob[:, :]), heads(prob[:, :]), per_head(top), ALU.subtract).then_inc(s_shift, 1)
                    dve.wait_ge(s_exp, i * TB + j + NT + 1)
                    st.done(dve.tensor_reduce(total[:, 0:H1], heads(prob[:, :]), AX, ALU.add))
                    st.done(dve.reciprocal(total[:, 0:H1], total[:, 0:H1]))
                    dve.tensor_tensor(heads(prob[:, :]), heads(prob[:, :]), per_head(total), ALU.mult).then_inc(s_prob, 1)
                for j in range(TB):
                    dve.wait_ge(s_y, i * TB + j + NT + 1)
                    dve.scalar_tensor_tensor(out=tile_of(x, i * TB + j), in0=y_ps, scalar=gates[:, 2:3],
                                             in1=tile_of(x, i * TB + j), op0=ALU.mult, op1=ALU.add).then_inc(s_res, 1)
            st.end_loop(B)

        SLOTS = 4
        UNITS = 2 * SLOTS
        HT = T // 2
        scratch.restart()
        ffn_region.restart()
        xT_all = scratch.take([P, C, T])
        weight_of = scratch.take([P, NT, E3 + 1])
        act_u = scratch.take([P, 2, HT])
        hid_u = scratch.take([P, 2, HT])
        expert_w = ffn_region.take([P, SLOTS, 3 * D])
        r_top = scratch.take([P, TB, 1])
        r_sum = scratch.take([P, TB, 1])
        moe_mark = scratch.at

        s_xall = sem("all_transposed")
        s_expert = [sem(f"expert_loaded_{k}") for k in range(SLOTS)]
        s_ugate = sem("unit_gate_ready")
        s_uup = sem("unit_up_ready")
        s_uact = sem("unit_act_ready")
        s_uhid = sem("unit_hidden_ready")
        s_udown = sem("unit_down_ready")
        s_uadd = sem("unit_tile_added")
        s_logit = sem("logits_ready")
        s_rshift = sem("logits_shifted")
        s_rexp = sem("router_exp_ready")
        s_routed = sem("router_done")

        gate_u = [bank(1), bank(2)]
        up_u = [bank(3), bank(4)]
        down_u = [bank(5, 2), None]
        down_banks = [(5, 6), (7, 0)]

        def down_of(k, q):
            b = down_banks[k][q // 2]
            return bank(b)[:, (q % 2) * D:(q % 2 + 1) * D]

        def experts_sync(sp, name, experts, before, units_before):
            for k in range(SLOTS):
                sp.dma_start(expert_w[:, k, :], A[name][k]).then_inc(s_expert[k], 16)
            if experts > 2 * SLOTS:
                with sp.Fori(1, experts // SLOTS) as t:
                    for k in range(SLOTS):
                        sp.wait_ge(s_udown, t * UNITS + (units_before + 2 * k + 2 + 2 - UNITS))
                        sp.dma_start(expert_w[:, k, :],
                                     A[name][bass.ds(t * SLOTS + k, 1), :, :].rearrange("e p n -> p (e n)"))\
                          .then_inc(s_expert[k], 16)
            if experts % SLOTS:
                sp.wait_ge(s_udown, 2 * experts + (units_before + 2 - UNITS))
                sp.dma_start(expert_w[:, 0, :], A[name][experts - 1]).then_inc(s_expert[0], 16)

        def unit_loop(eng, experts, unit):
            turns = (experts - 1) // SLOTS
            with eng.Fori(0, turns) as t:
                for u in range(UNITS):
                    unit(t, u, True)
            left = 2 * experts - turns * UNITS
            for u in range(left):
                unit(turns, u, u + 1 < left)

        def experts_tensor(pe, experts, before, units_before):
            def gate_up(t, u):
                k = u // 2 % SLOTS
                if u % 2 == 0:
                    pe.wait_ge(s_expert[k], (t + u // UNITS) * 16 + 16 * (before[k] + 1))
                pe.wait_ge(s_uhid, t * UNITS + (units_before + u + 1))
                for a, ps, ready in ((0, gate_u, s_ugate), (1, up_u, s_uup)):
                    for c in range(C):
                        at = (2 * c + a) * I1
                        ins = pe.matmul(ps[u % 2], expert_w[:, k, at:at + I1],
                                        xT_all[:, c, (u % 2) * HT:(u % 2 + 1) * HT], start=(c == 0), stop=(c == C - 1))
                    ins.then_inc(ready, 1)

            def down(t, u):
                pe.wait_ge(s_uhid, t * UNITS + (units_before + u + 1 + 2))
                pe.wait_ge(s_uadd, t * (4 * UNITS) + 4 * (units_before + u + 1))
                for q in range(4):
                    ins = pe.matmul(down_of(u % 2, q), hid_u[:, u % 2, q * P:(q + 1) * P],
                                    expert_w[:, u // 2, 2 * D:3 * D], start=True, stop=True)
                ins.then_inc(s_udown, 1)

            def unit(t, u, more):
                if more:
                    gate_up(t, u + 1)
                down(t, u)

            gate_up(0, 0)
            unit_loop(pe, experts, unit)

        def experts_scalar(act, experts, units_before):
            def tanh(t, u):
                act.wait_ge(s_ugate, t * UNITS + (units_before + u + 1))
                act.wait_ge(s_uhid, t * UNITS + (units_before + u + 1))
                act.activation(act_u[:, u % 2, :], gate_u[u % 2], ACT.Tanh, scale=0.5).then_inc(s_uact, 1)

            tanh(0, 0)
            unit_loop(act, experts, lambda t, u, more: tanh(t, u + 1) if more else None)

        def experts_vector(dve, st, experts, units_before):
            def hidden(t, u):
                k = u % 2
                dve.wait_ge(s_uact, t * UNITS + (units_before + u + 1))
                ins = dve.scalar_tensor_tensor(out=act_u[:, k, :], in0=act_u[:, k, :], scalar=1.0, in1=gate_u[k],
                                               op0=ALU.add, op1=ALU.mult)
                ins.then_inc(s_uown, 1)
                dve.wait_ge(s_uown, t * UNITS + (units_before + u + 1))
                dve.wait_ge(s_uup, t * UNITS + (units_before + u + 1))
                dve.wait_ge(s_udown, t * UNITS + (units_before + u + 1))
                dve.scalar_tensor_tensor(out=hid_u[:, k, :], in0=act_u[:, k, :], scalar=0.5, in1=up_u[k],
                                         op0=ALU.mult, op1=ALU.mult).then_inc(s_uhid, 1)

            def add(t, u):
                dve.wait_ge(s_udown, t * UNITS + (units_before + u + 1 + 2))
                dve.wait_ge(s_uadd, t * (4 * UNITS) + 4 * (units_before + u + 1))
                for q in range(4):
                    n = (u % 2) * 4 + q
                    weight = weight_of[:, n, bass.ds(t * SLOTS + u // 2, 1)]
                    dve.scalar_tensor_tensor(out=x[:, n, :], in0=down_of(u % 2, q), scalar=weight, in1=x[:, n, :],
                                             op0=ALU.mult, op1=ALU.add).then_inc(s_uadd, 1)

            def unit(t, u, more):
                if more:
                    hidden(t, u + 1)
                add(t, u)

            hidden(0, 0)
            unit_loop(dve, experts, unit)
            dve.wait_ge(s_uadd, 4 * (units_before + 2 * experts + 2))
            dve.engine_nop().then_inc(s_res, NT)

        s_uown = sem("unit_act_times_gate")

        W1 = E1 + 8
        f1_router = scratch.take([P, C, E1])
        f1_bias = scratch.take([1, E1])
        below = scratch.take([P, 8])
        r_prob = scratch.take([P, TB, W1])
        r_rest = scratch.take([P, TB, W1])
        r_eight = scratch.take([P, TB, 8])
        r_two = scratch.take([P, TB, 8])

        s_f1_load = sem("f1_load")
        logit_ps = bank(6)

        def l1_ffn_sync(sp):
            sp.wait_ge(s_res, 3 * NT)
            sp.dma_start(f1_router, A["f1_router"]).then_inc(s_f1_load, 16)
            sp.dma_start(f1_bias, A["f1_bias"]).then_inc(s_f1_load, 16)
            sp.dma_start(below, A["below"]).then_inc(s_f1_load, 16)
            experts_sync(sp, "f1_experts", E1 + 1, 0, 0)

        def router_tensor(pe, turns, n, r, load, load_at, router, experts, bias):
            pe.wait_ge(load, load_at)
            with pe.Fori(0, B) as i:
                turns.loop(i, 1)
                pe.wait_ge(s_ln_norm, i + n + 1)
                turn_batch(pe, turns, xn)
                pe.wait_ge(s_turn_out, turns.now())
                pe.wait_ge(s_rshift, i + r)
                for j in range(TB):
                    ps = logit_ps[:, j * experts:(j + 1) * experts]
                    if bias is not None:
                        pe.matmul(ps, ones[:, :], bias, start=True, stop=False)
                    for c in range(C):
                        ins = pe.matmul(ps, xT[:, c, j * P:(j + 1) * P], router[:, c, :],
                                        start=(bias is None and c == 0), stop=(c == C - 1))
                ins.then_inc(s_logit, 1)
            turns.end_loop(B)

        def router_scalar(act, turns, r, probs):
            with act.Fori(0, B) as i:
                turns.loop(i, 1)
                act.wait_ge(s_logit, i + r)
                act.wait_ge(s_xall, i + r)
                turn_evac(act, turns, xT)
                act.wait_ge(s_rshift, i + r + 1)
                act.activation(probs, probs, ACT.Exp).then_inc(s_rexp, 1)
            turns.end_loop(B)

        def router_gpsimd(pool, n, turns_before, r):
            with pool.Fori(0, B) as i:
                ln_gpsimd(pool, i + n)
                pool.wait_ge(s_turn_out, i + turns_before + 1)
                pool.tensor_copy(xT_all[:, :, bass.ds(i * S, S)], xT[:, :, :]).then_inc(s_xall, 1)

        def router_softmax(dve, st, i, r, probs, experts):
            logits = logit_ps[:, 0:TB * experts].rearrange("p (j e) -> p j e", j=TB)
            spread = lambda v: v.to_broadcast([P, TB, experts])
            dve.wait_ge(s_logit, i + r + 1)
            st.done(dve.tensor_reduce(r_top[:, :, 0], logits, AX, ALU.max))
            dve.tensor_tensor(probs, logits, spread(r_top), ALU.subtract).then_inc(s_rshift, 1)
            dve.wait_ge(s_rexp, i + r + 1)
            st.done(dve.tensor_reduce(r_sum[:, :, 0], probs, AX, ALU.add))
            st.done(dve.reciprocal(r_sum, r_sum))
            st.mark(dve.tensor_tensor(probs, probs, spread(r_sum), ALU.mult))
            st.wait()
            settle(dve)

        def l1_ffn_tensor(pe, turns):
            router_tensor(pe, turns, 3 * B, 0, s_f1_load, 48, f1_router, E1, f1_bias)
            pe.wait_ge(s_xall, B)
            pe.wait_ge(s_rshift, B)
            experts_tensor(pe, E1 + 1, [0] * SLOTS, 0)

        def l1_ffn_scalar(act, turns):
            router_scalar(act, turns, 0, r_prob[:, :, 0:E1])
            experts_scalar(act, E1 + 1, 0)

        def l1_ffn_gpsimd(pool):
            router_gpsimd(pool, 3 * B, 21, 0)

        def l1_ffn_vector(dve, st):
            dve.engine_nop().then_inc(s_uhid, 2)
            dve.engine_nop().then_inc(s_udown, 2)
            dve.engine_nop().then_inc(s_uadd, 8)
            dve.wait_ge(s_f1_load, 48)
            st.mark(dve.memset(weight_of[:, :, E1:E1 + 1], 1.0))
            for j in range(TB):
                st.mark(dve.tensor_copy(r_prob[:, j, E1:W1], below))
                st.mark(dve.tensor_copy(r_two[:, j, :], below))
            st.wait()
            with dve.Fori(0, B) as i:
                st.loop(i, 4 + 4 + 2 + 1 + 2 + 1 + 1 + 1 + 1 + 1 + 1)
                ln_vector(dve, st, i, i + 3 * B)
                ln_apply(dve, i, i + 21)
                probs = r_prob[:, :, 0:E1]
                spread = lambda v: v.to_broadcast([P, TB, E1])
                router_softmax(dve, st, i, 0, probs, E1)
                for j in range(TB):
                    st.mark(dve.max(r_eight[:, j, :], r_prob[:, j, 0:E1]))
                st.wait()
                st.mark(dve.tensor_copy(r_two[:, :, 0:2], r_eight[:, :, 0:2]))
                st.wait()
                settle(dve)
                for j in range(TB):
                    st.mark(dve.match_replace(out=r_rest[:, j, :], in_to_replace=r_two[:, j, :],
                                              in_values=r_prob[:, j, :], imm_value=-9.0))
                st.wait()
                st.done(dve.tensor_tensor(r_rest[:, :, 0:E1], r_rest[:, :, 0:E1], probs, ALU.not_equal))
                st.done(dve.tensor_tensor(r_rest[:, :, 0:E1], r_rest[:, :, 0:E1], probs, ALU.mult))
                st.done(dve.tensor_reduce(r_sum[:, :, 0], r_rest[:, :, 0:E1], AX, ALU.add))
                st.done(dve.tensor_scalar(r_sum, r_sum, 1e-9, None, ALU.add))
                st.done(dve.reciprocal(r_sum, r_sum))
                st.done(dve.tensor_tensor(weight_of[:, bass.ds(i * TB, TB), 0:E1], r_rest[:, :, 0:E1],
                                          spread(r_sum), ALU.mult))
            st.end_loop(B)
            st.done(dve.tensor_scalar(weight_of[:, :, 0:E1 + 1], weight_of[:, :, 0:E1 + 1], gates[:, 3:4], None, ALU.mult))
            dve.wait_ge(s_turned, 25)
            experts_vector(dve, st, E1 + 1, 0)

        scratch.restart()
        attn_region.restart()
        HG = 4
        SELF = H2 // HG
        CROSS = C
        TU = SELF + CROSS
        BU = TB * TU
        l2_w = attn_region.take([P, 6, C, D])
        l2_ctxT2 = attn_region.take([P, C, B, P])
        l2_cos = attn_region.take([P, S])
        l2_sin = attn_region.take([P, S])
        quad_of = attn_region.take([P, HG])
        l2_head_of = attn_region.take([P, H2 // C])
        l2_half = attn_region.take([P, 2])
        l2_gate = attn_region.take([P, H2])
        l2_kT = attn_region.take([P, C, S])
        l2_akT = attn_region.take([P, C, CT])
        l2_av = attn_region.take([P, B, D])
        l2_kdiag = attn_region.take([P, C, HG, S])
        l2_akdiag = attn_region.take([P, C, H2 // C, SK])
        l2_avdiag = attn_region.take([P, H2 // 2, 2, HD2])
        l2_mask = attn_region.take([P, TB, S])
        l2_v = attn_region.take([P, TB, D])
        l2_qT = attn_region.take([P, C, S])
        l2_rot = attn_region.take([P, 2, 2, C * S])
        l2_heads = attn_region.take([P, TB, D])
        l2_cross = attn_region.take([P, D])
        l2_oT = attn_region.take([P, C, S])
        l2_prob = attn_region.take([P, 2, 1024])
        l2_probT = attn_region.take([P, 2, 8, P])
        l2_max = attn_region.take([P, 2, HG])
        l2_neg = attn_region.take([P, 2, HG])
        l2_cmax = attn_region.take([P, 2, H2 // 2])
        l2_sum = attn_region.take([P, TB, H2])
        l2_csum = attn_region.take([P, TB, H2])

        s_l2_load = sem("l2_load")
        s_mask = sem("mask_loaded")
        s_mask_ok = sem("mask_clamped")
        s_l2_ctx = sem("l2_context_projected")
        s_l2_ctx_out = sem("l2_context_out")
        s_l2_qk = sem("l2_qk_projected")
        s_l2_v = sem("l2_v_projected")
        s_l2_v_out = sem("l2_v_out")
        s_l2_mul = sem("l2_qk_multiplied")
        s_l2_rot = sem("l2_qk_rotated")
        s_l2_diag = sem("l2_diag_ready")

        l2_sc = [bank(1, 2), bank(3, 2)]
        l2_pt_ps = bank(5, 2)
        l2_self_ps = bank(7)[:, 0:D]
        l2_cross_ps = bank(7)[:, D:2 * D]
        U0 = 2 * NT
        PV0 = NT
        O0 = NT
        V0 = 2 * NT

        def l2_attn_sync(sp):
            sp.wait_ge(s_res, 3 * NT)
            for dst, name in ((l2_w, "l2_w"), (l2_ctxT2, "ctxT2"), (l2_cos, "l2_cos"), (l2_sin, "l2_sin"),
                              (quad_of, "quad_of"), (l2_head_of, "l2_head_of"), (l2_half, "half_of"), (l2_gate, "l2_gate")):
                sp.dma_start(dst, A[name]).then_inc(s_l2_load, 16)
            with sp.Fori(0, B) as i:
                sp.wait_ge(s_shift, i * BU + U0)
                sp.dma_start(l2_mask, A["mask"][:, bass.ds(i * TB, TB), :]).then_inc(s_mask, 16)

        def l2_attn_gpsimd(pool):
            pool.wait_ge(s_l2_load, 16 * 8)
            pool.wait_ge(s_l2_ctx_out, 2)
            with pool.Fori(0, B) as i:
                pool.wait_ge(s_mask, i * 16 + 16)
                settle(pool)
                pool.tensor_scalar(l2_mask, l2_mask, float(np.finfo(np.float32).min), None, ALU.max).then_inc(s_mask_ok, 1)
                ln_gpsimd(pool, i + 4 * B)
                pool.wait_ge(s_score, i * BU + U0)
                pool.wait_ge(s_pv, i * BU + PV0)
                for a, dst in enumerate((l2_qT, l2_kT)):
                    pool.wait_ge(s_l2_mul, i * 2 + a + 1)
                    pool.tensor_tensor(flat(dst), l2_rot[:, a, 0, :], l2_rot[:, a, 1, :], ALU.add).then_inc(s_l2_rot, 1)
                pool.wait_ge(s_l2_rot, i * 2 + 2)
                for c in range(C):
                    pool.tensor_tensor(l2_kdiag[:, c, :, :], l2_kT[:, c:c + 1, :].to_broadcast([P, HG, S]),
                                       quad_of.unsqueeze(2).to_broadcast([P, HG, S]), ALU.mult)
                    pool.tensor_tensor(l2_akdiag[:, c, :, :],
                                       l2_akT[:, c:c + 1, bass.ds(i * SK, SK)].to_broadcast([P, H2 // C, SK]),
                                       l2_head_of.unsqueeze(2).to_broadcast([P, H2 // C, SK]), ALU.mult)
                pool.tensor_tensor(l2_avdiag, tile_of(l2_av, i).rearrange("p (g a d) -> p g a d", a=2, d=HD2),
                                   l2_half.unsqueeze(1).unsqueeze(3).to_broadcast([P, H2 // 2, 2, HD2]),
                                   ALU.mult).then_inc(s_l2_diag, 1)

        def l2_attn_tensor(pe, turns):
            pe.wait_ge(s_l2_load, 16 * 8)
            pe.wait_ge(s_res, 4 * NT)
            for m in range(C):
                for c in range(C):
                    ins = pe.matmul(bank(1)[:, m * CT:(m + 1) * CT], l2_w[:, 2, c, m * P:(m + 1) * P], ctxT[:, c, :],
                                    start=(c == 0), stop=(c == C - 1))
            ins.then_inc(s_l2_ctx, 1)
            for b in range(B):
                for c in range(C):
                    ins = pe.matmul(bank(3, 2)[:, b * D:(b + 1) * D], l2_ctxT2[:, c, b, :], l2_w[:, 4, c, :],
                                    start=(c == 0), stop=(c == C - 1))
            ins.then_inc(s_l2_ctx, 1)
            pe.wait_ge(s_l2_ctx_out, 2)
            with pe.Fori(0, B) as i:
                turns.loop(i, 2)
                pe.wait_ge(s_ln_norm, i + 4 * B + 1)
                turn_batch(pe, turns, xn)
                pe.wait_ge(s_turn_out, turns.now())
                pe.wait_ge(s_res, i * TB + 4 * NT)
                for a in range(4):
                    for m in range(C):
                        for c in range(C):
                            ins = pe.matmul(bank(1 + a)[:, m * S:(m + 1) * S], l2_w[:, a, c, m * P:(m + 1) * P],
                                            xT[:, c, :], start=(c == 0), stop=(c == C - 1))
                    if a % 2:
                        ins.then_inc(s_l2_qk, 1)
                for m in range(TB):
                    for c in range(C):
                        ins = pe.matmul(bank(5)[:, m * D:(m + 1) * D], xT[:, c, m * P:(m + 1) * P], l2_w[:, 4, c, :],
                                        start=(c == 0), stop=(c == C - 1))
                ins.then_inc(s_l2_v, 1)
                pe.wait_ge(s_l2_diag, i + 1)
                pe.wait_ge(s_l2_v_out, i + 1)

                def scores(u):
                    j, k = u // TU, u % TU
                    pe.wait_ge(s_shift, i * BU + (U0 + u - 1))
                    if k < SELF:
                        c, g = k // 4, k % 4
                        rows = slice(32 * g, 32 * g + 32)
                        for n in range(2):
                            ins = pe.matmul(l2_sc[u % 2][:, n * BANK:(n + 1) * BANK], l2_qT[rows, c, j * P:(j + 1) * P],
                                            l2_kdiag[rows, c, 2 * n:2 * n + 2, :].rearrange("p h k -> p (h k)"),
                                            start=True, stop=True)
                    else:
                        c = k - SELF
                        for n in range(2):
                            ins = pe.matmul(l2_sc[u % 2][:, n * BANK:(n + 1) * BANK], l2_qT[:, c, j * P:(j + 1) * P],
                                            l2_akdiag[:, c, 8 * n:8 * n + 8, :].rearrange("p h k -> p (h k)"),
                                            start=True, stop=True)
                    ins.then_inc(s_score, 1)

                def turn_probs(u):
                    pe.wait_ge(s_exp, i * BU + (U0 + u + 1))
                    pe.wait_ge(s_pt, i * BU + (U0 + u))
                    for g in range(8):
                        ins = pe.transpose(l2_pt_ps[:, g * P:(g + 1) * P], l2_prob[:, u % 2, g * P:(g + 1) * P], ident[:, :])
                    ins.then_inc(s_ptT, 1)

                def weigh(u):
                    j, k = u // TU, u % TU
                    pe.wait_ge(s_pt, i * BU + (U0 + u + 1))
                    if k == 0:
                        pe.wait_ge(s_o, i * TB + (O0 + j))
                    for g in range(8):
                        if k < SELF:
                            h, kt = 4 * k + g // 2, g % 2
                            ins = pe.matmul(l2_self_ps[:, h * HD2:(h + 1) * HD2], l2_probT[:, u % 2, g, :],
                                            l2_v[:, kt, h * HD2:(h + 1) * HD2], start=(kt == 0), stop=(kt == 1))
                        else:
                            pair = 8 * (k - SELF) + g
                            ins = pe.matmul(l2_cross_ps[:, pair * 16:(pair + 1) * 16], l2_probT[:, u % 2, g, :],
                                            l2_avdiag[:, pair, :, :].rearrange("p a d -> p (a d)"), start=True, stop=True)
                    ins.then_inc(s_pv, 1)

                scores(0)
                for u in range(BU + 1):
                    if u + 1 < BU:
                        scores(u + 1)
                    if u < BU:
                        turn_probs(u)
                    if u >= 1:
                        weigh(u - 1)
                pe.wait_ge(s_o, i * TB + (O0 + TB))
                turn_batch(pe, turns, l2_heads)
                pe.wait_ge(s_turn_out, turns.now())
                for j in range(TB):
                    for c in range(C):
                        ins = pe.matmul(bank(1 + 2 * j)[:, 0:D], l2_oT[:, c, j * P:(j + 1) * P], l2_w[:, 5, c, :],
                                        start=(c == 0), stop=(c == C - 1))
                    ins.then_inc(s_y, 1)
            turns.end_loop(B)

        def l2_attn_scalar(act, turns):
            act.wait_ge(s_l2_load, 16 * 8)
            act.activation(l2_gate, l2_gate, ACT.Tanh).then_inc(s_act_own, 1)
            act.wait_ge(s_l2_ctx, 1)
            act.activation(flat(l2_akT), bank(1), ACT.Copy).then_inc(s_l2_ctx_out, 1)
            act.wait_ge(s_l2_ctx, 2)
            act.activation(flat(l2_av), bank(3, 2), ACT.Copy).then_inc(s_l2_ctx_out, 1)
            with act.Fori(0, B) as i:
                turns.loop(i, 2)
                turn_evac(act, turns, xT)
                act.wait_ge(s_l2_v, i + 1)
                act.activation(flat(l2_v), bank(5), ACT.Copy).then_inc(s_l2_v_out, 1)

                def exps(u):
                    j, k = u // TU, u % TU
                    act.wait_ge(s_shift, i * BU + (U0 + u + 1))
                    if k < SELF:
                        for h in range(HG):
                            ins = act.activation(l2_prob[:, u % 2, h * S:(h + 1) * S], l2_prob[:, u % 2, h * S:(h + 1) * S],
                                                 ACT.Exp, bias=l2_neg[:, u % 2, h:h + 1],
                                                 accum_out=l2_sum[:, j, HG * k + h:HG * k + h + 1])
                    else:
                        ins = act.activation(l2_prob[:, u % 2, :], l2_prob[:, u % 2, :], ACT.Exp)
                    ins.then_inc(s_exp, 1)

                def evac(u):
                    act.wait_ge(s_ptT, i * BU + (U0 + u + 1))
                    act.wait_ge(s_pv, i * BU + (PV0 + u - 1))
                    act.activation(l2_probT[:, u % 2, :, :].rearrange("p g q -> p (g q)"), l2_pt_ps, ACT.Copy).then_inc(s_pt, 1)

                exps(0)
                for u in range(BU):
                    if u + 1 < BU:
                        exps(u + 1)
                    evac(u)
                turn_evac(act, turns, l2_oT)
            turns.end_loop(B)

        s_act_own = sem("l2_gate_set")

        def l2_attn_vector(dve, st):
            dve.wait_ge(s_l2_load, 16 * 8)
            dve.wait_ge(s_act_own, 1)
            with dve.Fori(0, B) as i:
                st.loop(i, 4 + TB * (SELF * HG + CROSS * 2 + 5))
                ln_vector(dve, st, i, i + 4 * B)
                ln_apply(dve, i, i * 2 + 25)
                dve.wait_ge(s_l2_rot, i * 2)
                for a in range(2):
                    dve.wait_ge(s_l2_qk, i * 2 + a + 1)
                    for k, table in enumerate((l2_cos, l2_sin)):
                        ins = dve.scalar_tensor_tensor(
                            out=l2_rot[:, a, k, :].rearrange("p (c s) -> p c s", c=C),
                            in0=bank(1 + 2 * a + k).rearrange("p (c s) -> p c s", c=C), scalar=HD2 ** -0.5 if a == 0 else 1.0,
                            in1=table.unsqueeze(1).to_broadcast([P, C, S]), op0=ALU.mult, op1=ALU.mult)
                    ins.then_inc(s_l2_mul, 1)
                dve.wait_ge(s_mask_ok, i + 1)

                def shift(u):
                    j, k = u // TU, u % TU
                    dve.wait_ge(s_score, i * BU + (U0 + u + 1))
                    dve.wait_ge(s_ptT, i * BU + (U0 + u - 1))
                    if j and k < CROSS:
                        st.wait()
                    if k < SELF:
                        settle(dve)
                        for h in range(HG):
                            st.mark(dve.tensor_tensor_reduce(out=l2_prob[:, u % 2, h * S:(h + 1) * S],
                                                             in0=l2_sc[u % 2][:, h * S:(h + 1) * S], in1=l2_mask[:, j, :],
                                                             scale=1.0, scalar=float(np.finfo(np.float32).min),
                                                             op0=ALU.add, op1=ALU.max, accum_out=l2_max[:, u % 2, h:h + 1]))
                        st.wait()
                        dve.tensor_scalar(l2_neg[:, u % 2, :], l2_max[:, u % 2, :], -1.0, None, ALU.mult).then_inc(s_shift, 1)
                    else:
                        heads = lambda v: v.rearrange("p (h k) -> p h k", k=SK)
                        st.done(dve.tensor_reduce(l2_cmax[:, u % 2, :], heads(l2_sc[u % 2]), AX, ALU.max))
                        dve.tensor_tensor(heads(l2_prob[:, u % 2, :]), heads(l2_sc[u % 2]),
                                          l2_cmax[:, u % 2, :].unsqueeze(2).to_broadcast([P, H2 // 2, SK]), ALU.subtract).then_inc(s_shift, 1)

                def sums(u):
                    j, c = u // TU, u % TU - SELF
                    if c >= 0:
                        dve.wait_ge(s_exp, i * BU + (U0 + u + 1))
                        st.mark(dve.tensor_reduce(l2_csum[:, j, 16 * c:16 * c + 16],
                                                  l2_prob[:, u % 2, :].rearrange("p (h k) -> p h k", k=SK), AX, ALU.add))

                def norm(j):
                    heads = lambda v: v.rearrange("p (h d) -> p h d", h=H2)
                    per_head = lambda v: v[:, j, :].unsqueeze(2).to_broadcast([P, H2, HD2])
                    st.wait()
                    st.mark(dve.reciprocal(l2_sum[:, j, :], l2_sum[:, j, :]))
                    st.done(dve.reciprocal(l2_csum[:, j, :], l2_csum[:, j, :]))
                    st.done(dve.tensor_tensor(l2_csum[:, j, :], l2_csum[:, j, :], l2_gate, ALU.mult))
                    dve.wait_ge(s_pv, i * BU + (PV0 + TU * (j + 1)))
                    st.mark(dve.tensor_tensor(heads(l2_heads[:, j, :]), heads(l2_self_ps), per_head(l2_sum), ALU.mult))
                    st.done(dve.tensor_tensor(heads(l2_cross), heads(l2_cross_ps), per_head(l2_csum), ALU.mult))
                    dve.tensor_tensor(l2_heads[:, j, :], l2_heads[:, j, :], l2_cross, ALU.add).then_inc(s_o, 1)

                for u in range(BU):
                    shift(u)
                    if u >= 1:
                        sums(u - 1)
                    if u == TU + 1:
                        norm(0)
                sums(BU - 1)
                norm(1)
                for j in range(TB):
                    dve.wait_ge(s_y, i * TB + (V0 + j + 1))
                    dve.scalar_tensor_tensor(out=tile_of(x, i * TB + j), in0=bank(1 + 2 * j)[:, 0:D], scalar=gates[:, 4:5],
                                             in1=tile_of(x, i * TB + j), op0=ALU.mult, op1=ALU.add).then_inc(s_res, 1)
            st.end_loop(B)

        scratch.restart()
        ffn_region.restart()
        K2 = (I2 + P - 1) // P
        ROUND = 1.5 * 2.0 ** 23
        f2_gate = ffn_region.take([P, C * 2 * I2])
        f2_down = ffn_region.take([P, K2 * D])
        f2_gate_q = ffn_region.take([P, C, 2 * I2], BF16)
        f2_down_q = ffn_region.take([P, K2, D], BF16)
        f2_norm = scratch.take([P, D])
        f2_dnorm = scratch.take([P, I2])
        ident_b = scratch.take([P, P], BF16)
        ones_sq = scratch.take([P, P])
        w_sum = scratch.take([P, 2])
        w_mean = scratch.take([P, 2])
        w_scale = scratch.take([P, 2])
        f2_junk = scratch.take([P, TB, I2])
        row_ss = scratch.take([P, TB])
        row_rms = scratch.take([P, TB])
        row_max = scratch.take([P, TB])
        row_q = scratch.take([P, TB])
        row_y = scratch.take([P, TB])
        row_half = scratch.take([P, TB])
        row_sq = scratch.take([P, TB])
        hrow_ss = scratch.take([P, TB])
        hrow_rms = scratch.take([P, TB])
        hrow_max = scratch.take([P, TB])
        hrow_q = scratch.take([P, TB])
        hrow_y = scratch.take([P, TB])
        f2_xq = scratch.take([P, TB, D], BF16)
        f2_xqT = scratch.take([P, C, S], BF16)
        f2_act = scratch.take([P, TB, I2])
        f2_hq = scratch.take([P, TB, I2], BF16)
        f2_hqT = scratch.take([P, K2, P], BF16)

        s_f2_load = sem("f2_load")
        s_wsum = sem("weights_summed")
        s_wmean = sem("weight_sums_spread")
        s_row_ss = sem("row_squares_summed")
        s_row_ms = sem("row_mean_square_ready")
        s_row_rms = sem("row_rms_ready")
        s_row_norm = sem("rows_normalised")
        s_xq = sem("rows_quantised")
        s_h2 = sem("f2_hidden_ready")
        s_hq = sem("hidden_quantised")

        turn_b = bank(0).bitcast(BF16)
        hq_ps = bank(5).bitcast(BF16)

        def l2_ffn_sync(sp):
            sp.wait_ge(s_res, 4 * NT)
            sp.dma_start(f2_gate, A["f2_gate"]).then_inc(s_f2_load, 16)
            sp.dma_start(f2_down, A["f2_down"]).then_inc(s_f2_load, 16)
            sp.dma_start(f2_norm, A["f2_norm"]).then_inc(s_f2_load, 16)
            sp.dma_start(f2_dnorm, A["f2_dnorm"]).then_inc(s_f2_load, 16)

        def l2_ffn_gpsimd(pool):
            pool.wait_ge(s_res, 4 * NT)
            pool.memset(ones_sq, 1.0).then_inc(s_wsum, 1)
            with pool.Fori(0, B) as i:
                ln_gpsimd(pool, i + 5 * B)
                for k, rms_of in enumerate((row_rms, hrow_rms, hrow_rms)):
                    pool.wait_ge(s_row_ms, i * 3 + k + 1)
                    v = rms_of if k == 0 else rms_of[:, k - 1:k]
                    pool.tensor_tensor(v, v, minus_half[:, 0:v.shape[1]], ALU.pow).then_inc(s_row_rms, 1)

        def l2_ffn_tensor(pe, turns):
            pe.wait_ge(s_res, 5 * NT)
            pe.wait_ge(s_wsum, 3)
            pe.matmul(bank(6)[:, 0:2], ones_sq, w_sum, start=True, stop=True).then_inc(s_wmean, 1)
            with pe.Fori(0, B) as i:
                turns.loop(i, 1)
                pe.wait_ge(s_xq, i + 2)
                pe.wait_ge(s_turn_out, turns.now())
                for c in range(C):
                    for j in range(TB):
                        ins = pe.transpose(turn_b[:, c * S + j * P:c * S + (j + 1) * P], f2_xq[:, j, c * P:(c + 1) * P], ident_b)
                ins.then_inc(s_turned, 1)
                turns.k += 1
                pe.wait_ge(s_turn_out, turns.now())
                for j in range(TB):
                    pe.wait_ge(s_h2, i * TB + j)
                    for a, ps, ready in ((0, gate_ps, s_gate), (1, up_ps, s_up)):
                        for n0, n1 in ((0, BANK), (BANK, I2)):
                            for c in range(C):
                                ins = pe.matmul(ps[:, n0:n1], f2_xqT[:, c, j * P:(j + 1) * P],
                                                f2_gate_q[:, c, a * I2 + n0:a * I2 + n1], start=(c == 0), stop=(c == C - 1))
                        ins.then_inc(ready, 1)
                for j in range(TB):
                    pe.wait_ge(s_hq, i * TB + j + 1)
                    pe.wait_ge(s_ht, i * TB + (NT + j))
                    for k in range(K2):
                        w = min(P, I2 - k * P)
                        ins = pe.transpose(hq_ps[0:w, k * P:(k + 1) * P], f2_hq[:, j, k * P:k * P + w], ident_b)
                    ins.then_inc(s_htT, 1)
                    pe.wait_ge(s_ht, i * TB + (NT + j + 1))
                    pe.wait_ge(s_res, i * TB + (5 * NT + j))
                    for k in range(K2):
                        w = min(P, I2 - k * P)
                        ins = pe.matmul(y_ps, f2_hqT[0:w, k, :], f2_down_q[0:w, k, :], start=(k == 0), stop=(k == K2 - 1))
                    ins.then_inc(s_fy, 1)
            turns.end_loop(B)

        def l2_ffn_scalar(act, turns):
            act.wait_ge(s_f2_load, 64)
            act.wait_ge(s_res, 5 * NT)
            act.activation(f2_gate_q.rearrange("p c n -> p (c n)"), f2_gate, ACT.Abs, accum_out=w_sum[:, 0:1])
            act.activation(f2_down_q.rearrange("p c n -> p (c n)"), f2_down, ACT.Abs, accum_out=w_sum[:, 1:2]).then_inc(s_wsum, 1)
            act.activation(ident_b, ident[:, :], ACT.Copy).then_inc(s_wsum, 1)
            with act.Fori(0, B) as i:
                turns.loop(i, 1)
                act.wait_ge(s_ln_norm, i + 5 * B + 1)
                act.wait_ge(s_xq, i + 1)
                for j in range(TB):
                    ins = act.activation(f2_junk[:, j, 0:D], xn[:, j, :], ACT.Square, accum_out=row_ss[:, j:j + 1])
                ins.then_inc(s_row_ss, 1)
                act.wait_ge(s_turned, turns.now() + 1)
                act.activation(f2_xqT.rearrange("p c s -> p (c s)"), turn_b[:, 0:C * S], ACT.Copy).then_inc(s_turn_out, 1)
                turns.k += 1
                for j in range(TB):
                    act.wait_ge(s_gate, i * TB + (NT + j + 1))
                    act.activation(f2_act[:, j, :], gate_ps[:, 0:I2], ACT.Tanh, scale=row_half[:, j:j + 1]).then_inc(s_act, 1)
                    act.wait_ge(s_h2, i * TB + j + 1)
                    act.activation(f2_junk[:, j, :], f2_act[:, j, :], ACT.Square, accum_out=hrow_ss[:, j:j + 1]).then_inc(s_row_ss, 1)
                for j in range(TB):
                    act.wait_ge(s_htT, i * TB + (NT + j + 1))
                    act.wait_ge(s_fy, i * TB + (NT + j))
                    act.activation(f2_hqT[:, 0:K2 - 1, :].rearrange("p k q -> p (k q)"), hq_ps[:, 0:(K2 - 1) * P], ACT.Copy)
                    act.activation(f2_hqT[0:I2 % P, K2 - 1, :], hq_ps[0:I2 % P, (K2 - 1) * P:K2 * P], ACT.Copy).then_inc(s_ht, 1)
            turns.end_loop(B)

        def quantise(dve, st, v, whole, scales, low, high):
            for j, scale in enumerate(scales):
                st.mark(dve.tensor_scalar(v[j], v[j], scale, ROUND, ALU.mult, ALU.add))
            st.wait()
            for j in range(len(scales)):
                st.mark(dve.tensor_scalar(v[j], v[j], ROUND, high, ALU.subtract, ALU.min))
            st.wait()
            return [dve.tensor_scalar(whole[j], v[j], low, None, ALU.max) for j in range(len(scales))][-1]

        def l2_ffn_vector(dve, st):
            dve.wait_ge(s_wmean, 1)
            sizes = (2 * I2 * D, I2 * D)
            for k in range(2):
                st.mark(dve.tensor_scalar(w_mean[:, k:k + 1], bank(6)[:, k:k + 1], 1.0 / sizes[k], 1e-5, ALU.mult, ALU.max))
            st.wait()
            st.done(dve.reciprocal(w_scale, w_mean))
            quantise(dve, st, [f2_gate, f2_down], [f2_gate_q.rearrange("p c n -> p (c n)"), f2_down_q.rearrange("p c n -> p (c n)")],
                     [w_scale[:, 0:1], w_scale[:, 1:2]], -1.0, 1.0).then_inc(s_xq, 1)
            with dve.Fori(0, B) as i:
                st.loop(i, 4 + 9 + 4 + TB * 10)
                ln_vector(dve, st, i, i + 5 * B)
                ln_apply(dve, i, i + 33)
                dve.wait_ge(s_row_ss, i * 3 + 1)
                dve.tensor_scalar(row_rms, row_ss, 1.0 / D, 1e-5, ALU.mult, ALU.add).then_inc(s_row_ms, 1)
                dve.wait_ge(s_row_rms, i * 3 + 1)
                for j in range(TB):
                    st.mark(dve.scalar_tensor_tensor(out=xn[:, j, :], in0=xn[:, j, :], scalar=row_rms[:, j:j + 1],
                                                     in1=f2_norm, op0=ALU.mult, op1=ALU.mult))
                st.wait()
                st.done(dve.tensor_reduce(row_max, xn[:, :, :], AX, ALU.max, apply_absolute_value=True))
                st.done(dve.tensor_scalar(row_max, row_max, 1e-5, None, ALU.max))
                st.mark(dve.reciprocal(row_q, row_max))
                st.done(dve.tensor_scalar(row_y, row_max, 1.0 / 127.0, w_mean[:, 0:1], ALU.mult, ALU.mult))
                st.mark(dve.tensor_scalar(row_q, row_q, 127.0, None, ALU.mult))
                st.mark(dve.tensor_scalar(row_half, row_y, 0.5, None, ALU.mult))
                st.done(dve.scalar_tensor_tensor(out=row_sq, in0=row_y, scalar=0.5, in1=row_y, op0=ALU.mult, op1=ALU.mult))
                quantise(dve, st, [xn[:, j, :] for j in range(TB)], [f2_xq[:, j, :] for j in range(TB)],
                         [row_q[:, j:j + 1] for j in range(TB)], -128.0, 127.0).then_inc(s_xq, 1)
                for j in range(TB):
                    h = f2_act[:, j, :]
                    dve.wait_ge(s_act, i * TB + (NT + j + 1))
                    st.done(dve.scalar_tensor_tensor(out=h, in0=h, scalar=1.0, in1=gate_ps[:, 0:I2], op0=ALU.add, op1=ALU.mult))
                    dve.wait_ge(s_up, i * TB + (NT + j + 1))
                    dve.scalar_tensor_tensor(out=h, in0=h, scalar=row_sq[:, j:j + 1], in1=up_ps[:, 0:I2],
                                             op0=ALU.mult, op1=ALU.mult).then_inc(s_h2, 1)
                    dve.wait_ge(s_row_ss, i * 3 + j + 2)
                    dve.tensor_scalar(hrow_rms[:, j:j + 1], hrow_ss[:, j:j + 1], 1.0 / I2, 1e-5, ALU.mult, ALU.add).then_inc(s_row_ms, 1)
                    dve.wait_ge(s_row_rms, i * 3 + j + 2)
                    st.done(dve.scalar_tensor_tensor(out=h, in0=h, scalar=hrow_rms[:, j:j + 1], in1=f2_dnorm,
                                                     op0=ALU.mult, op1=ALU.mult))
                    top1, q1, y1 = hrow_max[:, j:j + 1], hrow_q[:, j:j + 1], hrow_y[:, j:j + 1]
                    st.done(dve.tensor_reduce(top1, h, AX, ALU.max, apply_absolute_value=True))
                    st.done(dve.tensor_scalar(top1, top1, 1e-5, None, ALU.max))
                    st.mark(dve.reciprocal(q1, top1))
                    st.done(dve.tensor_scalar(y1, top1, 1.0 / 127.0, w_mean[:, 1:2], ALU.mult, ALU.mult))
                    st.mark(dve.tensor_scalar(y1, y1, gates[:, 5:6], None, ALU.mult))
                    st.done(dve.tensor_scalar(q1, q1, 127.0, None, ALU.mult))
                    quantise(dve, st, [h], [f2_hq[:, j, :]], [q1], -128.0, 127.0).then_inc(s_hq, 1)
                for j in range(TB):
                    dve.wait_ge(s_fy, i * TB + (NT + j + 1))
                    dve.scalar_tensor_tensor(out=tile_of(x, i * TB + j), in0=y_ps, scalar=hrow_y[:, j:j + 1],
                                             in1=tile_of(x, i * TB + j), op0=ALU.mult, op1=ALU.add).then_inc(s_res, 1)
            st.end_loop(B)

        scratch.restart()
        attn_region.restart()
        l3_w = attn_region.take([P, 2, C, D])
        l3_in_bias = attn_region.take([P, C])
        l3_out_bias = attn_region.take([1, D])
        l3_affine = attn_region.take([P, 2, D])
        l3_decay = attn_region.take([P, 1])
        l3_decays = attn_region.take([P, SK])
        l3_in = attn_region.take([P, C, CT])
        l3_state = attn_region.take([P, C, CT])
        l3_mean = attn_region.take([P, C, B])
        l3_mean_wide = attn_region.take([P, C, B, P])
        l3_summary = attn_region.take([P, B, D])
        l3_y = attn_region.take([P, TB, D])

        s_l3_load = sem("l3_load")
        s_l3_in = sem("l3_context_projected")
        s_l3_in_out = sem("l3_context_out")
        s_l3_mean = sem("l3_means_ready")
        s_l3_sum = sem("l3_summary_ready")
        s_l3_sum_out = sem("l3_summary_out")

        def l3_attn_sync(sp):
            sp.wait_ge(s_res, 5 * NT)
            for dst, name in ((l3_w, "l3_w"), (l3_in_bias, "l3_in_bias"), (l3_out_bias, "l3_out_bias"),
                              (l3_affine, "l3_affine"), (l3_decay, "l3_decay")):
                sp.dma_start(dst, A[name]).then_inc(s_l3_load, 16)

        def l3_attn_gpsimd(pool):
            with pool.Fori(0, B) as i:
                ln_gpsimd(pool, i * 2 + 6 * B)
                ln_gpsimd(pool, i * 2 + (6 * B + 1))

        def l3_attn_tensor(pe, turns):
            pe.wait_ge(s_l3_load, 16 * 5)
            for m in range(C):
                for c in range(C):
                    ins = pe.matmul(bank(1)[:, m * CT:(m + 1) * CT], l3_w[:, 0, c, m * P:(m + 1) * P], ctxT[:, c, :],
                                    start=(c == 0), stop=(c == C - 1))
            ins.then_inc(s_l3_in, 1)
            pe.wait_ge(s_l3_mean, 1)
            for b in range(B):
                ps = bank(2, 2)[:, b * D:(b + 1) * D]
                pe.matmul(ps, ones[:, :], l3_out_bias, start=True, stop=False)
                for c in range(C):
                    ins = pe.matmul(ps, l3_mean_wide[:, c, b, :], l3_w[:, 1, c, :], start=False, stop=(c == C - 1))
            ins.then_inc(s_l3_sum, 1)

        def l3_attn_scalar(act, turns):
            act.wait_ge(s_l3_load, 16 * 5)
            act.activation(l3_decay, l3_decay, ACT.Tanh, scale=0.5).then_inc(s_l3_in_out, 1)
            act.wait_ge(s_l3_in, 1)
            for c in range(C):
                ins = act.activation(l3_in[:, c, :], bank(1)[:, c * CT:(c + 1) * CT], ACT.Identity, bias=l3_in_bias[:, c:c + 1])
            ins.then_inc(s_l3_in_out, 1)
            act.wait_ge(s_l3_sum, 1)
            act.activation(flat(l3_summary), bank(2, 2), ACT.Copy).then_inc(s_l3_sum_out, 1)

        def l3_attn_vector(dve, st):
            dve.wait_ge(s_l3_in_out, 2)
            st.done(dve.tensor_scalar(l3_decay, l3_decay, 1.0, 0.5, ALU.add, ALU.mult))
            st.done(dve.tensor_copy(l3_decays, l3_decay.to_broadcast([P, SK])))
            for c in range(C):
                for b in range(B):
                    at = slice(b * SK, (b + 1) * SK)
                    st.mark(dve.tensor_tensor_scan(l3_state[:, c, at], l3_decays, l3_in[:, c, at], 0.0, ALU.mult, ALU.add))
            st.wait()
            st.done(dve.tensor_reduce(l3_mean, l3_state.rearrange("p c (b k) -> p c b k", b=B), AX, ALU.add))
            st.done(dve.tensor_scalar(l3_mean, l3_mean, 1.0 / SK, None, ALU.mult))
            dve.tensor_copy(l3_mean_wide, l3_mean.unsqueeze(3).to_broadcast([P, C, B, P])).then_inc(s_l3_mean, 1)
            dve.wait_ge(s_l3_sum_out, 1)
            with dve.Fori(0, B) as i:
                st.loop(i, 4 + 2 + 1 + 4 + 2 + 2)
                ln_vector(dve, st, i, i * 2 + 6 * B)
                for j in range(TB):
                    st.mark(dve.tensor_scalar(l3_y[:, j, :], tile_of(x, i * TB + j), ln_mv[:, j, 0:1], ln_rstd[:, j, :],
                                              ALU.subtract, ALU.mult))
                st.wait()
                st.done(dve.tensor_tensor(l3_y, l3_y, l3_summary[:, bass.ds(i, 1), :].to_broadcast([P, TB, D]), ALU.add))
                for j in range(TB):
                    st.mark(dve.bn_stats(ln_stats[:, j, :], l3_y[:, j, :]))
                st.wait()
                settle(dve)
                for j in range(TB):
                    st.mark(dve.bn_aggr(ln_mv[:, j, :], ln_stats[:, j, :]))
                st.wait()
                dve.tensor_scalar(ln_mv[:, :, 1:2], ln_mv[:, :, 1:2], 1e-5, None, ALU.add).then_inc(s_ln_var, 1)
                dve.wait_ge(s_ln_rstd, i * 2 + (6 * B + 2))
                for j in range(TB):
                    st.mark(dve.tensor_scalar(l3_y[:, j, :], l3_y[:, j, :], ln_mv[:, j, 0:1], ln_rstd[:, j, :],
                                              ALU.subtract, ALU.mult))
                st.wait()
                for k, op in enumerate((ALU.mult, ALU.add)):
                    st.done(dve.tensor_tensor(l3_y, l3_y, l3_affine[:, k:k + 1, :].to_broadcast([P, TB, D]), op))
                for j in range(TB):
                    dve.scalar_tensor_tensor(out=tile_of(x, i * TB + j), in0=l3_y[:, j, :], scalar=gates[:, 6:7],
                                             in1=tile_of(x, i * TB + j), op0=ALU.mult, op1=ALU.add).then_inc(s_res, 1)
                dve.wait_ge(s_res, i * TB + (6 * NT + TB))
            st.end_loop(B)

        scratch.restart()
        scratch.at = moe_mark
        ffn_region.restart()
        f3_expert_w = ffn_region.take([P, SLOTS, 3 * D])
        EZ = E3 + Z3
        f3_router = scratch.take([P, C, EZ])
        f3_bias = scratch.take([P, EZ])
        earlier = scratch.take([P, P])
        all_ones = scratch.take([P, P])
        c_prob = scratch.take([P, TB, EZ])
        c_biased = scratch.take([P, TB, EZ])
        c_rest = scratch.take([P, TB, EZ])
        c_eight = scratch.take([P, TB, 8])
        c_sum = scratch.take([P, TB, 1])
        c_idle = scratch.take([P, TB, 1])
        taken = scratch.take([P, TB, E3])
        taken_before = scratch.take([P, E3])
        c_keep = scratch.take([P, TB, E3])

        s_f3_load = sem("f3_load")
        s_taken = sem("experts_taken")
        s_place = sem("places_counted")
        place_ps = bank(7)[:, 0:TB * E3].rearrange("p (j e) -> p j e", j=TB)

        def l3_ffn_sync(sp):
            sp.wait_ge(s_res, 7 * NT)
            for dst, name in ((f3_router, "f3_router"), (f3_bias, "f3_bias"), (earlier, "earlier")):
                sp.dma_start(dst, A[name]).then_inc(s_f3_load, 16)
            experts_sync(sp, "f3_experts", E3, 0, 2 * (E1 + 1))

        def l3_ffn_gpsimd(pool):
            pool.wait_ge(s_res, 7 * NT)
            pool.memset(all_ones, 1.0).then_inc(s_const, 1)
            router_gpsimd(pool, 8 * B, 37, B)

        def l3_ffn_scalar(act, turns):
            router_scalar(act, turns, B, c_prob)
            experts_scalar(act, E3, 2 * (E1 + 1))

        def l3_ffn_tensor(pe, turns):
            pe.wait_ge(s_f3_load, 48)
            pe.wait_ge(s_const, 4)
            with pe.Fori(0, B) as i:
                turns.loop(i, 1)
                pe.wait_ge(s_ln_norm, i + 6 * B + 1)
                turn_batch(pe, turns, xn)
                pe.wait_ge(s_turn_out, turns.now())
                pe.wait_ge(s_rshift, i + B)
                for j in range(TB):
                    for c in range(C):
                        ins = pe.matmul(logit_ps[:, j * EZ:(j + 1) * EZ], xT[:, c, j * P:(j + 1) * P], f3_router[:, c, :],
                                        start=(c == 0), stop=(c == C - 1))
                ins.then_inc(s_logit, 1)
                for j in range(TB):
                    pe.wait_ge(s_taken, i * TB + j + 1)
                    pe.matmul(place_ps[:, j, :], all_ones, taken_before, start=True, stop=False)
                    pe.matmul(place_ps[:, j, :], earlier, taken[:, j, :], start=False, stop=True).then_inc(s_place, 1)
            turns.end_loop(B)
            pe.wait_ge(s_xall, 2 * B)
            pe.wait_ge(s_rshift, 2 * B)
            experts_tensor(pe, E3, [5, 4, 4, 4], 2 * (E1 + 1))

        def l3_ffn_vector(dve, st):
            dve.wait_ge(s_f3_load, 48)
            st.done(dve.memset(taken_before, 0.0))
            with dve.Fori(0, B) as i:
                st.loop(i, 4 + 4 + 5 + 8 + 2 * TB + 1)
                ln_vector(dve, st, i, i + 8 * B)
                ln_apply(dve, i, i + 37)
                spread = lambda v, n: v.to_broadcast([P, TB, n])
                router_softmax(dve, st, i, B, c_prob, EZ)
                st.mark(dve.tensor_tensor(c_biased, c_prob, f3_bias.unsqueeze(1).to_broadcast([P, TB, EZ]), ALU.add))
                st.wait()
                settle(dve)
                for j in range(TB):
                    st.mark(dve.max(c_eight[:, j, :], c_biased[:, j, :]))
                st.wait()
                settle(dve)
                for j in range(TB):
                    st.mark(dve.match_replace(out=c_rest[:, j, :], in_to_replace=c_eight[:, j, :],
                                              in_values=c_biased[:, j, :], imm_value=-3e38))
                st.wait()
                st.done(dve.tensor_tensor(c_rest, c_rest, c_biased, ALU.not_equal))
                st.done(dve.tensor_copy(taken, c_rest[:, :, 0:E3]))
                st.done(dve.tensor_tensor(c_rest, c_rest, c_prob, ALU.mult))
                st.done(dve.tensor_reduce(c_sum[:, :, 0], c_rest, AX, ALU.add))
                st.done(dve.tensor_scalar(c_sum, c_sum, 1e-20, None, ALU.add))
                st.done(dve.reciprocal(c_sum, c_sum))
                st.done(dve.scalar_tensor_tensor(out=c_rest, in0=c_rest, scalar=1.5, in1=spread(c_sum, EZ),
                                                 op0=ALU.mult, op1=ALU.mult))
                st.mark(dve.tensor_reduce(c_idle[:, :, 0], c_rest[:, :, E3:EZ], AX, ALU.add))
                for j in range(TB):
                    st.wait()
                    settle(dve)
                    dve.engine_nop().then_inc(s_taken, 1)
                    dve.wait_ge(s_place, i * TB + j + 1)
                    st.mark(dve.tensor_tensor(taken_before, taken_before, taken[:, j, :], ALU.add))
                    st.done(dve.tensor_scalar(c_keep[:, j, :], place_ps[:, j, :], float(CAP3), None, ALU.is_lt))
                st.done(dve.tensor_tensor(c_keep, c_keep, c_rest[:, :, 0:E3], ALU.mult))
                dve.scalar_tensor_tensor(out=weight_of[:, bass.ds(i * TB, TB), 0:E3], in0=spread(c_idle, E3), scalar=1.0,
                                         in1=c_keep, op0=ALU.add, op1=ALU.mult).then_inc(s_weighed, 1)
            st.end_loop(B)
            dve.wait_ge(s_weighed, B)
            st.done(dve.tensor_scalar(weight_of[:, :, 0:E3], weight_of[:, :, 0:E3], gates[:, 7:8], None, ALU.mult))
            experts_vector(dve, st, E3, 2 * (E1 + 1))

        s_weighed = sem("tokens_weighed")

        stage_list = [
            dict(sync=l0_attn_sync, gpsimd=l0_attn_gpsimd, scalar=l0_attn_scalar, vector=l0_attn_vector, tensor=l0_attn_tensor),
            dict(sync=l0_ffn_sync, gpsimd=l0_ffn_gpsimd, scalar=l0_ffn_scalar, vector=l0_ffn_vector, tensor=l0_ffn_tensor),
            dict(sync=l1_attn_sync, gpsimd=l1_attn_gpsimd, scalar=l1_attn_scalar, vector=l1_attn_vector, tensor=l1_attn_tensor),
            dict(sync=l1_ffn_sync, gpsimd=l1_ffn_gpsimd, scalar=l1_ffn_scalar, vector=l1_ffn_vector, tensor=l1_ffn_tensor),
            dict(sync=l2_attn_sync, gpsimd=l2_attn_gpsimd, scalar=l2_attn_scalar, vector=l2_attn_vector, tensor=l2_attn_tensor),
            dict(sync=l2_ffn_sync, gpsimd=l2_ffn_gpsimd, scalar=l2_ffn_scalar, vector=l2_ffn_vector, tensor=l2_ffn_tensor),
            dict(sync=l3_attn_sync, gpsimd=l3_attn_gpsimd, scalar=l3_attn_scalar, vector=l3_attn_vector, tensor=l3_attn_tensor),
            dict(sync=l3_ffn_sync, gpsimd=l3_ffn_gpsimd, scalar=l3_ffn_scalar, vector=l3_ffn_vector, tensor=l3_ffn_tensor),
        ]

        block = ctx.enter_context(nc.Block())

        @block.sync
        def _(sp):
            sp.dma_start(gates[:, :], A["gates"]).then_inc(s_load, 16)
            sp.dma_start(ident[:, :], A["ident"]).then_inc(s_load, 16)
            sp.dma_start(x[:, :, :], A["x"]).then_inc(s_load, 16)
            for n, stage in enumerate(stage_list[:stages]):
                stage["sync"](sp)
            sp.wait_ge(s_res, stages * NT)
            sp.dma_start(out, x[:, :, :]).then_inc(s_store, 16)
            sp.wait_ge(s_store, 16)

        @block.gpsimd
        def _(pool):
            pool.memset(ones[:, :], 1.0).then_inc(s_const, 1)
            pool.memset(minus_half[:, :], -0.5).then_inc(s_const, 1)
            pool.wait_ge(s_const, 2)
            for stage in stage_list[:stages]:
                stage["gpsimd"](pool)

        @block.scalar
        def _(act):
            turns = Tally(s_turned)
            act.wait_ge(s_load, 48)
            act.activation(gates[:, :], gates[:, :], ACT.Tanh).then_inc(s_const, 1)
            for stage in stage_list[:stages]:
                stage["scalar"](act, turns)

        @block.vector
        def _(dve):
            st = Steps(dve, s_dve)
            dve.wait_ge(s_load, 48)
            dve.wait_ge(s_const, 3)
            for n, stage in enumerate(stage_list[:stages]):
                stage["vector"](dve, st)
                dve.wait_ge(s_res, (n + 1) * NT)

        @block.tensor
        def _(pe):
            turns = Tally(s_turned)
            pe.wait_ge(s_load, 48)
            for stage in stage_list[:stages]:
                stage["tensor"](pe, turns)


def laid_out(inp):
    f = np.float32

    def chunks(w):
        return w.reshape(-1, P, w.shape[-1]).transpose(1, 0, 2)

    def rows(v):
        return np.broadcast_to(v.reshape(1, -1), (P, v.size))

    a = {}
    a["x"] = inp["x"].reshape(NT, P, D).transpose(1, 0, 2)
    a["gates"] = rows(np.stack([inp["g_xattn"], inp["g_ffn"]], axis=1).reshape(-1))
    a["ident"] = np.eye(P, dtype=f)
    context = inp["ctx_2048"].reshape(CT, D).T
    a["ctxT"] = chunks(context)
    a["ctxT2"] = np.repeat(chunks(context).reshape(P, C, B, 1, SK), 2, axis=3).reshape(P, C, B, P)
    a["l0_w"] = np.stack([chunks(inp["L0_xattn_" + k]) for k in ("Wq", "Wk_img", "Wv_img", "Wo")], axis=1)
    a["l0_rows"] = np.stack([inp["L0_xattn_" + k] for k in ("bq", "bk_img", "bv_img", "bo")])[None]
    a["l0_gain"] = np.stack([rows(inp["L0_xattn_" + k]) for k in ("gq", "gk_img")], axis=1)
    a["head_of"] = np.repeat(np.eye(HB0, dtype=f), HD0, axis=0)
    a["half_of"] = np.repeat(np.eye(2, dtype=f), SK, axis=0)
    a["f0_w"] = np.stack([chunks(inp["L0_ffn_w_gate"]), chunks(inp["L0_ffn_w_up"])], axis=1)
    a["f0_down"] = chunks(inp["L0_ffn_w_down"])
    a["l1_kvc"] = chunks(inp["L1_xattn_W_kvc"])
    a["l1_dq"] = chunks(inp["L1_xattn_W_dq"])
    a["l1_uqT"] = inp["L1_xattn_W_uq"].reshape(QC1, H1, HD1).transpose(2, 1, 0)
    swap = (np.arange(R1) + R1 // 2) % R1
    qr = inp["L1_xattn_W_qr"].reshape(QC1, H1, R1)
    a["l1_qr"] = np.stack([qr, qr[:, :, swap]], axis=1).reshape(QC1, 2, H1 * R1)
    a["l1_uk"] = inp["L1_xattn_W_uk"]
    kr = inp["L1_xattn_W_kr"]
    a["l1_kr"] = np.stack([np.concatenate([w, w], axis=1) for w in (kr, kr[:, swap])], axis=1)
    a["l1_uv"] = inp["L1_xattn_W_uv"]
    a["l1_wo"] = inp["L1_xattn_W_o"].reshape(H1, HD1, D).transpose(1, 0, 2)
    a["seg"] = inp["itok_BxS_0_1023"].reshape(NT, P).T
    half = R1 // 2
    angle = np.arange(S, dtype=f)[:, None] * (f(1.0) / f(10000.0) ** (np.arange(half, dtype=f) / f(half)))
    a["l1_cos"] = np.tile(np.cos(angle).T, (4, 1)).astype(f)
    a["l1_sin"] = np.tile(np.concatenate([-np.sin(angle).T, np.sin(angle).T]), (2, 1)).astype(f)
    a["key_at"] = rows(np.arange(SK, dtype=f))
    a["key_last"] = rows(np.arange(SK, dtype=f) + f(LOOKBACK))

    def experts(gate, up, down):
        n = gate.shape[0]
        gu = np.stack([gate.reshape(n, C, P, I1), up.reshape(n, C, P, I1)], axis=3)
        return np.concatenate([gu.transpose(0, 2, 1, 3, 4).reshape(n, P, 2 * D), down], axis=2)

    a["f1_experts"] = experts(*(np.concatenate([inp["L1_ffn_" + k], inp["L1_ffn_s" + k][None]]) for k in ("Wg", "Wu", "Wd")))
    a["f1_router"] = chunks(inp["L1_ffn_Wr"].T)
    a["f1_bias"] = inp["L1_ffn_bias"].reshape(1, E1)
    a["below"] = rows(-np.arange(1, 9, dtype=f))
    swap = (np.arange(HD2) + HD2 // 2) % HD2
    swapped = lambda w: w.reshape(D, H2, HD2)[:, :, swap].reshape(D, D)
    wq, wk, wv, wo = (inp["L2_xattn_" + k] for k in ("Wq", "Wk", "Wv", "Wo"))
    a["l2_w"] = np.stack([chunks(w) for w in (wq, swapped(wq), wk, swapped(wk), wv, wo)], axis=1)
    freqs = np.outer(np.arange(S, dtype=f), f(1.0) / f(10000.0) ** (np.arange(0, HD2, 2, dtype=f) / f(HD2)))
    a["l2_cos"] = np.tile(np.cos(freqs).T, (P // HD2 * 2, 1)).astype(f)
    a["l2_sin"] = np.tile(np.concatenate([-np.sin(freqs).T, np.sin(freqs).T]), (P // HD2, 1)).astype(f)
    a["quad_of"] = np.tile(np.repeat(np.eye(4, dtype=f), HD2, axis=0), (4, 1))
    a["l2_gate"] = rows(inp["L2_xattn_gate"].reshape(-1))
    a["mask"] = inp["mask_Bx1xSxS_fk0"].reshape(NT, P, S).transpose(1, 0, 2)
    a["l2_head_of"] = np.repeat(np.eye(P // HD2, dtype=f), HD2, axis=0)
    a["f2_gate"] = chunks(inp["L2_ffn_gate_w"].T).reshape(P, -1)
    down = np.zeros((-(-I2 // P) * P, D), f)
    down[:I2] = inp["L2_ffn_down_w"].T
    a["f2_down"] = chunks(down).reshape(P, -1)
    a["f2_norm"] = rows(inp["L2_ffn_gate_norm_w"])
    a["f2_dnorm"] = rows(inp["L2_ffn_down_norm_w"])
    a["l3_w"] = np.stack([chunks(inp["L3_xattn_" + k].T) for k in ("W_in", "W_out")], axis=1)
    a["l3_in_bias"] = inp["L3_xattn_b_in"].reshape(C, P).T
    a["l3_out_bias"] = inp["L3_xattn_b_out"].reshape(1, D)
    a["l3_affine"] = np.stack([rows(inp["L3_xattn_" + k]) for k in ("gamma", "beta")], axis=1)
    a["l3_decay"] = rows(inp["L3_xattn_decay"].reshape(1))
    gu = inp["L3_ffn_w_gate_up"]
    a["f3_experts"] = experts(gu[:, :, :I3], gu[:, :, I3:], inp["L3_ffn_w_down"])
    a["f3_router"] = chunks(inp["L3_ffn_w_cls"].T)
    a["f3_bias"] = rows(inp["L3_ffn_bias"])
    a["earlier"] = np.triu(np.ones((P, P), f), 1)
    return {k: np.ascontiguousarray(v) for k, v in a.items()}


def kernel(**inputs):
    from concourse import bacc
    from concourse.bass_utils import run_bass_kernel_spmd

    nc = bacc.Bacc("TRN2", target_bir_lowering=False, num_devices=1)
    arrays = laid_out({k: np.asarray(v) for k, v in inputs.items()})
    A = {k: nc.dram_tensor(f"in_{k}_dram", v.shape, mybir.dt.from_np(v.dtype), kind="ExternalInput").ap()
         for k, v in arrays.items()}
    out = nc.dram_tensor("out_0_dram", (P, NT, D), F32, kind="ExternalOutput").ap()
    flamingo(nc, A, out)
    r = run_bass_kernel_spmd(nc, [{f"in_{k}_dram": v for k, v in arrays.items()}], core_ids=[0])
    return r.results[0]["out_0_dram"].transpose(1, 0, 2).reshape(B, S, D)
```

```python
from contextlib import ExitStack

import numpy as np

import concourse.bass as bass
from concourse import mybir

F32 = mybir.dt.float32
BF16 = mybir.dt.bfloat16
I32 = mybir.dt.int32
ALU = mybir.AluOpType
ACT = mybir.ActivationFunctionType
AX = mybir.AxisListType.X

P = 128
D = 256
C = D // P
B = 4
S = 256
TB = S // P
NT = B * TB
T = B * S
SK = 64
CT = B * SK
BANK = 512

H0, HD0 = 16, 16
HB0 = P // HD0
I0 = 1024
H1, HD1, R1, QC1, KC1 = 16, 128, 64, 96, 64
LOOKBACK = 8
I1, E1 = 128, 16
H2, HD2 = 32, 8
I2 = 704
I3, E3, Z3, TOP3, CAP3 = 128, 32, 32, 8, 128


class Tally:

    def __init__(self, sem):
        self.sem, self.base, self.k, self.i, self.per = sem, 0, 0, 0, 0

    def loop(self, i, per):
        self.base += self.k
        self.k, self.i, self.per = 0, i, per

    def end_loop(self, trips):
        assert self.k == self.per, (self.sem, self.k, self.per)
        self.base += trips * self.per
        self.k, self.i, self.per = 0, 0, 0

    def now(self):
        return self.i * self.per + (self.base + self.k)


class Steps(Tally):

    def __init__(self, eng, sem):
        super().__init__(sem)
        self.eng = eng

    def mark(self, ins):
        self.k += 1
        return ins.then_inc(self.sem, 1)

    def wait(self):
        self.eng.wait_ge(self.sem, self.now())

    def done(self, ins):
        self.mark(ins)
        self.wait()


def tile_of(x, t):
    return x[:, bass.ds(t, 1), :].rearrange("p a n -> p (a n)")


def flat(x):
    return x.rearrange("p a n -> p (a n)")


class Region:

    def __init__(self, tensor):
        self.tensor, self.at = tensor, 0

    def restart(self):
        self.at = 0

    def take(self, shape, dt=F32):
        n = int(np.prod(shape[1:]))
        words = n if dt != BF16 else (n + 1) // 2
        v = self.tensor[0:shape[0], self.at:self.at + words]
        self.at += words
        assert self.at <= self.tensor.shape[1], (self.at, self.tensor.shape)
        if dt != F32:
            v = v.bitcast(dt)
        if len(shape) == 2:
            return v
        axes = [f"d{k}" for k in range(len(shape) - 1)]
        return v.rearrange(f"p ({' '.join(axes)}) -> p {' '.join(axes)}", **dict(zip(axes[1:], shape[2:])))


def flamingo(nc, A, out, stages=8):
    ctx = ExitStack()
    with ctx:
        def sb(name, shape, dt=F32):
            return ctx.enter_context(nc.sbuf_tensor(name, shape, dt))

        def sem(name):
            return ctx.enter_context(nc.semaphore(name))

        psum = ctx.enter_context(nc.psum_tensor("psum", [P, 8, BANK], F32))

        def bank(i, n=1):
            return psum[:, i:i + n, :].rearrange("p a n -> p (a n)")

        x = sb("x", [P, NT, D])
        xn = sb("xn", [P, TB, D])
        xT = sb("xT", [P, C, S])
        ident = sb("ident", [P, P])
        ones = sb("ones", [1, P])
        gates = sb("gates", [P, 8])
        minus_half = sb("minus_half", [P, 8])
        ln_stats = sb("ln_stats", [P, TB, 6])
        ln_mv = sb("ln_mv", [P, TB, 2])
        ln_rstd = sb("ln_rstd", [P, TB, 1])
        ctxT = sb("ctxT", [P, C, CT])

        prob = sb("prob", [P, 1024])
        probT = sb("probT", [P, 8, P])
        scratch = Region(sb("scratch", [P, 11264]))
        attn_region = Region(sb("attn_region", [P, 24704]))
        ffn_region = Region(sb("ffn_region", [P, 6912]))

        turn = bank(0).rearrange("p (c s) -> p c s", c=C)

        s_load = sem("load_x")
        s_const = sem("const_set")
        s_gates = sem("gates_set")
        s_dve = sem("vector_step")
        s_pool = sem("gpsimd_step")
        s_act = sem("scalar_step")
        s_ln_var = sem("ln_var_ready")
        s_ln_rstd = sem("ln_rstd_ready")
        s_ln_norm = sem("ln_norm_ready")
        s_turned = sem("turned")
        s_turn_out = sem("turn_out")
        s_store = sem("store_out")

        def settle(eng):
            eng.sem_inc(s_settled, 1)

        s_settled = sem("settled")

        def ln_vector(dve, st, i, n):
            for j in range(TB):
                st.mark(dve.bn_stats(ln_stats[:, j, :], tile_of(x, i * TB + j)))
            st.wait()
            settle(dve)
            for j in range(TB):
                st.mark(dve.bn_aggr(ln_mv[:, j, :], ln_stats[:, j, :]))
            st.wait()
            dve.tensor_scalar(ln_mv[:, :, 1:2], ln_mv[:, :, 1:2], 1e-5, None, ALU.add).then_inc(s_ln_var, 1)
            dve.wait_ge(s_ln_rstd, n + 1)
            return n

        def ln_apply(dve, i, turned_before):
            dve.wait_ge(s_turned, turned_before)
            for j in range(TB):
                ins = dve.tensor_scalar(xn[:, j, :], tile_of(x, i * TB + j), ln_mv[:, j, 0:1],
                                        ln_rstd[:, j, :], ALU.subtract, ALU.mult)
            ins.then_inc(s_ln_norm, 1)

        def ln_gpsimd(pool, n):
            pool.wait_ge(s_ln_var, n + 1)
            pool.tensor_tensor(ln_rstd[:, :, 0], ln_mv[:, :, 1], minus_half[:, 0:TB],
                               ALU.pow).then_inc(s_ln_rstd, 1)

        def turn_batch(pe, turns, src):
            pe.wait_ge(s_turn_out, turns.now())
            for c in range(C):
                for j in range(TB):
                    ins = pe.transpose(turn[:, c, j * P:(j + 1) * P], src[:, j, c * P:(c + 1) * P],
                                       ident[:, :])
            ins.then_inc(s_turned, 1)
            turns.k += 1

        def turn_evac(act, turns, dst):
            act.wait_ge(s_turned, turns.now() + 1)
            act.activation(flat(dst[:, :, :]), bank(0), ACT.Copy).then_inc(s_turn_out, 1)
            turns.k += 1

        l0_w = attn_region.take([P, 4, C, D])
        l0_rows = attn_region.take([1, 4, D])
        l0_gain = attn_region.take([P, 2, D])
        ctxT2 = attn_region.take([P, C, B, P])
        head_of = sb("head_of", [P, HB0])
        half_of = sb("half_of", [P, 2])
        l0_kT = attn_region.take([P, C, CT])
        l0_v = attn_region.take([P, B, D])
        l0_kdiag = scratch.take([P, C, HB0, SK])
        l0_vdiag = scratch.take([P, H0 // 2, 2, HD0])
        junk = scratch.take([P, TB, D])
        ssq = scratch.take([P, TB])
        rms = scratch.take([P, TB])
        qn = scratch.take([P, TB, D])
        qT = scratch.take([P, C, S])
        top = sb("top", [P, H2])
        total = sb("total", [P, H2])
        oT = scratch.take([P, C, S])

        s_l0_load = sem("l0_load")
        s_proj = sem("rows_projected")
        s_ssq = sem("squares_summed")
        s_ms = sem("mean_square_ready")
        s_rms = sem("rms_ready")
        s_scaled = sem("rows_scaled")
        s_v = sem("l0_v_projected")
        s_vout = sem("l0_v_ready")
        s_diag = sem("l0_diag_ready")
        s_score = sem("scores_ready")
        s_shift = sem("scores_shifted")
        s_exp = sem("exp_ready")
        s_ptT = sem("probs_turned")
        s_pt = sem("probs_turn_out")
        s_pv = sem("pv_ready")
        s_o = sem("heads_ready")
        s_y = sem("attn_out_ready")
        s_res = sem("residual_added")

        q_ps = bank(1).rearrange("p (j d) -> p j d", j=TB)
        sc_ps = bank(2, 2)
        pt_ps = bank(4, 2)
        pv_ps = bank(6)[:, 0:D]
        y_ps = bank(7)[:, 0:D]

        def l0_attn_sync(sp):
            for dst, name in ((ctxT[:, :, :], "ctxT"), (l0_w[:, :, :, :], "l0_w"), (l0_rows[:, :, :], "l0_rows"),
                              (l0_gain[:, :, :], "l0_gain"), (ctxT2[:, :, :, :], "ctxT2"),
                              (head_of[:, :], "head_of"), (half_of[:, :], "half_of")):
                sp.dma_start(dst, A[name]).then_inc(s_l0_load, 16)

        def rms_scalar(act, n):
            act.wait_ge(s_proj, n + 1)
            for j in range(TB):
                ins = act.activation(junk[:, j, :], q_ps[:, j, :], ACT.Square, accum_out=ssq[:, j:j + 1])
            ins.then_inc(s_ssq, 1)

        def rms_vector(dve, n, gain, turned_before):
            dve.wait_ge(s_ssq, n + 1)
            dve.tensor_scalar(rms[:, :], ssq[:, :], 1.0 / D, 1e-6, ALU.mult, ALU.add).then_inc(s_ms, 1)
            dve.wait_ge(s_rms, n + 1)
            dve.wait_ge(s_turned, turned_before)
            for j in range(TB):
                ins = dve.scalar_tensor_tensor(out=qn[:, j, :], in0=q_ps[:, j, :], scalar=rms[:, j:j + 1],
                                               in1=gain, op0=ALU.mult, op1=ALU.mult)
            ins.then_inc(s_scaled, 1)

        def rms_gpsimd(pool, n):
            pool.wait_ge(s_ms, n + 1)
            pool.tensor_tensor(rms[:, :], rms[:, :], minus_half[:, 0:TB], ALU.pow).then_inc(s_rms, 1)

        def l0_attn_tensor(pe, turns):
            pe.wait_ge(s_l0_load, 16 * 7)
            pe.wait_ge(s_const, 3)
            for m in range(TB):
                pe.matmul(q_ps[:, m, :], ones[:, :], l0_rows[:, 1, :], start=True, stop=False)
                for c in range(C):
                    ins = pe.matmul(q_ps[:, m, :], ctxT[:, c, m * P:(m + 1) * P], l0_w[:, 1, c, :],
                                    start=False, stop=(c == C - 1))
            ins.then_inc(s_proj, 1)
            for b in range(B):
                v_ps = sc_ps[:, b * D:(b + 1) * D]
                pe.matmul(v_ps, ones[:, :], l0_rows[:, 2, :], start=True, stop=False)
                for c in range(C):
                    ins = pe.matmul(v_ps, ctxT2[:, c, b, :], l0_w[:, 2, c, :], start=False, stop=(c == C - 1))
            ins.then_inc(s_v, 1)
            pe.wait_ge(s_scaled, 1)
            turn_batch(pe, turns, qn)
            pe.wait_ge(s_vout, 1)
            with pe.Fori(0, B) as i:
                turns.loop(i, 3)
                pe.wait_ge(s_ln_norm, i + 1)
                turn_batch(pe, turns, xn)
                pe.wait_ge(s_turn_out, turns.now())
                for j in range(TB):
                    pe.matmul(q_ps[:, j, :], ones[:, :], l0_rows[:, 0, :], start=True, stop=False)
                    for c in range(C):
                        ins = pe.matmul(q_ps[:, j, :], xT[:, c, j * P:(j + 1) * P], l0_w[:, 0, c, :],
                                        start=False, stop=(c == C - 1))
                ins.then_inc(s_proj, 1)
                pe.wait_ge(s_scaled, i + 2)
                turn_batch(pe, turns, qn)
                pe.wait_ge(s_turn_out, turns.now())
                pe.wait_ge(s_diag, i + 1)

                def scores(j):
                    pe.wait_ge(s_shift, i * TB + j + 1)
                    for c in range(C):
                        ins = pe.matmul(sc_ps[:, c * BANK:(c + 1) * BANK], qT[:, c, j * P:(j + 1) * P],
                                        l0_kdiag[:, c, :, :].rearrange("p h k -> p (h k)"),
                                        start=True, stop=True)
                    ins.then_inc(s_score, 1)

                def weigh(j):
                    pe.wait_ge(s_exp, i * TB + j + 1)
                    pe.wait_ge(s_pt, i * TB + j + 1)
                    for g in range(8):
                        ins = pe.transpose(pt_ps[:, g * P:(g + 1) * P], prob[:, g * P:(g + 1) * P], ident[:, :])
                    ins.then_inc(s_ptT, 1)
                    pe.wait_ge(s_pt, i * TB + j + 2)
                    pe.wait_ge(s_o, i * TB + j + 1)
                    for g in range(8):
                        ins = pe.matmul(pv_ps[:, g * 32:(g + 1) * 32], probT[:, g, :],
                                        l0_vdiag[:, g, :, :].rearrange("p a d -> p (a d)"), start=True, stop=True)
                    ins.then_inc(s_pv, 1)

                scores(0)
                scores(1)
                weigh(0)
                weigh(1)
                pe.wait_ge(s_o, i * TB + TB + 1)
                turn_batch(pe, turns, qn)
                pe.wait_ge(s_turn_out, turns.now())
                for j in range(TB):
                    pe.wait_ge(s_res, i * TB + j + 1)
                    pe.matmul(y_ps, ones[:, :], l0_rows[:, 3, :], start=True, stop=False)
                    for c in range(C):
                        ins = pe.matmul(y_ps, oT[:, c, j * P:(j + 1) * P], l0_w[:, 3, c, :],
                                        start=False, stop=(c == C - 1))
                    ins.then_inc(s_y, 1)
            turns.end_loop(B)

        def l0_attn_scalar(act, turns):
            rms_scalar(act, 0)
            act.wait_ge(s_v, 1)
            act.activation(l0_v[:, :, :].rearrange("p b d -> p (b d)"), sc_ps, ACT.Copy).then_inc(s_vout, 1)
            turn_evac(act, turns, l0_kT)
            with act.Fori(0, B) as i:
                turns.loop(i, 3)
                turn_evac(act, turns, xT)
                rms_scalar(act, i + 1)
                turn_evac(act, turns, qT)
                for j in range(TB):
                    act.wait_ge(s_shift, i * TB + j + 2)
                    act.activation(prob[:, :], prob[:, :], ACT.Exp, scale=HD0 ** -0.5).then_inc(s_exp, 1)
                    act.wait_ge(s_ptT, i * TB + j + 2)
                    act.wait_ge(s_pv, i * TB + j + 1)
                    act.activation(probT[:, :, :].rearrange("p g q -> p (g q)"), pt_ps, ACT.Copy).then_inc(s_pt, 1)
                turn_evac(act, turns, oT)
            turns.end_loop(B)

        def l0_attn_gpsimd(pool):
            rms_gpsimd(pool, 0)
            pool.wait_ge(s_l0_load, 16 * 7)
            pool.wait_ge(s_turn_out, 1)
            pool.wait_ge(s_vout, 1)
            with pool.Fori(0, B) as i:
                ln_gpsimd(pool, i)
                pool.wait_ge(s_score, i * TB + 1)
                pool.wait_ge(s_pv, i * TB + 1)
                for c in range(C):
                    pool.tensor_tensor(l0_kdiag[:, c, :, :],
                                       l0_kT[:, c:c + 1, bass.ds(i * SK, SK)].to_broadcast([P, HB0, SK]),
                                       head_of[:, :].unsqueeze(2).to_broadcast([P, HB0, SK]), ALU.mult)
                pool.tensor_tensor(l0_vdiag[:, :, :, :],
                                   tile_of(l0_v, i).rearrange("p (g a d) -> p g a d", a=2, d=HD0),
                                   half_of[:, :].unsqueeze(1).unsqueeze(3).to_broadcast([P, H0 // 2, 2, HD0]),
                                   ALU.mult).then_inc(s_diag, 1)
                rms_gpsimd(pool, i + 1)

        def l0_attn_vector(dve, st):
            dve.wait_ge(s_l0_load, 16 * 7)
            rms_vector(dve, 0, l0_gain[:, 1, :], 0)
            with dve.Fori(0, B) as i:
                st.loop(i, 4 + TB * 3)
                ln_vector(dve, st, i, i)
                ln_apply(dve, i, i * 3 + 1)
                rms_vector(dve, i + 1, l0_gain[:, 0, :], i * 3 + 1)

                def shift(j):
                    dve.wait_ge(s_score, i * TB + j + 2)
                    st.done(dve.tensor_reduce(top[:, 0:H0], sc_ps.rearrange("p (h k) -> p h k", h=H0), AX, ALU.max))
                    dve.wait_ge(s_ptT, i * TB + j + 1)
                    dve.tensor_tensor(prob[:, :].rearrange("p (h k) -> p h k", h=H0),
                                      sc_ps.rearrange("p (h k) -> p h k", h=H0),
                                      top[:, 0:H0].unsqueeze(2).to_broadcast([P, H0, SK]),
                                      ALU.subtract).then_inc(s_shift, 1)

                def norm(j):
                    dve.wait_ge(s_exp, i * TB + j + 1)
                    st.done(dve.tensor_reduce(total[:, 0:H0], prob[:, :].rearrange("p (h k) -> p h k", h=H0), AX, ALU.add))
                    st.done(dve.reciprocal(total[:, 0:H0], total[:, 0:H0]))

                def heads(j):
                    dve.wait_ge(s_pv, i * TB + j + 2)
                    dve.tensor_tensor(qn[:, j, :].rearrange("p (h d) -> p h d", h=H0),
                                      pv_ps.rearrange("p (h d) -> p h d", h=H0),
                                      total[:, 0:H0].unsqueeze(2).to_broadcast([P, H0, HD0]),
                                      ALU.mult).then_inc(s_o, 1)

                for j in range(TB):
                    shift(j)
                    norm(j)
                    heads(j)
                for j in range(TB):
                    dve.wait_ge(s_y, i * TB + j + 1)
                    dve.scalar_tensor_tensor(out=tile_of(x, i * TB + j), in0=y_ps, scalar=gates[:, 0:1],
                                             in1=tile_of(x, i * TB + j), op0=ALU.mult, op1=ALU.add).then_inc(s_res, 1)
            st.end_loop(B)

        scratch.restart()
        f0_w = ffn_region.take([P, 2, C, I0])
        f0_down = ffn_region.take([P, I0 // P, D])
        act_f = scratch.take([P, I0])
        hid = scratch.take([P, I0])
        mag = scratch.take([P, I0])
        beats = scratch.take([P, 6, I0 // 4], BF16)
        wins = scratch.take([P, 4, I0 // 4], BF16)
        hidT = scratch.take([P, I0 // P, P])

        s_f0_load = sem("f0_load")
        s_gate = sem("gate_ready")
        s_up = sem("up_ready")
        s_act = sem("act_ready")
        s_hid = sem("hidden_ready")
        s_mag = sem("magnitude_ready")
        s_kept = sem("hidden_kept")
        s_htT = sem("hidden_turned")
        s_ht = sem("hidden_turn_out")
        s_fy = sem("ffn_out_ready")

        gate_ps = bank(1, 2)
        up_ps = bank(3, 2)
        ht_ps = bank(5, 2)

        def l0_ffn_sync(sp):
            sp.dma_start(f0_w[:, :, :, :], A["f0_w"]).then_inc(s_f0_load, 16)
            sp.dma_start(f0_down[:, :, :], A["f0_down"]).then_inc(s_f0_load, 16)

        def l0_ffn_gpsimd(pool):
            with pool.Fori(0, B) as i:
                ln_gpsimd(pool, i + B)

        def l0_ffn_tensor(pe, turns):
            pe.wait_ge(s_f0_load, 32)
            pe.wait_ge(s_res, NT + 1)
            with pe.Fori(0, B) as i:
                turns.loop(i, 1)
                pe.wait_ge(s_ln_norm, i + B + 1)
                turn_batch(pe, turns, xn)
                pe.wait_ge(s_turn_out, turns.now())
                for j in range(TB):
                    pe.wait_ge(s_hid, i * TB + j + 1)
                    for w, ps, ready in ((0, gate_ps, s_gate), (1, up_ps, s_up)):
                        for n in range(I0 // BANK):
                            for c in range(C):
                                ins = pe.matmul(ps[:, n * BANK:(n + 1) * BANK], xT[:, c, j * P:(j + 1) * P],
                                                f0_w[:, w, c, n * BANK:(n + 1) * BANK],
                                                start=(c == 0), stop=(c == C - 1))
                        ins.then_inc(ready, 1)
                for j in range(TB):
                    pe.wait_ge(s_kept, i * TB + j + 2)
                    pe.wait_ge(s_ht, i * TB + j + 1)
                    for g in range(I0 // P):
                        ins = pe.transpose(ht_ps[:, g * P:(g + 1) * P], hid[:, g * P:(g + 1) * P], ident[:, :])
                    ins.then_inc(s_htT, 1)
                    pe.wait_ge(s_ht, i * TB + j + 2)
                    pe.wait_ge(s_res, i * TB + j + NT + 1)
                    for g in range(I0 // P):
                        ins = pe.matmul(y_ps, hidT[:, g, :], f0_down[:, g, :], start=(g == 0), stop=(g == I0 // P - 1))
                    ins.then_inc(s_fy, 1)
            turns.end_loop(B)

        def l0_ffn_scalar(act, turns):
            with act.Fori(0, B) as i:
                turns.loop(i, 1)
                turn_evac(act, turns, xT)
                for j in range(TB):
                    act.wait_ge(s_gate, i * TB + j + 1)
                    act.wait_ge(s_hid, i * TB + j + 1)
                    act.activation(act_f[:, :], gate_ps, ACT.Tanh, scale=0.5).then_inc(s_act, 1)
                    act.wait_ge(s_hid, i * TB + j + 2)
                    act.wait_ge(s_kept, i * TB + j + 1)
                    act.activation(mag[:, :], hid[:, :], ACT.Abs).then_inc(s_mag, 1)
                    act.wait_ge(s_htT, i * TB + j + 2)
                    act.wait_ge(s_fy, i * TB + j + 1)
                    act.activation(hidT[:, :, :].rearrange("p g q -> p (g q)"), ht_ps, ACT.Copy).then_inc(s_ht, 1)
            turns.end_loop(B)

        def l0_ffn_vector(dve, st):
            quad = lambda v: v.rearrange("p (n f) -> p f n", f=4)
            with dve.Fori(0, B) as i:
                st.loop(i, 4 + TB * 12)
                ln_vector(dve, st, i, i + B)
                ln_apply(dve, i, i + 13)
                for j in range(TB):
                    dve.wait_ge(s_act, i * TB + j + 1)
                    st.done(dve.scalar_tensor_tensor(out=act_f[:, :], in0=act_f[:, :], scalar=1.0, in1=gate_ps,
                                                     op0=ALU.add, op1=ALU.mult))
                    dve.wait_ge(s_up, i * TB + j + 1)
                    dve.wait_ge(s_htT, i * TB + j + 1)
                    dve.scalar_tensor_tensor(out=hid[:, :], in0=act_f[:, :], scalar=0.5, in1=up_ps,
                                             op0=ALU.mult, op1=ALU.mult).then_inc(s_hid, 1)
                    dve.wait_ge(s_mag, i * TB + j + 1)
                    m = quad(mag[:, :])
                    for first, n, at in ((0, 3, 0), (1, 2, 3), (2, 1, 5)):
                        st.mark(dve.tensor_tensor(beats[:, at:at + n, :],
                                                  m[:, first:first + 1, :].to_broadcast([P, n, I0 // 4]),
                                                  m[:, first + 1:4, :], ALU.is_ge))
                    st.wait()
                    for v, (a, b, op) in enumerate(((0, 1, ALU.add), (3, 4, ALU.add), (5, 1, ALU.subtract), (2, 4, ALU.add))):
                        st.mark(dve.tensor_tensor(wins[:, v, :], beats[:, a, :], beats[:, b, :], op))
                    st.wait()
                    for v, (c, op) in enumerate(((2, ALU.add), (0, ALU.subtract), (3, ALU.subtract), (5, ALU.add))):
                        st.mark(dve.tensor_tensor(wins[:, v, :], wins[:, v, :], beats[:, c, :], op))
                    st.wait()
                    h = quad(hid[:, :])
                    for v, (bound, op) in enumerate(((2.0, ALU.is_ge), (1.0, ALU.is_ge), (0.0, ALU.is_ge), (1.0, ALU.is_le))):
                        ins = dve.scalar_tensor_tensor(out=h[:, v, :], in0=wins[:, v, :], scalar=bound, in1=h[:, v, :],
                                                       op0=op, op1=ALU.mult)
                    ins.then_inc(s_kept, 1)
                add_residual(dve, i, 1, s_fy)
            st.end_loop(B)

        def add_residual(dve, i, gate, ready):
            for j in range(TB):
                dve.wait_ge(ready, i * TB + j + 2)
                dve.scalar_tensor_tensor(out=tile_of(x, i * TB + j), in0=y_ps, scalar=gates[:, gate:gate + 1],
                                         in1=tile_of(x, i * TB + j), op0=ALU.mult, op1=ALU.add).then_inc(s_res, 1)

        scratch.restart()
        attn_region.restart()
        l1_kvc = attn_region.take([P, C, KC1])
        l1_dq = attn_region.take([P, C, QC1])
        l1_uqT = attn_region.take([P, H1, QC1])
        l1_qr = attn_region.take([QC1, 2, H1 * R1])
        l1_uk = attn_region.take([KC1, H1 * HD1])
        l1_kr = attn_region.take([KC1, 2, P])
        l1_uv = attn_region.take([KC1, H1 * HD1])
        l1_wo = attn_region.take([P, H1, D])
        l1_keys = attn_region.take([QC1, B, H1, SK])
        l1_vals = attn_region.take([P, B, H1 // 2, D])
        l1_cos = scratch.take([P, S])
        l1_sin = scratch.take([P, S])
        kvT = scratch.take([KC1, CT])
        kv_h = scratch.take([P, 2, 2, CT])
        krot = scratch.take([P, 2, CT])
        krdiag = scratch.take([P, B, 2, SK])
        qcT = scratch.take([QC1, S])
        qrot = scratch.take([P, 2, 2, S])
        qrT = scratch.take([P, H1 // 2, S])
        seg_i = sb("seg_i", [P, NT], I32)
        seg = scratch.take([P, NT])
        key_at = scratch.take([P, SK])
        key_last = scratch.take([P, SK])
        seen = scratch.take([P, NT, SK])
        unseen = scratch.take([P, NT, SK])

        s_l1_load = sem("l1_load")
        s_kvT = sem("kv_compressed")
        s_kvT_out = sem("kv_compressed_out")
        s_kr = sem("keys_to_rotate")
        s_krdiag = sem("rotated_keys_ready")
        s_kvh = sem("head_kv_ready")
        s_kvh_out = sem("head_kv_out")
        s_keys = sem("head_keys_ready")
        s_keys_out = sem("head_keys_out")
        s_vals = sem("pair_values_ready")
        s_vals_out = sem("pair_values_out")
        s_qc = sem("queries_compressed")
        s_qc_out = sem("queries_compressed_out")
        s_qr = sem("queries_to_rotate")
        s_qrot = sem("queries_multiplied")
        s_qrT = sem("queries_rotated")
        s_prob = sem("probs_ready")

        L1_LOADS = 13
        l1_names = ("l1_kvc", "l1_dq", "l1_uqT", "l1_qr", "l1_uk", "l1_kr", "l1_uv", "l1_wo")

        def l1_attn_sync(sp):
            sp.wait_ge(s_res, NT + 1)
            for dst, name in zip((l1_kvc, l1_dq, l1_uqT, l1_qr, l1_uk, l1_kr, l1_uv, l1_wo), l1_names):
                sp.dma_start(dst, A[name]).then_inc(s_l1_load, 16)
            sp.dma_start(seg_i[:, :], A["seg"]).then_inc(s_l1_load, 16)
            sp.wait_ge(s_res, 2 * NT + 1)
            for dst, name in ((l1_cos, "l1_cos"), (l1_sin, "l1_sin"), (key_at, "key_at"), (key_last, "key_last")):
                sp.dma_start(dst, A[name]).then_inc(s_l1_load, 16)

        def l1_attn_gpsimd(pool):
            with pool.Fori(0, B) as i:
                ln_gpsimd(pool, i + 2 * B)
                for g in range(4):
                    pool.wait_ge(s_qrot, i * 4 + g + 1)
                    pool.wait_ge(s_score, i * TB + NT + 1)
                    pool.tensor_tensor(qrT[:, 2 * g:2 * g + 2, :], qrot[:, 0, :, :], qrot[:, 1, :, :],
                                       ALU.add).then_inc(s_qrT, 1)

        kvh_ps = [bank(1 + k).rearrange("p (a n) -> p a n", a=2) for k in range(2)]
        keys_ps = bank(3).rearrange("p (a n) -> p a n", a=2)
        vals_ps = [bank(4, 2), bank(6, 2)]
        qr_ps = [[bank(1), bank(2)], [bank(4), bank(5)]]
        sc1_ps = bank(2, 2)

        def l1_attn_tensor(pe, turns):
            pe.wait_ge(s_l1_load, 16 * L1_LOADS)
            pe.wait_ge(s_res, 2 * NT + 1)
            for c in range(C):
                ins = pe.matmul(kvh_ps[0][0:KC1, 0, :], l1_kvc[:, c, :], ctxT[:, c, :], start=(c == 0), stop=(c == C - 1))
            ins.then_inc(s_kvT, 1)
            pe.wait_ge(s_kvT_out, 1)
            for a in range(2):
                ins = pe.matmul(keys_ps[:, a, :], l1_kr[:, a, :], kvT, start=True, stop=True)
            ins.then_inc(s_kr, 1)

            def head_kv(h):
                if h >= 2:
                    pe.wait_ge(s_kvh_out, h - 1)
                pe.matmul(kvh_ps[h % 2][:, 0, :], l1_uk[:, h * HD1:(h + 1) * HD1], kvT, start=True, stop=True)
                pe.matmul(kvh_ps[h % 2][:, 1, :], l1_uv[:, h * HD1:(h + 1) * HD1], kvT, start=True, stop=True)\
                  .then_inc(s_kvh, 1)

            head_kv(0)
            pe.wait_ge(s_krdiag, 1)
            for h in range(H1):
                if h + 1 < H1:
                    head_kv(h + 1)
                pe.wait_ge(s_kvh_out, h + 1)
                if h >= 2:
                    pe.wait_ge(s_keys_out, h - 1)
                pe.matmul(keys_ps[0:QC1, h % 2, :], l1_uqT[:, h, :], kv_h[:, h % 2, 0, :],
                          start=True, stop=True).then_inc(s_keys, 1)
                if h % 2 == 0 and h >= 4:
                    pe.wait_ge(s_vals_out, h // 2 - 1)
                for b in range(B):
                    ins = pe.matmul(vals_ps[h // 2 % 2][SK * (h % 2):SK * (h % 2) + SK, b * D:(b + 1) * D],
                                    kv_h[:, h % 2, 1, b * SK:(b + 1) * SK], l1_wo[:, h, :], start=True, stop=True)
                ins.then_inc(s_vals, 1)
            pe.wait_ge(s_vals_out, H1 // 2)
            pe.wait_ge(s_keys_out, H1)
            with pe.Fori(0, B) as i:
                turns.loop(i, 1)
                pe.wait_ge(s_ln_norm, i + 2 * B + 1)
                turn_batch(pe, turns, xn)
                pe.wait_ge(s_turn_out, turns.now())
                for c in range(C):
                    ins = pe.matmul(pv_ps[0:QC1, :], l1_dq[:, c, :], xT[:, c, :], start=(c == 0), stop=(c == C - 1))
                ins.then_inc(s_qc, 1)
                pe.wait_ge(s_qc_out, i + 1)
                pe.wait_ge(s_shift, i * TB + NT + 1)
                for g in range(4):
                    if g >= 2:
                        pe.wait_ge(s_qrot, i * 4 + g - 1)
                    for a in range(2):
                        for k in range(2):
                            h = 2 * (2 * g + k)
                            ins = pe.matmul(qr_ps[g % 2][a][:, k * S:(k + 1) * S], l1_qr[:, a, h * R1:(h + 2) * R1], qcT,
                                            start=True, stop=True)
                    ins.then_inc(s_qr, 1)
                pe.wait_ge(s_qrT, i * 4 + 5)
                for j in range(TB):
                    pe.wait_ge(s_shift, i * TB + j + NT + 1)
                    for n in range(2):
                        keys = l1_keys[:, bass.ds(i, 1), 8 * n:8 * n + 8, :].rearrange("p a h k -> p (a h k)")
                        pe.matmul(sc1_ps[:, n * BANK:(n + 1) * BANK], qcT[:, j * P:(j + 1) * P], keys,
                                  start=True, stop=False)
                        for g in range(4 * n, 4 * n + 4):
                            ins = pe.matmul(sc1_ps[:, g * P:(g + 1) * P], qrT[:, g, j * P:(j + 1) * P],
                                            krdiag[:, bass.ds(i, 1), :, :].rearrange("p b a k -> p (b a k)"),
                                            start=False, stop=(g % 4 == 3))
                    ins.then_inc(s_score, 1)
                    pe.wait_ge(s_prob, i * TB + j + 1)
                    pe.wait_ge(s_pt, i * TB + j + NT + 1)
                    for g in range(8):
                        ins = pe.transpose(pt_ps[:, g * P:(g + 1) * P], prob[:, g * P:(g + 1) * P], ident[:, :])
                    ins.then_inc(s_ptT, 1)
                    pe.wait_ge(s_pt, i * TB + j + NT + 2)
                    pe.wait_ge(s_res, i * TB + j + 2 * NT + 1)
                    for g in range(8):
                        ins = pe.matmul(y_ps, probT[:, g, :],
                                        l1_vals[:, bass.ds(i, 1), g, :].rearrange("p b n -> p (b n)"),
                                        start=(g == 0), stop=(g == 7))
                    ins.then_inc(s_y, 1)
            turns.end_loop(B)

        def l1_attn_scalar(act, turns):
            act.wait_ge(s_kvT, 1)
            act.activation(kvT, kvh_ps[0][0:KC1, 0, :], ACT.Copy).then_inc(s_kvT_out, 1)
            for h in range(H1):
                act.wait_ge(s_kvh, h + 1)
                if h >= 2:
                    act.wait_ge(s_vals, h - 1)
                act.activation(kv_h[:, h % 2, :, :], kvh_ps[h % 2], ACT.Copy).then_inc(s_kvh_out, 1)
                act.wait_ge(s_keys, h + 1)
                act.activation(l1_keys[:, :, h, :], keys_ps[0:QC1, h % 2, :].rearrange("p (b k) -> p b k", b=B),
                               ACT.Copy).then_inc(s_keys_out, 1)
            with act.Fori(0, B) as i:
                turns.loop(i, 1)
                turn_evac(act, turns, xT)
                act.wait_ge(s_qc, i + 1)
                act.wait_ge(s_score, i * TB + NT + 1)
                act.activation(qcT, pv_ps[0:QC1, :], ACT.Copy).then_inc(s_qc_out, 1)
                for j in range(TB):
                    act.wait_ge(s_shift, i * TB + j + NT + 2)
                    act.activation(prob[:, :], prob[:, :], ACT.Exp, scale=(HD1 + R1) ** -0.5).then_inc(s_exp, 1)
                    act.wait_ge(s_ptT, i * TB + j + NT + 2)
                    act.wait_ge(s_y, i * TB + j + NT)
                    act.activation(probT[:, :, :].rearrange("p g q -> p (g q)"), pt_ps, ACT.Copy).then_inc(s_pt, 1)
            turns.end_loop(B)

        def l1_attn_vector(dve, st):
            dve.wait_ge(s_l1_load, 16 * L1_LOADS)
            st.done(dve.tensor_copy(seg, seg_i[:, :]))
            wide = lambda v, axis: v.unsqueeze(axis).to_broadcast([P, NT, SK])
            st.mark(dve.tensor_tensor(seen, wide(key_at, 1), wide(seg, 2), ALU.is_le))
            st.done(dve.tensor_tensor(unseen, wide(key_last, 1), wide(seg, 2), ALU.is_ge))
            st.done(dve.tensor_tensor(unseen, unseen, seen, ALU.mult))
            st.done(dve.tensor_scalar(unseen, unseen, -1.0, 1e30, ALU.add, ALU.mult))
            dve.wait_ge(s_kr, 1)
            for a, table in enumerate((l1_cos, l1_sin)):
                st.mark(dve.tensor_tensor(krot[:, a, :].rearrange("p (b k) -> p b k", b=B),
                                          keys_ps[:, a, :].rearrange("p (b k) -> p b k", b=B),
                                          table[:, 0:SK].unsqueeze(1).to_broadcast([P, B, SK]), ALU.mult))
            st.wait()
            st.done(dve.tensor_tensor(krot[:, 0, :], krot[:, 0, :], krot[:, 1, :], ALU.add))
            for b in range(B):
                ins = st.mark(dve.tensor_tensor(krdiag[:, b, :, :],
                                                krot[:, 0:1, b * SK:(b + 1) * SK].to_broadcast([P, 2, SK]),
                                                half_of[:, :].unsqueeze(2).to_broadcast([P, 2, SK]), ALU.mult))
            st.wait()
            dve.engine_nop().then_inc(s_krdiag, 1)
            for g in range(H1 // 2):
                dve.wait_ge(s_vals, 2 * g + 2)
                dve.tensor_copy(l1_vals[:, :, g, :], vals_ps[g % 2].rearrange("p (b n) -> p b n", b=B)).then_inc(s_vals_out, 1)
            with dve.Fori(0, B) as i:
                st.loop(i, 4 + TB * 4)
                ln_vector(dve, st, i, i + 2 * B)
                ln_apply(dve, i, i + 17)
                for g in range(4):
                    dve.wait_ge(s_qr, i * 4 + g + 1)
                    dve.wait_ge(s_qrT, i * 4 + g + 1)
                    for a, table in enumerate((l1_cos, l1_sin)):
                        ins = dve.tensor_tensor(qrot[:, a, :, :], qr_ps[g % 2][a].rearrange("p (k s) -> p k s", k=2),
                                                table.unsqueeze(1).to_broadcast([P, 2, S]), ALU.mult)
                    ins.then_inc(s_qrot, 1)
                for j in range(TB):
                    heads = lambda v: v.rearrange("p (h k) -> p h k", h=H1)
                    per_head = lambda v: v[:, 0:H1].unsqueeze(2).to_broadcast([P, H1, SK])
                    dve.wait_ge(s_score, i * TB + j + NT + 2)
                    dve.wait_ge(s_ptT, i * TB + j + NT + 1)
                    st.done(dve.tensor_tensor(heads(prob[:, :]), heads(sc1_ps),
                                              unseen[:, bass.ds(i * TB + j, 1), :].to_broadcast([P, H1, SK]), ALU.add))
                    st.done(dve.tensor_reduce(top[:, 0:H1], heads(prob[:, :]), AX, ALU.max))
                    dve.tensor_tensor(heads(prob[:, :]), heads(prob[:, :]), per_head(top), ALU.subtract).then_inc(s_shift, 1)
                    dve.wait_ge(s_exp, i * TB + j + NT + 1)
                    st.done(dve.tensor_reduce(total[:, 0:H1], heads(prob[:, :]), AX, ALU.add))
                    st.done(dve.reciprocal(total[:, 0:H1], total[:, 0:H1]))
                    dve.tensor_tensor(heads(prob[:, :]), heads(prob[:, :]), per_head(total), ALU.mult).then_inc(s_prob, 1)
                for j in range(TB):
                    dve.wait_ge(s_y, i * TB + j + NT + 1)
                    dve.scalar_tensor_tensor(out=tile_of(x, i * TB + j), in0=y_ps, scalar=gates[:, 2:3],
                                             in1=tile_of(x, i * TB + j), op0=ALU.mult, op1=ALU.add).then_inc(s_res, 1)
            st.end_loop(B)

        SLOTS = 4
        UNITS = 2 * SLOTS
        HT = T // 2
        scratch.restart()
        ffn_region.restart()
        xT_all = scratch.take([P, C, T])
        weight_of = scratch.take([P, NT, E3 + 1])
        act_u = scratch.take([P, 2, HT])
        hid_u = scratch.take([P, 2, HT])
        expert_w = ffn_region.take([P, SLOTS, 3 * D])
        r_top = scratch.take([P, TB, 1])
        r_sum = scratch.take([P, TB, 1])
        moe_mark = scratch.at

        s_xall = sem("all_transposed")
        s_expert = [sem(f"expert_loaded_{k}") for k in range(SLOTS)]
        s_ugate = sem("unit_gate_ready")
        s_uup = sem("unit_up_ready")
        s_uact = sem("unit_act_ready")
        s_uhid = sem("unit_hidden_ready")
        s_udown = sem("unit_down_ready")
        s_uadd = sem("unit_tile_added")
        s_logit = sem("logits_ready")
        s_rshift = sem("logits_shifted")
        s_rexp = sem("router_exp_ready")
        s_routed = sem("router_done")

        gate_u = [bank(1), bank(2)]
        up_u = [bank(3), bank(4)]
        down_u = [bank(5, 2), None]
        down_banks = [(5, 6), (7, 0)]

        def down_of(k, q):
            b = down_banks[k][q // 2]
            return bank(b)[:, (q % 2) * D:(q % 2 + 1) * D]

        def experts_sync(sp, name, experts, before, units_before):
            for k in range(SLOTS):
                sp.dma_start(expert_w[:, k, :], A[name][k]).then_inc(s_expert[k], 16)
            if experts > 2 * SLOTS:
                with sp.Fori(1, experts // SLOTS) as t:
                    for k in range(SLOTS):
                        sp.wait_ge(s_udown, t * UNITS + (units_before + 2 * k + 2 + 2 - UNITS))
                        sp.dma_start(expert_w[:, k, :],
                                     A[name][bass.ds(t * SLOTS + k, 1), :, :].rearrange("e p n -> p (e n)"))\
                          .then_inc(s_expert[k], 16)
            if experts % SLOTS:
                sp.wait_ge(s_udown, 2 * experts + (units_before + 2 - UNITS))
                sp.dma_start(expert_w[:, 0, :], A[name][experts - 1]).then_inc(s_expert[0], 16)

        def unit_loop(eng, experts, unit):
            turns = (experts - 1) // SLOTS
            with eng.Fori(0, turns) as t:
                for u in range(UNITS):
                    unit(t, u, True)
            left = 2 * experts - turns * UNITS
            for u in range(left):
                unit(turns, u, u + 1 < left)

        def experts_tensor(pe, experts, before, units_before):
            def gate_up(t, u):
                k = u // 2 % SLOTS
                if u % 2 == 0:
                    pe.wait_ge(s_expert[k], (t + u // UNITS) * 16 + 16 * (before[k] + 1))
                pe.wait_ge(s_uhid, t * UNITS + (units_before + u + 1))
                for a, ps, ready in ((0, gate_u, s_ugate), (1, up_u, s_uup)):
                    for c in range(C):
                        at = (2 * c + a) * I1
                        ins = pe.matmul(ps[u % 2], expert_w[:, k, at:at + I1],
                                        xT_all[:, c, (u % 2) * HT:(u % 2 + 1) * HT], start=(c == 0), stop=(c == C - 1))
                    ins.then_inc(ready, 1)

            def down(t, u):
                pe.wait_ge(s_uhid, t * UNITS + (units_before + u + 1 + 2))
                pe.wait_ge(s_uadd, t * (4 * UNITS) + 4 * (units_before + u + 1))
                for q in range(4):
                    ins = pe.matmul(down_of(u % 2, q), hid_u[:, u % 2, q * P:(q + 1) * P],
                                    expert_w[:, u // 2, 2 * D:3 * D], start=True, stop=True)
                ins.then_inc(s_udown, 1)

            def unit(t, u, more):
                if more:
                    gate_up(t, u + 1)
                down(t, u)

            gate_up(0, 0)
            unit_loop(pe, experts, unit)

        def experts_scalar(act, experts, units_before):
            def tanh(t, u):
                act.wait_ge(s_ugate, t * UNITS + (units_before + u + 1))
                act.wait_ge(s_uhid, t * UNITS + (units_before + u + 1))
                act.activation(act_u[:, u % 2, :], gate_u[u % 2], ACT.Tanh, scale=0.5).then_inc(s_uact, 1)

            tanh(0, 0)
            unit_loop(act, experts, lambda t, u, more: tanh(t, u + 1) if more else None)

        def experts_vector(dve, st, experts, units_before):
            def hidden(t, u):
                k = u % 2
                dve.wait_ge(s_uact, t * UNITS + (units_before + u + 1))
                ins = dve.scalar_tensor_tensor(out=act_u[:, k, :], in0=act_u[:, k, :], scalar=1.0, in1=gate_u[k],
                                               op0=ALU.add, op1=ALU.mult)
                ins.then_inc(s_uown, 1)
                dve.wait_ge(s_uown, t * UNITS + (units_before + u + 1))
                dve.wait_ge(s_uup, t * UNITS + (units_before + u + 1))
                dve.wait_ge(s_udown, t * UNITS + (units_before + u + 1))
                dve.scalar_tensor_tensor(out=hid_u[:, k, :], in0=act_u[:, k, :], scalar=0.5, in1=up_u[k],
                                         op0=ALU.mult, op1=ALU.mult).then_inc(s_uhid, 1)

            def add(t, u):
                dve.wait_ge(s_udown, t * UNITS + (units_before + u + 1 + 2))
                dve.wait_ge(s_uadd, t * (4 * UNITS) + 4 * (units_before + u + 1))
                for q in range(4):
                    n = (u % 2) * 4 + q
                    weight = weight_of[:, n, bass.ds(t * SLOTS + u // 2, 1)]
                    dve.scalar_tensor_tensor(out=x[:, n, :], in0=down_of(u % 2, q), scalar=weight, in1=x[:, n, :],
                                             op0=ALU.mult, op1=ALU.add).then_inc(s_uadd, 1)

            def unit(t, u, more):
                if more:
                    hidden(t, u + 1)
                add(t, u)

            hidden(0, 0)
            unit_loop(dve, experts, unit)
            dve.wait_ge(s_uadd, 4 * (units_before + 2 * experts + 2))
            dve.engine_nop().then_inc(s_res, NT)

        s_uown = sem("unit_act_times_gate")

        W1 = E1 + 8
        f1_router = scratch.take([P, C, E1])
        f1_bias = scratch.take([1, E1])
        below = scratch.take([P, 8])
        r_prob = scratch.take([P, TB, W1])
        r_rest = scratch.take([P, TB, W1])
        r_eight = scratch.take([P, TB, 8])
        r_two = scratch.take([P, TB, 8])

        s_f1_load = sem("f1_load")
        logit_ps = bank(6)

        def l1_ffn_sync(sp):
            sp.wait_ge(s_res, 3 * NT + 1)
            sp.dma_start(f1_router, A["f1_router"]).then_inc(s_f1_load, 16)
            sp.dma_start(f1_bias, A["f1_bias"]).then_inc(s_f1_load, 16)
            sp.dma_start(below, A["below"]).then_inc(s_f1_load, 16)
            experts_sync(sp, "f1_experts", E1 + 1, 0, 0)

        def router_tensor(pe, turns, n, r, load, load_at, router, experts, bias):
            pe.wait_ge(load, load_at)
            with pe.Fori(0, B) as i:
                turns.loop(i, 1)
                pe.wait_ge(s_ln_norm, i + n + 1)
                turn_batch(pe, turns, xn)
                pe.wait_ge(s_turn_out, turns.now())
                pe.wait_ge(s_rshift, i + r + 1)
                for j in range(TB):
                    ps = logit_ps[:, j * experts:(j + 1) * experts]
                    if bias is not None:
                        pe.matmul(ps, ones[:, :], bias, start=True, stop=False)
                    for c in range(C):
                        ins = pe.matmul(ps, xT[:, c, j * P:(j + 1) * P], router[:, c, :],
                                        start=(bias is None and c == 0), stop=(c == C - 1))
                ins.then_inc(s_logit, 1)
            turns.end_loop(B)

        def router_scalar(act, turns, r, probs):
            with act.Fori(0, B) as i:
                turns.loop(i, 1)
                act.wait_ge(s_logit, i + r + 1)
                act.wait_ge(s_xall, i + r + 1)
                turn_evac(act, turns, xT)
                act.wait_ge(s_rshift, i + r + 2)
                act.activation(probs, probs, ACT.Exp).then_inc(s_rexp, 1)
            turns.end_loop(B)

        def router_gpsimd(pool, n, turns_before, r):
            with pool.Fori(0, B) as i:
                ln_gpsimd(pool, i + n)
                pool.wait_ge(s_turn_out, i + turns_before + 1)
                pool.tensor_copy(xT_all[:, :, bass.ds(i * S, S)], xT[:, :, :]).then_inc(s_xall, 1)

        def router_softmax(dve, st, i, r, probs, experts):
            logits = logit_ps[:, 0:TB * experts].rearrange("p (j e) -> p j e", j=TB)
            spread = lambda v: v.to_broadcast([P, TB, experts])
            dve.wait_ge(s_logit, i + r + 2)
            st.done(dve.tensor_reduce(r_top[:, :, 0], logits, AX, ALU.max))
            dve.tensor_tensor(probs, logits, spread(r_top), ALU.subtract).then_inc(s_rshift, 1)
            dve.wait_ge(s_rexp, i + r + 1)
            st.done(dve.tensor_reduce(r_sum[:, :, 0], probs, AX, ALU.add))
            st.done(dve.reciprocal(r_sum, r_sum))
            st.mark(dve.tensor_tensor(probs, probs, spread(r_sum), ALU.mult))
            st.wait()
            settle(dve)

        def l1_ffn_tensor(pe, turns):
            router_tensor(pe, turns, 3 * B, 0, s_f1_load, 48, f1_router, E1, f1_bias)
            pe.wait_ge(s_xall, B + 1)
            pe.wait_ge(s_rshift, B + 1)
            experts_tensor(pe, E1 + 1, [0] * SLOTS, 0)

        def l1_ffn_scalar(act, turns):
            router_scalar(act, turns, 0, r_prob[:, :, 0:E1])
            experts_scalar(act, E1 + 1, 0)

        def l1_ffn_gpsimd(pool):
            router_gpsimd(pool, 3 * B, 21, 0)

        def l1_ffn_vector(dve, st):
            dve.engine_nop().then_inc(s_uhid, 2)
            dve.engine_nop().then_inc(s_udown, 2)
            dve.engine_nop().then_inc(s_uadd, 8)
            dve.wait_ge(s_f1_load, 48)
            st.mark(dve.memset(weight_of[:, :, E1:E1 + 1], 1.0))
            for j in range(TB):
                st.mark(dve.tensor_copy(r_prob[:, j, E1:W1], below))
                st.mark(dve.tensor_copy(r_two[:, j, :], below))
            st.wait()
            with dve.Fori(0, B) as i:
                st.loop(i, 4 + 4 + 2 + 1 + 2 + 1 + 1 + 1 + 1 + 1 + 1)
                ln_vector(dve, st, i, i + 3 * B)
                ln_apply(dve, i, i + 21)
                probs = r_prob[:, :, 0:E1]
                spread = lambda v: v.to_broadcast([P, TB, E1])
                router_softmax(dve, st, i, 0, probs, E1)
                for j in range(TB):
                    st.mark(dve.max(r_eight[:, j, :], r_prob[:, j, 0:E1]))
                st.wait()
                st.mark(dve.tensor_copy(r_two[:, :, 0:2], r_eight[:, :, 0:2]))
                st.wait()
                settle(dve)
                for j in range(TB):
                    st.mark(dve.match_replace(out=r_rest[:, j, :], in_to_replace=r_two[:, j, :],
                                              in_values=r_prob[:, j, :], imm_value=-9.0))
                st.wait()
                st.done(dve.tensor_tensor(r_rest[:, :, 0:E1], r_rest[:, :, 0:E1], probs, ALU.not_equal))
                st.done(dve.tensor_tensor(r_rest[:, :, 0:E1], r_rest[:, :, 0:E1], probs, ALU.mult))
                st.done(dve.tensor_reduce(r_sum[:, :, 0], r_rest[:, :, 0:E1], AX, ALU.add))
                st.done(dve.tensor_scalar(r_sum, r_sum, 1e-9, None, ALU.add))
                st.done(dve.reciprocal(r_sum, r_sum))
                st.done(dve.tensor_tensor(weight_of[:, bass.ds(i * TB, TB), 0:E1], r_rest[:, :, 0:E1],
                                          spread(r_sum), ALU.mult))
            st.end_loop(B)
            st.done(dve.tensor_scalar(weight_of[:, :, 0:E1 + 1], weight_of[:, :, 0:E1 + 1], gates[:, 3:4], None, ALU.mult))
            dve.wait_ge(s_turned, 25)
            experts_vector(dve, st, E1 + 1, 0)

        scratch.restart()
        scratch.at = 1280
        attn_region.restart()
        HQ = 4
        QC = P // (HQ * HD2)
        NQ = H2 // HQ
        W = HQ * HD2
        SELF = C * HQ
        CROSS = C
        TU = SELF + CROSS
        BU = TB * TU
        LAG = 4
        l2_w = attn_region.take([P, 6, C, D])
        l2_ctxT2 = attn_region.take([P, C, B, P])
        l2_cos = attn_region.take([P, S])
        l2_sin = attn_region.take([P, S])
        eight_of = attn_region.take([P, HQ, 2])
        l2_head_of = attn_region.take([P, H2 // C])
        l2_gate = attn_region.take([P, H2])
        l2_kT = attn_region.take([P, C, S])
        l2_akT = attn_region.take([P, C, CT])
        l2_av = attn_region.take([P, B, D])
        l2_kdiag = attn_region.take([P, C, HQ, 2, S])
        l2_akdiag = attn_region.take([P, C, H2 // C, SK])
        l2_vwide = attn_region.take([P, W + TB * H2 * W])
        l2_avwide = attn_region.take([P, W + H2 // 2 * W])
        l2_v_at = l2_vwide[:, W:].rearrange("p (n w) -> p n w", w=W)
        l2_av_at = l2_avwide[:, W:].rearrange("p (n w) -> p n w", w=W)
        l2_mask = attn_region.take([P, TB, S])
        l2_qT = attn_region.take([P, C, S])
        l2_rot = scratch.take([P, 2, 2, C * S])
        l2_rep = scratch.take([P, 2, D])
        l2_raw = scratch.take([P, 2, C, P])
        l2_oT = scratch.take([P, C, S])
        l2_prob = attn_region.take([P, LAG, 1024])
        l2_probT = scratch.take([P, 2, 8, P])
        l2_halves = scratch.take([P, H2 // 2, SK // 2])
        l2_max = attn_region.take([P, LAG, HQ])
        l2_neg = attn_region.take([P, LAG, HQ])
        l2_cmax = attn_region.take([P, LAG, H2 // 2])
        l2_sum = attn_region.take([P, TB, H2])
        l2_csum = attn_region.take([P, TB, H2])

        s_l2_load = sem("l2_load")
        s_mask = sem("mask_loaded")
        s_mask_ok = sem("mask_clamped")
        s_l2_ctx = sem("l2_context_projected")
        s_l2_ctx_out = sem("l2_context_out")
        s_l2_qk = sem("l2_qk_projected")
        s_l2_v = sem("l2_v_projected")
        s_l2_v_out = sem("l2_v_out")
        s_l2_mul = sem("l2_qk_multiplied")
        s_l2_rot = sem("l2_qk_rotated")
        s_l2_diag = sem("l2_diag_ready")
        s_l2_zero = sem("l2_zeros_set")
        s_ptT_b = sem("probs_turned_second_half")
        s_pt_b = sem("probs_turn_out_second_half")
        s_csum = sem("l2_context_sums_ready")
        s_rep = sem("l2_inverse_sums_ready")
        s_repT = sem("l2_inverse_sums_turned")
        s_oT = sem("l2_heads_ready")

        l2_sc = [bank(1, 2), bank(3, 2)]
        l2_pt_ps = [bank(5), bank(6)]
        l2_o_ps = bank(7).rearrange("p (a c q) -> p a c q", a=2, c=C)
        l2_repT_ps = bank(0)
        l2_y_ps = bank(0)[:, 0:D]
        U0 = 2 * NT
        PV0 = NT
        O0 = NT
        V0 = 2 * NT
        HALF = BANK // P

        L2_LOADS = 7

        def l2_attn_sync(sp):
            sp.wait_ge(s_res, 3 * NT + 1)
            for dst, name in ((l2_w, "l2_w"), (l2_ctxT2, "ctxT2"), (l2_cos, "l2_cos"), (l2_sin, "l2_sin"),
                              (eight_of, "eight_of"), (l2_head_of, "l2_head_of"), (l2_gate, "l2_gate")):
                sp.dma_start(dst, A[name]).then_inc(s_l2_load, 16)
            with sp.Fori(0, B) as i:
                sp.wait_ge(s_shift, i * BU + (U0 - CROSS + 1))
                sp.dma_start(l2_mask, A["mask"][:, bass.ds(i * TB, TB), :]).then_inc(s_mask, 16)

        def l2_attn_gpsimd(pool):
            for signal, start in ((s_ptT_b, LAG), (s_pt_b, 1), (s_csum, 1), (s_repT, 1), (s_oT, 1),
                                  (s_l2_mul, 1)):
                pool.sem_inc(signal, start)
            pool.wait_ge(s_res, 3 * NT + 1)
            pool.memset(l2_vwide, 0.0).then_inc(s_l2_zero, 1)
            pool.memset(l2_avwide, 0.0).then_inc(s_l2_zero, 1)
            pool.wait_ge(s_l2_load, 16 * L2_LOADS)
            pool.wait_ge(s_l2_ctx_out, 2)
            pool.wait_ge(s_l2_zero, 2)
            st = Steps(pool, s_pool)

            def clamp_mask(b):
                pool.wait_ge(s_mask, b * 16 + 16)
                settle(pool)
                pool.tensor_scalar(l2_mask, l2_mask, float(np.finfo(np.float32).min), None, ALU.max).then_inc(s_mask_ok, 1)

            def rotated(b, a, dst):
                pool.tensor_tensor(flat(dst), l2_rot[:, a, 0, :], l2_rot[:, a, 1, :], ALU.add).then_inc(s_l2_rot, 1)

            def prepare(b):
                pool.wait_ge(s_l2_mul, b * 4 + 5)
                rotated(b, 1, l2_kT)
                pool.wait_ge(s_l2_rot, b * 2 + 2)
                for c in range(C):
                    for h in range(HQ):
                        pool.wait_ge(s_score, b * BU + (U0 - TU + HQ * c + h + 2))
                        pool.tensor_tensor(l2_kdiag[:, c, h, :, :], l2_kT[:, c:c + 1, :].to_broadcast([P, 2, S]),
                                           eight_of[:, h, :].unsqueeze(2).to_broadcast([P, 2, S]), ALU.mult).then_inc(s_l2_diag, 1)
                pool.wait_ge(s_score, b * BU + (U0 + 1))
                rotated(b, 0, l2_qT)
                clamp_mask(b)
                for c in range(C):
                    pool.tensor_tensor(l2_akdiag[:, c, :, :],
                                       l2_akT[:, c:c + 1, bass.ds(b * SK, SK)].to_broadcast([P, H2 // C, SK]),
                                       l2_head_of.unsqueeze(2).to_broadcast([P, H2 // C, SK]), ALU.mult).then_inc(s_l2_diag, 1)

            def context_sums(i, j):
                for c in range(CROSS):
                    u = TU * j + SELF + c
                    pool.wait_ge(s_exp, i * BU + (U0 + u + 1))
                    pool.wait_ge(s_csum, i * TB * CROSS + (1 + CROSS * j + c))
                    part = l2_prob[:, u % LAG, :].rearrange("p (h k) -> p h k", k=SK)
                    width = SK // 2
                    while width > 1:
                        half = l2_halves[:, :, 0:width]
                        st.done(pool.tensor_tensor(half, part[:, :, 0:width], part[:, :, width:2 * width], ALU.add))
                        part, width = half, width // 2
                    pool.tensor_tensor(l2_csum[:, j, 16 * c:16 * c + 16].unsqueeze(2), part[:, :, 0:1], part[:, :, 1:2],
                                       ALU.add).then_inc(s_csum, 1)

            def batch(i, more):
                if more:
                    ln_gpsimd(pool, i + 1 + 4 * B)
                context_sums(i, 0)
                if more:
                    prepare(i + 1)
                context_sums(i, 1)

            ln_gpsimd(pool, 4 * B)
            prepare(0)
            with pool.Fori(0, B - 1) as i:
                st.loop(i, TB * CROSS * 5)
                batch(i, True)
            st.end_loop(B - 1)
            batch(B - 1, False)

        def l2_attn_tensor(pe, turns):
            pe.wait_ge(s_l2_load, 16 * L2_LOADS)
            pe.wait_ge(s_res, 4 * NT + 1)
            for m in range(C):
                for c in range(C):
                    ins = pe.matmul(bank(1)[:, m * CT:(m + 1) * CT], l2_w[:, 2, c, m * P:(m + 1) * P], ctxT[:, c, :],
                                    start=(c == 0), stop=(c == C - 1))
            ins.then_inc(s_l2_ctx, 1)
            for b in range(B):
                for c in range(C):
                    ins = pe.matmul(bank(3, 2)[:, b * D:(b + 1) * D], l2_ctxT2[:, c, b, :], l2_w[:, 4, c, :],
                                    start=(c == 0), stop=(c == C - 1))
            ins.then_inc(s_l2_ctx, 1)
            pe.wait_ge(s_l2_ctx_out, 2)

            def turn(b):
                pe.wait_ge(s_ln_norm, b + 4 * B + 1)
                turn_batch(pe, turns, xn)

            def project(b, a):
                pe.wait_ge(s_turn_out, turns.now())
                pe.wait_ge(s_l2_mul, b * 4 + a + 1)
                for m in range(C):
                    for c in range(C):
                        ins = pe.matmul(bank(0)[:, m * S:(m + 1) * S], l2_w[:, a, c, m * P:(m + 1) * P],
                                        xT[:, c, :], start=(c == 0), stop=(c == C - 1))
                ins.then_inc(s_l2_qk, 1)

            def project_values(b):
                for m in range(TB):
                    for c in range(C):
                        ins = pe.matmul(bank(5)[:, m * D:(m + 1) * D], xT[:, c, m * P:(m + 1) * P], l2_w[:, 4, c, :],
                                        start=(c == 0), stop=(c == C - 1))
                ins.then_inc(s_l2_v, 1)

            def batch(i, more):
                def scores(u):
                    j, k = u % BU // TU, u % TU
                    pe.wait_ge(s_shift, i * BU + (U0 + u))
                    c = k // HQ if k < SELF else k - SELF
                    if j == 0:
                        pe.wait_ge(s_l2_diag, i * TU + (u // BU * TU + k + 1))
                        pe.wait_ge(s_l2_rot, i * 2 + (u // BU * 2 + 3))
                    for n in range(2):
                        if k < SELF:
                            rows = slice(2 * W * n, 2 * W * n + 2 * W)
                            keys = l2_kdiag[rows, c, k % HQ, :, :].rearrange("p a k -> p (a k)")
                        else:
                            rows = slice(0, P)
                            keys = l2_akdiag[:, c, 8 * n:8 * n + 8, :].rearrange("p h k -> p (h k)")
                        ins = pe.matmul(l2_sc[u % 2][:, n * BANK:(n + 1) * BANK], l2_qT[rows, c, j * P:(j + 1) * P], keys,
                                        start=True, stop=True)
                    ins.then_inc(s_score, 1)

                def turn_probs(u):
                    pe.wait_ge(s_exp, i * BU + (U0 + u + 1))
                    pe.wait_ge(s_pt, i * BU + (U0 + u) + 1)
                    for g in range(HALF):
                        ins = pe.transpose(l2_pt_ps[0][:, g * P:(g + 1) * P], l2_prob[:, u % LAG, g * P:(g + 1) * P], ident[:, :])
                    ins.then_inc(s_ptT, 1)
                    pe.wait_ge(s_pt_b, i * BU + (u + 1))
                    for g in range(HALF):
                        ins = pe.transpose(l2_pt_ps[1][:, g * P:(g + 1) * P], l2_prob[:, u % LAG, (HALF + g) * P:(HALF + g + 1) * P],
                                           ident[:, :])
                    ins.then_inc(s_ptT_b, 1)

                def weigh(u):
                    j, k = u // TU, u % TU
                    pe.wait_ge(s_pt, i * BU + (U0 + u + 2))
                    pe.wait_ge(s_pt_b, i * BU + (u + 2))
                    if k == 0:
                        pe.wait_ge(s_o, i * TB + (O0 + j) + 1)
                    for e in range(2):
                        for g in range(QC):
                            rows = slice(W * g, W * g + W)
                            if k < SELF:
                                c, h = k // HQ, k % HQ
                                at = W * (1 + e * H2 + 16 * c + HQ * g + h) - HD2 * h
                                ins = pe.matmul(l2_o_ps[rows, 0, c, :], l2_vwide[:, at:at + W], l2_probT[:, u % 2, 2 * g + e, :],
                                          start=(h == 0 and e == 0), stop=(h == HQ - 1 and e == 1))
                            else:
                                c = k - SELF
                                at = W * (1 + 8 * c + 2 * g + e) - 2 * HD2 * e
                                ins = pe.matmul(l2_o_ps[rows, 1, c, :], l2_avwide[:, at:at + W], l2_probT[:, u % 2, 2 * g + e, :],
                                          start=(e == 0), stop=(e == 1))
                    ins.then_inc(s_pv, 1)

                def turn_sums(j):
                    pe.wait_ge(s_rep, i * TB + (j + 1))
                    if j:
                        pe.wait_ge(s_res, i * TB + (4 * NT + j) + 1)
                    for g in range(2 * C):
                        ins = pe.transpose(l2_repT_ps[:, g * P:(g + 1) * P], flat(l2_rep)[:, g * P:(g + 1) * P], ident[:, :])
                    ins.then_inc(s_repT, 1)

                def result(j):
                    pe.wait_ge(s_oT, i * TB + (j + 2))
                    for c in range(C):
                        ins = pe.matmul(l2_y_ps, l2_oT[:, c, j * P:(j + 1) * P], l2_w[:, 5, c, :],
                                        start=(c == 0), stop=(c == C - 1))
                    ins.then_inc(s_y, 1)

                if i is None:
                    i = 0
                    scores(0)
                    scores(1)
                    return
                pe.wait_ge(s_l2_v_out, i + 1)
                for u in range(BU + 1):
                    if u < BU and (more or u + 2 < BU):
                        scores(u + 2)
                    if u < BU:
                        turn_probs(u)
                    if u >= 1:
                        weigh(u - 1)
                    if more and u == 2:
                        pe.wait_ge(s_res, i * TB + 4 * NT + 1)
                        turn(i + 1)
                    if more and 4 <= u < 8:
                        project(i + 1, u - 4)
                    if u == TU + 1:
                        turn_sums(0)
                    if u == TU + 3:
                        result(0)
                if more:
                    project_values(i + 1)
                turn_sums(1)
                result(1)

            turn(0)
            for a in range(4):
                project(0, a)
            project_values(0)
            batch(None, True)
            with pe.Fori(0, B - 1) as i:
                turns.loop(i, 1)
                batch(i, True)
            turns.end_loop(B - 1)
            batch(B - 1, False)

        def l2_attn_scalar(act, turns):
            act.wait_ge(s_l2_load, 16 * L2_LOADS)
            act.activation(l2_gate, l2_gate, ACT.Tanh).then_inc(s_act_own, 1)
            act.wait_ge(s_l2_ctx, 1)
            act.activation(flat(l2_akT), bank(1), ACT.Copy).then_inc(s_l2_ctx_out, 1)
            act.wait_ge(s_l2_ctx, 2)
            act.activation(flat(l2_av), bank(3, 2), ACT.Copy).then_inc(s_l2_ctx_out, 1)
            act.wait_ge(s_l2_zero, 2)
            act.wait_ge(s_l2_ctx_out, 2)

            def values_out(b):
                act.wait_ge(s_l2_v, b + 1)
                act.activation(l2_v_at[:, :, 0:HD2], bank(5).rearrange("p (n d) -> p n d", d=HD2), ACT.Copy)
                for half in range(2):
                    rows = slice(half * SK, half * SK + SK)
                    ins = act.activation(l2_av_at[rows, :, half * HD2:half * HD2 + HD2],
                                         tile_of(l2_av, b)[rows, :].rearrange("p (n a d) -> p n a d", a=2, d=HD2)[:, :, half, :], ACT.Copy)
                ins.then_inc(s_l2_v_out, 1)

            def batch(i, more):
                def exps(u):
                    j, k = u % BU // TU, u % TU
                    act.wait_ge(s_shift, i * BU + (U0 + u + 2))
                    if k < SELF:
                        for g in range(QC):
                            h = 16 * (k // HQ) + HQ * g + k % HQ
                            ins = act.activation(l2_prob[:, u % LAG, g * S:(g + 1) * S], l2_prob[:, u % LAG, g * S:(g + 1) * S],
                                                 ACT.Exp, bias=l2_neg[:, u % LAG, g:g + 1],
                                                 accum_out=l2_sum[:, j, h:h + 1])
                    else:
                        ins = act.activation(l2_prob[:, u % LAG, :], l2_prob[:, u % LAG, :], ACT.Exp)
                    ins.then_inc(s_exp, 1)

                def evac(u):
                    act.wait_ge(s_ptT, i * BU + (U0 + u + 2))
                    act.wait_ge(s_pv, i * BU + (PV0 + u))
                    act.activation(l2_probT[:, u % 2, 0:HALF, :].rearrange("p g q -> p (g q)"), l2_pt_ps[0], ACT.Copy).then_inc(s_pt, 1)
                    if u % TU >= SELF:
                        act.wait_ge(s_ptT_b, i * BU + (u + 1 + LAG))
                        act.activation(l2_probT[:, u % 2, HALF:, :].rearrange("p g q -> p (g q)"), l2_pt_ps[1],
                                       ACT.Copy).then_inc(s_pt_b, 1)

                def products_out(j):
                    act.wait_ge(s_pv, i * BU + (PV0 + TU * (j + 1)) + 1)
                    act.wait_ge(s_oT, i * TB + (j + 1))
                    act.activation(l2_raw.rearrange("p a c q -> p (a c q)"), bank(7), ACT.Copy).then_inc(s_o, 1)

                if i is None:
                    i = 0
                    exps(0)
                    exps(1)
                    return
                for u in range(BU):
                    evac(u)
                    if more or u + 2 < BU:
                        exps(u + 2)
                    if more and u == 2:
                        turn_evac(act, turns, xT)
                    if u == TU:
                        products_out(0)
                products_out(1)
                if more:
                    values_out(i + 1)

            turn_evac(act, turns, xT)
            values_out(0)
            batch(None, True)
            with act.Fori(0, B - 1) as i:
                turns.loop(i, 1)
                batch(i, True)
            turns.end_loop(B - 1)
            batch(B - 1, False)

        s_act_own = sem("l2_gate_set")

        def l2_attn_vector(dve, st):
            dve.wait_ge(s_l2_load, 16 * L2_LOADS)
            dve.wait_ge(s_act_own, 1)

            def normalise(b):
                ln_vector(dve, st, b, b + 4 * B)
                ln_apply(dve, b, b + 25)

            def multiply(b, a):
                if a == 0:
                    dve.wait_ge(s_l2_rot, b * 2 + 1)
                dve.wait_ge(s_l2_qk, b * 4 + a + 1)
                dve.scalar_tensor_tensor(out=l2_rot[:, a // 2, a % 2, :].rearrange("p (c s) -> p c s", c=C),
                                         in0=bank(0).rearrange("p (c s) -> p c s", c=C), scalar=HD2 ** -0.5 if a < 2 else 1.0,
                                         in1=(l2_cos, l2_sin)[a % 2].unsqueeze(1).to_broadcast([P, C, S]),
                                         op0=ALU.mult, op1=ALU.mult).then_inc(s_l2_mul, 1)

            def batch(i, more):
                def shift(u):
                    j, k = u % BU // TU, u % TU
                    if u % BU == 0:
                        dve.wait_ge(s_mask_ok, i + (u // BU + 1))
                    dve.wait_ge(s_score, i * BU + (U0 + u + 2))
                    dve.wait_ge(s_ptT_b, i * BU + (u + 1))
                    if u in (2, TU + 2, TU + 3):
                        dve.wait_ge(s_csum, i * TB * CROSS + (1 if u == 2 else u - TU))
                    if k < SELF:
                        settle(dve)
                        for g in range(QC):
                            st.mark(dve.tensor_tensor_reduce(out=l2_prob[:, u % LAG, g * S:(g + 1) * S],
                                                             in0=l2_sc[u % 2][:, g * S:(g + 1) * S], in1=l2_mask[:, j, :],
                                                             scale=1.0, scalar=float(np.finfo(np.float32).min),
                                                             op0=ALU.add, op1=ALU.max, accum_out=l2_max[:, u % LAG, g:g + 1]))
                        st.wait()
                        dve.tensor_scalar(l2_neg[:, u % LAG, :], l2_max[:, u % LAG, :], -1.0, None, ALU.mult).then_inc(s_shift, 1)
                    else:
                        heads = lambda v: v.rearrange("p (h k) -> p h k", k=SK)
                        st.done(dve.tensor_reduce(l2_cmax[:, u % LAG, :], heads(l2_sc[u % 2]), AX, ALU.max))
                        dve.tensor_tensor(heads(l2_prob[:, u % LAG, :]), heads(l2_sc[u % 2]),
                                          l2_cmax[:, u % LAG, :].unsqueeze(2).to_broadcast([P, H2 // 2, SK]), ALU.subtract).then_inc(s_shift, 1)

                def evac_second(u):
                    if u % TU < SELF:
                        dve.wait_ge(s_ptT_b, i * BU + (u + 1 + LAG))
                        dve.wait_ge(s_pv, i * BU + (PV0 + u))
                        dve.tensor_copy(l2_probT[:, u % 2, HALF:, :].rearrange("p g q -> p (g q)"), l2_pt_ps[1]).then_inc(s_pt_b, 1)

                def inverse_sums(j):
                    wide = lambda v: v[:, j, :].unsqueeze(2).to_broadcast([P, H2, HD2])
                    dve.wait_ge(s_exp, i * BU + (U0 + TU * (j + 1)))
                    dve.wait_ge(s_csum, i * TB * CROSS + (1 + CROSS * (j + 1)))
                    st.mark(dve.reciprocal(l2_sum[:, j, :], l2_sum[:, j, :]))
                    st.done(dve.reciprocal(l2_csum[:, j, :], l2_csum[:, j, :]))
                    st.done(dve.tensor_tensor(l2_csum[:, j, :], l2_csum[:, j, :], l2_gate, ALU.mult))
                    dve.wait_ge(s_repT, i * TB + (j + 1))
                    dve.tensor_copy(l2_rep[:, 0, :].rearrange("p (h d) -> p h d", h=H2), wide(l2_sum))
                    dve.tensor_copy(l2_rep[:, 1, :].rearrange("p (h d) -> p h d", h=H2), wide(l2_csum)).then_inc(s_rep, 1)

                def scale_products(j):
                    dve.wait_ge(s_o, i * TB + (O0 + j + 2))
                    dve.wait_ge(s_repT, i * TB + (j + 2))
                    st.done(dve.tensor_tensor(l2_raw.rearrange("p a c q -> p (a c q)"), l2_raw.rearrange("p a c q -> p (a c q)"),
                                              l2_repT_ps, ALU.mult))
                    dve.tensor_tensor(l2_oT[:, :, j * P:(j + 1) * P], l2_raw[:, 0, :, :], l2_raw[:, 1, :, :],
                                      ALU.add).then_inc(s_oT, 1)

                def add_result(j):
                    dve.wait_ge(s_y, i * TB + (V0 + j + 1))
                    dve.scalar_tensor_tensor(out=tile_of(x, i * TB + j), in0=l2_y_ps, scalar=gates[:, 4:5],
                                             in1=tile_of(x, i * TB + j), op0=ALU.mult, op1=ALU.add).then_inc(s_res, 1)

                if i is None:
                    i = 0
                    shift(0)
                    shift(1)
                    return
                for u in range(BU):
                    if more or u + 2 < BU:
                        shift(u + 2)
                    evac_second(u)
                    if more and u == 0:
                        normalise(i + 1)
                    if more and 4 <= u < 8:
                        multiply(i + 1, u - 4)
                    if u == TU:
                        inverse_sums(0)
                    if u == TU + 2:
                        scale_products(0)
                    if u == TU + 4:
                        add_result(0)
                inverse_sums(1)
                scale_products(1)
                add_result(1)

            normalise(0)
            for a in range(4):
                multiply(0, a)
            batch(None, True)
            with dve.Fori(0, B - 1) as i:
                st.loop(i, 4 + TB * (SELF * QC + CROSS + 4))
                batch(i, True)
            st.end_loop(B - 1)
            batch(B - 1, False)

        scratch.restart()
        ffn_region.restart()
        K2 = (I2 + P - 1) // P
        ROUND = 1.5 * 2.0 ** 23
        f2_gate = ffn_region.take([P, C * 2 * I2])
        f2_down = ffn_region.take([P, K2 * D])
        f2_gate_q = ffn_region.take([P, C, 2 * I2], BF16)
        f2_down_q = ffn_region.take([P, K2, D], BF16)
        f2_norm = scratch.take([P, D])
        f2_dnorm = scratch.take([P, I2])
        ident_b = scratch.take([P, P], BF16)
        ones_sq = scratch.take([P, P])
        w_sum = scratch.take([P, 2])
        w_mean = scratch.take([P, 2])
        w_scale = scratch.take([P, 2])
        f2_junk = scratch.take([P, TB, I2])
        row_ss = scratch.take([P, TB])
        row_rms = scratch.take([P, TB])
        row_max = scratch.take([P, TB])
        row_q = scratch.take([P, TB])
        row_y = scratch.take([P, TB])
        row_half = scratch.take([P, TB])
        row_sq = scratch.take([P, TB])
        hrow_ss = scratch.take([P, TB])
        hrow_rms = scratch.take([P, TB])
        hrow_max = scratch.take([P, TB])
        hrow_q = scratch.take([P, TB])
        hrow_y = scratch.take([P, TB])
        f2_xq = scratch.take([P, TB, D], BF16)
        f2_xqT = scratch.take([P, C, S], BF16)
        f2_act = scratch.take([P, TB, I2])
        f2_hq = scratch.take([P, TB, I2], BF16)
        f2_hqT = scratch.take([P, K2, P], BF16)

        s_f2_load = sem("f2_load")
        s_wsum = sem("weights_summed")
        s_wmean = sem("weight_sums_spread")
        s_row_ss = sem("row_squares_summed")
        s_row_ms = sem("row_mean_square_ready")
        s_row_rms = sem("row_rms_ready")
        s_row_norm = sem("rows_normalised")
        s_xq = sem("rows_quantised")
        s_h2 = sem("f2_hidden_ready")
        s_hq = sem("hidden_quantised")

        turn_b = bank(0).bitcast(BF16)
        hq_ps = bank(5).bitcast(BF16)

        def l2_ffn_sync(sp):
            sp.wait_ge(s_res, 4 * NT + 1)
            sp.dma_start(f2_gate, A["f2_gate"]).then_inc(s_f2_load, 16)
            sp.dma_start(f2_down, A["f2_down"]).then_inc(s_f2_load, 16)
            sp.dma_start(f2_norm, A["f2_norm"]).then_inc(s_f2_load, 16)
            sp.dma_start(f2_dnorm, A["f2_dnorm"]).then_inc(s_f2_load, 16)

        def l2_ffn_gpsimd(pool):
            pool.wait_ge(s_res, 4 * NT + 1)
            pool.memset(ones_sq, 1.0).then_inc(s_wsum, 1)
            with pool.Fori(0, B) as i:
                ln_gpsimd(pool, i + 5 * B)
                for k, rms_of in enumerate((row_rms, hrow_rms, hrow_rms)):
                    pool.wait_ge(s_row_ms, i * 3 + k + 1)
                    v = rms_of if k == 0 else rms_of[:, k - 1:k]
                    pool.tensor_tensor(v, v, minus_half[:, 0:v.shape[1]], ALU.pow).then_inc(s_row_rms, 1)

        def l2_ffn_tensor(pe, turns):
            pe.wait_ge(s_res, 5 * NT + 1)
            pe.wait_ge(s_wsum, 3)
            pe.matmul(bank(6)[:, 0:2], ones_sq, w_sum, start=True, stop=True).then_inc(s_wmean, 1)
            with pe.Fori(0, B) as i:
                turns.loop(i, 1)
                pe.wait_ge(s_xq, i + 2)
                pe.wait_ge(s_turn_out, turns.now())
                for c in range(C):
                    for j in range(TB):
                        ins = pe.transpose(turn_b[:, c * S + j * P:c * S + (j + 1) * P], f2_xq[:, j, c * P:(c + 1) * P], ident_b)
                ins.then_inc(s_turned, 1)
                turns.k += 1
                pe.wait_ge(s_turn_out, turns.now())
                for j in range(TB):
                    pe.wait_ge(s_h2, i * TB + j + 1)
                    for a, ps, ready in ((0, gate_ps, s_gate), (1, up_ps, s_up)):
                        for n0, n1 in ((0, BANK), (BANK, I2)):
                            for c in range(C):
                                ins = pe.matmul(ps[:, n0:n1], f2_xqT[:, c, j * P:(j + 1) * P],
                                                f2_gate_q[:, c, a * I2 + n0:a * I2 + n1], start=(c == 0), stop=(c == C - 1))
                        ins.then_inc(ready, 1)
                for j in range(TB):
                    pe.wait_ge(s_hq, i * TB + j + 1)
                    pe.wait_ge(s_ht, i * TB + (NT + j) + 1)
                    for k in range(K2):
                        w = min(P, I2 - k * P)
                        ins = pe.transpose(hq_ps[0:w, k * P:(k + 1) * P], f2_hq[:, j, k * P:k * P + w], ident_b)
                    ins.then_inc(s_htT, 1)
                    pe.wait_ge(s_ht, i * TB + (NT + j + 2))
                    pe.wait_ge(s_res, i * TB + (5 * NT + j) + 1)
                    for k in range(K2):
                        w = min(P, I2 - k * P)
                        ins = pe.matmul(y_ps, f2_hqT[0:w, k, :], f2_down_q[0:w, k, :], start=(k == 0), stop=(k == K2 - 1))
                    ins.then_inc(s_fy, 1)
            turns.end_loop(B)

        def l2_ffn_scalar(act, turns):
            act.wait_ge(s_f2_load, 64)
            act.wait_ge(s_res, 5 * NT + 1)
            act.activation(f2_gate_q.rearrange("p c n -> p (c n)"), f2_gate, ACT.Abs, accum_out=w_sum[:, 0:1])
            act.activation(f2_down_q.rearrange("p c n -> p (c n)"), f2_down, ACT.Abs, accum_out=w_sum[:, 1:2]).then_inc(s_wsum, 1)
            act.activation(ident_b, ident[:, :], ACT.Copy).then_inc(s_wsum, 1)
            with act.Fori(0, B) as i:
                turns.loop(i, 1)
                act.wait_ge(s_ln_norm, i + 5 * B + 1)
                act.wait_ge(s_xq, i + 1)
                for j in range(TB):
                    ins = act.activation(f2_junk[:, j, 0:D], xn[:, j, :], ACT.Square, accum_out=row_ss[:, j:j + 1])
                ins.then_inc(s_row_ss, 1)
                act.wait_ge(s_turned, turns.now() + 1)
                act.activation(f2_xqT.rearrange("p c s -> p (c s)"), turn_b[:, 0:C * S], ACT.Copy).then_inc(s_turn_out, 1)
                turns.k += 1
                for j in range(TB):
                    act.wait_ge(s_gate, i * TB + (NT + j + 1))
                    act.activation(f2_act[:, j, :], gate_ps[:, 0:I2], ACT.Tanh, scale=row_half[:, j:j + 1]).then_inc(s_act, 1)
                    act.wait_ge(s_h2, i * TB + j + 2)
                    act.activation(f2_junk[:, j, :], f2_act[:, j, :], ACT.Square, accum_out=hrow_ss[:, j:j + 1]).then_inc(s_row_ss, 1)
                for j in range(TB):
                    act.wait_ge(s_htT, i * TB + (NT + j + 2))
                    act.wait_ge(s_fy, i * TB + (NT + j) + 1)
                    act.activation(f2_hqT[:, 0:K2 - 1, :].rearrange("p k q -> p (k q)"), hq_ps[:, 0:(K2 - 1) * P], ACT.Copy)
                    act.activation(f2_hqT[0:I2 % P, K2 - 1, :], hq_ps[0:I2 % P, (K2 - 1) * P:K2 * P], ACT.Copy).then_inc(s_ht, 1)
            turns.end_loop(B)

        def quantise(dve, st, v, whole, scales, low, high):
            for j, scale in enumerate(scales):
                st.mark(dve.tensor_scalar(v[j], v[j], scale, ROUND, ALU.mult, ALU.add))
            st.wait()
            for j in range(len(scales)):
                st.mark(dve.tensor_scalar(v[j], v[j], ROUND, high, ALU.subtract, ALU.min))
            st.wait()
            return [dve.tensor_scalar(whole[j], v[j], low, None, ALU.max) for j in range(len(scales))][-1]

        def l2_ffn_vector(dve, st):
            dve.wait_ge(s_wmean, 1)
            sizes = (2 * I2 * D, I2 * D)
            for k in range(2):
                st.mark(dve.tensor_scalar(w_mean[:, k:k + 1], bank(6)[:, k:k + 1], 1.0 / sizes[k], 1e-5, ALU.mult, ALU.max))
            st.wait()
            st.done(dve.reciprocal(w_scale, w_mean))
            quantise(dve, st, [f2_gate, f2_down], [f2_gate_q.rearrange("p c n -> p (c n)"), f2_down_q.rearrange("p c n -> p (c n)")],
                     [w_scale[:, 0:1], w_scale[:, 1:2]], -1.0, 1.0).then_inc(s_xq, 1)
            with dve.Fori(0, B) as i:
                st.loop(i, 4 + 9 + 4 + TB * 10)
                ln_vector(dve, st, i, i + 5 * B)
                ln_apply(dve, i, i + 29)
                dve.wait_ge(s_row_ss, i * 3 + 1)
                dve.tensor_scalar(row_rms, row_ss, 1.0 / D, 1e-5, ALU.mult, ALU.add).then_inc(s_row_ms, 1)
                dve.wait_ge(s_row_rms, i * 3 + 1)
                for j in range(TB):
                    st.mark(dve.scalar_tensor_tensor(out=xn[:, j, :], in0=xn[:, j, :], scalar=row_rms[:, j:j + 1],
                                                     in1=f2_norm, op0=ALU.mult, op1=ALU.mult))
                st.wait()
                st.done(dve.tensor_reduce(row_max, xn[:, :, :], AX, ALU.max, apply_absolute_value=True))
                st.done(dve.tensor_scalar(row_max, row_max, 1e-5, None, ALU.max))
                st.mark(dve.reciprocal(row_q, row_max))
                st.done(dve.tensor_scalar(row_y, row_max, 1.0 / 127.0, w_mean[:, 0:1], ALU.mult, ALU.mult))
                st.mark(dve.tensor_scalar(row_q, row_q, 127.0, None, ALU.mult))
                st.mark(dve.tensor_scalar(row_half, row_y, 0.5, None, ALU.mult))
                st.done(dve.scalar_tensor_tensor(out=row_sq, in0=row_y, scalar=0.5, in1=row_y, op0=ALU.mult, op1=ALU.mult))
                quantise(dve, st, [xn[:, j, :] for j in range(TB)], [f2_xq[:, j, :] for j in range(TB)],
                         [row_q[:, j:j + 1] for j in range(TB)], -128.0, 127.0).then_inc(s_xq, 1)
                for j in range(TB):
                    h = f2_act[:, j, :]
                    dve.wait_ge(s_act, i * TB + (NT + j + 1))
                    st.done(dve.scalar_tensor_tensor(out=h, in0=h, scalar=1.0, in1=gate_ps[:, 0:I2], op0=ALU.add, op1=ALU.mult))
                    dve.wait_ge(s_up, i * TB + (NT + j + 1))
                    dve.scalar_tensor_tensor(out=h, in0=h, scalar=row_sq[:, j:j + 1], in1=up_ps[:, 0:I2],
                                             op0=ALU.mult, op1=ALU.mult).then_inc(s_h2, 1)
                    dve.wait_ge(s_row_ss, i * 3 + j + 2)
                    dve.tensor_scalar(hrow_rms[:, j:j + 1], hrow_ss[:, j:j + 1], 1.0 / I2, 1e-5, ALU.mult, ALU.add).then_inc(s_row_ms, 1)
                    dve.wait_ge(s_row_rms, i * 3 + j + 2)
                    st.done(dve.scalar_tensor_tensor(out=h, in0=h, scalar=hrow_rms[:, j:j + 1], in1=f2_dnorm,
                                                     op0=ALU.mult, op1=ALU.mult))
                    top1, q1, y1 = hrow_max[:, j:j + 1], hrow_q[:, j:j + 1], hrow_y[:, j:j + 1]
                    st.done(dve.tensor_reduce(top1, h, AX, ALU.max, apply_absolute_value=True))
                    st.done(dve.tensor_scalar(top1, top1, 1e-5, None, ALU.max))
                    st.mark(dve.reciprocal(q1, top1))
                    st.done(dve.tensor_scalar(y1, top1, 1.0 / 127.0, w_mean[:, 1:2], ALU.mult, ALU.mult))
                    st.mark(dve.tensor_scalar(y1, y1, gates[:, 5:6], None, ALU.mult))
                    st.done(dve.tensor_scalar(q1, q1, 127.0, None, ALU.mult))
                    quantise(dve, st, [h], [f2_hq[:, j, :]], [q1], -128.0, 127.0).then_inc(s_hq, 1)
                for j in range(TB):
                    dve.wait_ge(s_fy, i * TB + (NT + j + 2))
                    dve.scalar_tensor_tensor(out=tile_of(x, i * TB + j), in0=y_ps, scalar=hrow_y[:, j:j + 1],
                                             in1=tile_of(x, i * TB + j), op0=ALU.mult, op1=ALU.add).then_inc(s_res, 1)
            st.end_loop(B)

        scratch.restart()
        attn_region.restart()
        l3_w = attn_region.take([P, 2, C, D])
        l3_in_bias = attn_region.take([P, C])
        l3_out_bias = attn_region.take([1, D])
        l3_affine = attn_region.take([P, 2, D])
        l3_decay = attn_region.take([P, 1])
        l3_decays = attn_region.take([P, SK])
        l3_in = attn_region.take([P, C, CT])
        l3_state = attn_region.take([P, C, CT])
        l3_mean = attn_region.take([P, C, B])
        l3_mean_wide = attn_region.take([P, C, B, P])
        l3_summary = attn_region.take([P, B, D])
        l3_y = attn_region.take([P, TB, D])

        s_l3_load = sem("l3_load")
        s_l3_in = sem("l3_context_projected")
        s_l3_in_out = sem("l3_context_out")
        s_l3_mean = sem("l3_means_ready")
        s_l3_sum = sem("l3_summary_ready")
        s_l3_sum_out = sem("l3_summary_out")

        def l3_attn_sync(sp):
            sp.wait_ge(s_res, 5 * NT + 1)
            for dst, name in ((l3_w, "l3_w"), (l3_in_bias, "l3_in_bias"), (l3_out_bias, "l3_out_bias"),
                              (l3_affine, "l3_affine"), (l3_decay, "l3_decay")):
                sp.dma_start(dst, A[name]).then_inc(s_l3_load, 16)

        def l3_attn_gpsimd(pool):
            with pool.Fori(0, B) as i:
                ln_gpsimd(pool, i * 2 + 6 * B)
                ln_gpsimd(pool, i * 2 + (6 * B + 1))

        def l3_attn_tensor(pe, turns):
            pe.wait_ge(s_l3_load, 16 * 5)
            for m in range(C):
                for c in range(C):
                    ins = pe.matmul(bank(1)[:, m * CT:(m + 1) * CT], l3_w[:, 0, c, m * P:(m + 1) * P], ctxT[:, c, :],
                                    start=(c == 0), stop=(c == C - 1))
            ins.then_inc(s_l3_in, 1)
            pe.wait_ge(s_l3_mean, 1)
            for b in range(B):
                ps = bank(2, 2)[:, b * D:(b + 1) * D]
                pe.matmul(ps, ones[:, :], l3_out_bias, start=True, stop=False)
                for c in range(C):
                    ins = pe.matmul(ps, l3_mean_wide[:, c, b, :], l3_w[:, 1, c, :], start=False, stop=(c == C - 1))
            ins.then_inc(s_l3_sum, 1)

        def l3_attn_scalar(act, turns):
            act.wait_ge(s_l3_load, 16 * 5)
            act.activation(l3_decay, l3_decay, ACT.Tanh, scale=0.5).then_inc(s_l3_in_out, 1)
            act.wait_ge(s_l3_in, 1)
            for c in range(C):
                ins = act.activation(l3_in[:, c, :], bank(1)[:, c * CT:(c + 1) * CT], ACT.Identity, bias=l3_in_bias[:, c:c + 1])
            ins.then_inc(s_l3_in_out, 1)
            act.wait_ge(s_l3_sum, 1)
            act.activation(flat(l3_summary), bank(2, 2), ACT.Copy).then_inc(s_l3_sum_out, 1)

        def l3_attn_vector(dve, st):
            dve.wait_ge(s_l3_in_out, 2)
            st.done(dve.tensor_scalar(l3_decay, l3_decay, 1.0, 0.5, ALU.add, ALU.mult))
            st.done(dve.tensor_copy(l3_decays, l3_decay.to_broadcast([P, SK])))
            for c in range(C):
                for b in range(B):
                    at = slice(b * SK, (b + 1) * SK)
                    st.mark(dve.tensor_tensor_scan(l3_state[:, c, at], l3_decays, l3_in[:, c, at], 0.0, ALU.mult, ALU.add))
            st.wait()
            st.done(dve.tensor_reduce(l3_mean, l3_state.rearrange("p c (b k) -> p c b k", b=B), AX, ALU.add))
            st.done(dve.tensor_scalar(l3_mean, l3_mean, 1.0 / SK, None, ALU.mult))
            dve.tensor_copy(l3_mean_wide, l3_mean.unsqueeze(3).to_broadcast([P, C, B, P])).then_inc(s_l3_mean, 1)
            dve.wait_ge(s_l3_sum_out, 1)
            with dve.Fori(0, B) as i:
                st.loop(i, 4 + 2 + 1 + 4 + 2 + 2)
                ln_vector(dve, st, i, i * 2 + 6 * B)
                for j in range(TB):
                    st.mark(dve.tensor_scalar(l3_y[:, j, :], tile_of(x, i * TB + j), ln_mv[:, j, 0:1], ln_rstd[:, j, :],
                                              ALU.subtract, ALU.mult))
                st.wait()
                st.done(dve.tensor_tensor(l3_y, l3_y, l3_summary[:, bass.ds(i, 1), :].to_broadcast([P, TB, D]), ALU.add))
                for j in range(TB):
                    st.mark(dve.bn_stats(ln_stats[:, j, :], l3_y[:, j, :]))
                st.wait()
                settle(dve)
                for j in range(TB):
                    st.mark(dve.bn_aggr(ln_mv[:, j, :], ln_stats[:, j, :]))
                st.wait()
                dve.tensor_scalar(ln_mv[:, :, 1:2], ln_mv[:, :, 1:2], 1e-5, None, ALU.add).then_inc(s_ln_var, 1)
                dve.wait_ge(s_ln_rstd, i * 2 + (6 * B + 2))
                for j in range(TB):
                    st.mark(dve.tensor_scalar(l3_y[:, j, :], l3_y[:, j, :], ln_mv[:, j, 0:1], ln_rstd[:, j, :],
                                              ALU.subtract, ALU.mult))
                st.wait()
                for k, op in enumerate((ALU.mult, ALU.add)):
                    st.done(dve.tensor_tensor(l3_y, l3_y, l3_affine[:, k:k + 1, :].to_broadcast([P, TB, D]), op))
                for j in range(TB):
                    dve.scalar_tensor_tensor(out=tile_of(x, i * TB + j), in0=l3_y[:, j, :], scalar=gates[:, 6:7],
                                             in1=tile_of(x, i * TB + j), op0=ALU.mult, op1=ALU.add).then_inc(s_res, 1)
                dve.wait_ge(s_res, i * TB + (6 * NT + TB) + 1)
            st.end_loop(B)

        scratch.restart()
        scratch.at = moe_mark
        ffn_region.restart()
        f3_expert_w = ffn_region.take([P, SLOTS, 3 * D])
        EZ = E3 + Z3
        f3_router = scratch.take([P, C, EZ])
        f3_bias = scratch.take([P, EZ])
        earlier = scratch.take([P, P])
        all_ones = scratch.take([P, P])
        c_prob = scratch.take([P, TB, EZ])
        c_biased = scratch.take([P, TB, EZ])
        c_rest = scratch.take([P, TB, EZ])
        c_eight = scratch.take([P, TB, 8])
        c_sum = scratch.take([P, TB, 1])
        c_idle = scratch.take([P, TB, 1])
        taken = scratch.take([P, TB, E3])
        taken_before = scratch.take([P, E3])
        c_keep = scratch.take([P, TB, E3])

        s_f3_load = sem("f3_load")
        s_taken = sem("experts_taken")
        s_place = sem("places_counted")
        place_ps = bank(7)[:, 0:TB * E3].rearrange("p (j e) -> p j e", j=TB)

        def l3_ffn_sync(sp):
            sp.wait_ge(s_res, 7 * NT + 1)
            for dst, name in ((f3_router, "f3_router"), (f3_bias, "f3_bias"), (earlier, "earlier")):
                sp.dma_start(dst, A[name]).then_inc(s_f3_load, 16)
            experts_sync(sp, "f3_experts", E3, 0, 2 * (E1 + 1))

        def l3_ffn_gpsimd(pool):
            pool.wait_ge(s_res, 7 * NT + 1)
            pool.memset(all_ones, 1.0).then_inc(s_const, 1)
            router_gpsimd(pool, 8 * B, 33, B)

        def l3_ffn_scalar(act, turns):
            router_scalar(act, turns, B, c_prob)
            experts_scalar(act, E3, 2 * (E1 + 1))

        def l3_ffn_tensor(pe, turns):
            pe.wait_ge(s_f3_load, 48)
            pe.wait_ge(s_const, 4)
            with pe.Fori(0, B) as i:
                turns.loop(i, 1)
                pe.wait_ge(s_ln_norm, i + 6 * B + 1)
                turn_batch(pe, turns, xn)
                pe.wait_ge(s_turn_out, turns.now())
                pe.wait_ge(s_rshift, i + B + 1)
                for j in range(TB):
                    for c in range(C):
                        ins = pe.matmul(logit_ps[:, j * EZ:(j + 1) * EZ], xT[:, c, j * P:(j + 1) * P], f3_router[:, c, :],
                                        start=(c == 0), stop=(c == C - 1))
                ins.then_inc(s_logit, 1)
                for j in range(TB):
                    pe.wait_ge(s_taken, i * TB + j + 1)
                    pe.matmul(place_ps[:, j, :], all_ones, taken_before, start=True, stop=False)
                    pe.matmul(place_ps[:, j, :], earlier, taken[:, j, :], start=False, stop=True).then_inc(s_place, 1)
            turns.end_loop(B)
            pe.wait_ge(s_xall, 2 * B + 1)
            pe.wait_ge(s_rshift, 2 * B + 1)
            experts_tensor(pe, E3, [5, 4, 4, 4], 2 * (E1 + 1))

        def l3_ffn_vector(dve, st):
            dve.wait_ge(s_f3_load, 48)
            st.done(dve.memset(taken_before, 0.0))
            with dve.Fori(0, B) as i:
                st.loop(i, 4 + 4 + 5 + 8 + 2 * TB + 1)
                ln_vector(dve, st, i, i + 8 * B)
                ln_apply(dve, i, i + 33)
                spread = lambda v, n: v.to_broadcast([P, TB, n])
                router_softmax(dve, st, i, B, c_prob, EZ)
                st.mark(dve.tensor_tensor(c_biased, c_prob, f3_bias.unsqueeze(1).to_broadcast([P, TB, EZ]), ALU.add))
                st.wait()
                settle(dve)
                for j in range(TB):
                    st.mark(dve.max(c_eight[:, j, :], c_biased[:, j, :]))
                st.wait()
                settle(dve)
                for j in range(TB):
                    st.mark(dve.match_replace(out=c_rest[:, j, :], in_to_replace=c_eight[:, j, :],
                                              in_values=c_biased[:, j, :], imm_value=-3e38))
                st.wait()
                st.done(dve.tensor_tensor(c_rest, c_rest, c_biased, ALU.not_equal))
                st.done(dve.tensor_copy(taken, c_rest[:, :, 0:E3]))
                st.done(dve.tensor_tensor(c_rest, c_rest, c_prob, ALU.mult))
                st.done(dve.tensor_reduce(c_sum[:, :, 0], c_rest, AX, ALU.add))
                st.done(dve.tensor_scalar(c_sum, c_sum, 1e-20, None, ALU.add))
                st.done(dve.reciprocal(c_sum, c_sum))
                st.done(dve.scalar_tensor_tensor(out=c_rest, in0=c_rest, scalar=1.5, in1=spread(c_sum, EZ),
                                                 op0=ALU.mult, op1=ALU.mult))
                st.mark(dve.tensor_reduce(c_idle[:, :, 0], c_rest[:, :, E3:EZ], AX, ALU.add))
                for j in range(TB):
                    st.wait()
                    settle(dve)
                    dve.engine_nop().then_inc(s_taken, 1)
                    dve.wait_ge(s_place, i * TB + j + 1)
                    st.mark(dve.tensor_tensor(taken_before, taken_before, taken[:, j, :], ALU.add))
                    st.done(dve.tensor_scalar(c_keep[:, j, :], place_ps[:, j, :], float(CAP3), None, ALU.is_lt))
                st.done(dve.tensor_tensor(c_keep, c_keep, c_rest[:, :, 0:E3], ALU.mult))
                dve.scalar_tensor_tensor(out=weight_of[:, bass.ds(i * TB, TB), 0:E3], in0=spread(c_idle, E3), scalar=1.0,
                                         in1=c_keep, op0=ALU.add, op1=ALU.mult).then_inc(s_weighed, 1)
            st.end_loop(B)
            dve.wait_ge(s_weighed, B)
            st.done(dve.tensor_scalar(weight_of[:, :, 0:E3], weight_of[:, :, 0:E3], gates[:, 7:8], None, ALU.mult))
            experts_vector(dve, st, E3, 2 * (E1 + 1))

        s_weighed = sem("tokens_weighed")

        stage_list = [
            dict(sync=l0_attn_sync, gpsimd=l0_attn_gpsimd, scalar=l0_attn_scalar, vector=l0_attn_vector, tensor=l0_attn_tensor),
            dict(sync=l0_ffn_sync, gpsimd=l0_ffn_gpsimd, scalar=l0_ffn_scalar, vector=l0_ffn_vector, tensor=l0_ffn_tensor),
            dict(sync=l1_attn_sync, gpsimd=l1_attn_gpsimd, scalar=l1_attn_scalar, vector=l1_attn_vector, tensor=l1_attn_tensor),
            dict(sync=l1_ffn_sync, gpsimd=l1_ffn_gpsimd, scalar=l1_ffn_scalar, vector=l1_ffn_vector, tensor=l1_ffn_tensor),
            dict(sync=l2_attn_sync, gpsimd=l2_attn_gpsimd, scalar=l2_attn_scalar, vector=l2_attn_vector, tensor=l2_attn_tensor),
            dict(sync=l2_ffn_sync, gpsimd=l2_ffn_gpsimd, scalar=l2_ffn_scalar, vector=l2_ffn_vector, tensor=l2_ffn_tensor),
            dict(sync=l3_attn_sync, gpsimd=l3_attn_gpsimd, scalar=l3_attn_scalar, vector=l3_attn_vector, tensor=l3_attn_tensor),
            dict(sync=l3_ffn_sync, gpsimd=l3_ffn_gpsimd, scalar=l3_ffn_scalar, vector=l3_ffn_vector, tensor=l3_ffn_tensor),
        ]

        block = ctx.enter_context(nc.Block())

        @block.sync
        def _(sp):
            sp.dma_start(gates[:, :], A["gates"]).then_inc(s_load, 16)
            sp.dma_start(ident[:, :], A["ident"]).then_inc(s_load, 16)
            sp.dma_start(x[:, :, :], A["x"]).then_inc(s_load, 16)
            for n, stage in enumerate(stage_list[:stages]):
                stage["sync"](sp)
            sp.wait_ge(s_res, stages * NT + 1)
            sp.dma_start(out, x[:, :, :]).then_inc(s_store, 16)
            sp.wait_ge(s_store, 16)

        @block.gpsimd
        def _(pool):
            for signal in (s_shift, s_pt, s_o, s_res, s_pv, s_score, s_ptT, s_hid, s_ht, s_kept, s_fy, s_htT, s_qrT,
                           s_rshift, s_logit, s_xall, s_l2_rot, s_h2):
                pool.sem_inc(signal, 1)
            pool.memset(ones[:, :], 1.0).then_inc(s_const, 1)
            pool.memset(minus_half[:, :], -0.5).then_inc(s_const, 1)
            pool.wait_ge(s_const, 2)
            for stage in stage_list[:stages]:
                stage["gpsimd"](pool)

        @block.scalar
        def _(act):
            turns = Tally(s_turned)
            act.wait_ge(s_load, 48)
            act.activation(gates[:, :], gates[:, :], ACT.Tanh).then_inc(s_const, 1)
            for stage in stage_list[:stages]:
                stage["scalar"](act, turns)

        @block.vector
        def _(dve):
            st = Steps(dve, s_dve)
            dve.wait_ge(s_load, 48)
            dve.wait_ge(s_const, 3)
            for n, stage in enumerate(stage_list[:stages]):
                stage["vector"](dve, st)
                dve.wait_ge(s_res, (n + 1) * NT + 1)

        @block.tensor
        def _(pe):
            turns = Tally(s_turned)
            pe.wait_ge(s_load, 48)
            for stage in stage_list[:stages]:
                stage["tensor"](pe, turns)


def laid_out(inp):
    f = np.float32

    def chunks(w):
        return w.reshape(-1, P, w.shape[-1]).transpose(1, 0, 2)

    def rows(v):
        return np.broadcast_to(v.reshape(1, -1), (P, v.size))

    a = {}
    a["x"] = inp["x"].reshape(NT, P, D).transpose(1, 0, 2)
    a["gates"] = rows(np.stack([inp["g_xattn"], inp["g_ffn"]], axis=1).reshape(-1))
    a["ident"] = np.eye(P, dtype=f)
    context = inp["ctx_2048"].reshape(CT, D).T
    a["ctxT"] = chunks(context)
    a["ctxT2"] = np.repeat(chunks(context).reshape(P, C, B, 1, SK), 2, axis=3).reshape(P, C, B, P)
    a["l0_w"] = np.stack([chunks(inp["L0_xattn_" + k]) for k in ("Wq", "Wk_img", "Wv_img", "Wo")], axis=1)
    a["l0_rows"] = np.stack([inp["L0_xattn_" + k] for k in ("bq", "bk_img", "bv_img", "bo")])[None]
    a["l0_gain"] = np.stack([rows(inp["L0_xattn_" + k]) for k in ("gq", "gk_img")], axis=1)
    a["head_of"] = np.repeat(np.eye(HB0, dtype=f), HD0, axis=0)
    a["half_of"] = np.repeat(np.eye(2, dtype=f), SK, axis=0)
    a["f0_w"] = np.stack([chunks(inp["L0_ffn_w_gate"]), chunks(inp["L0_ffn_w_up"])], axis=1)
    a["f0_down"] = chunks(inp["L0_ffn_w_down"])
    a["l1_kvc"] = chunks(inp["L1_xattn_W_kvc"])
    a["l1_dq"] = chunks(inp["L1_xattn_W_dq"])
    a["l1_uqT"] = inp["L1_xattn_W_uq"].reshape(QC1, H1, HD1).transpose(2, 1, 0)
    swap = (np.arange(R1) + R1 // 2) % R1
    qr = inp["L1_xattn_W_qr"].reshape(QC1, H1, R1)
    a["l1_qr"] = np.stack([qr, qr[:, :, swap]], axis=1).reshape(QC1, 2, H1 * R1)
    a["l1_uk"] = inp["L1_xattn_W_uk"]
    kr = inp["L1_xattn_W_kr"]
    a["l1_kr"] = np.stack([np.concatenate([w, w], axis=1) for w in (kr, kr[:, swap])], axis=1)
    a["l1_uv"] = inp["L1_xattn_W_uv"]
    a["l1_wo"] = inp["L1_xattn_W_o"].reshape(H1, HD1, D).transpose(1, 0, 2)
    a["seg"] = inp["itok_BxS_0_1023"].reshape(NT, P).T
    half = R1 // 2
    angle = np.arange(S, dtype=f)[:, None] * (f(1.0) / f(10000.0) ** (np.arange(half, dtype=f) / f(half)))
    a["l1_cos"] = np.tile(np.cos(angle).T, (4, 1)).astype(f)
    a["l1_sin"] = np.tile(np.concatenate([-np.sin(angle).T, np.sin(angle).T]), (2, 1)).astype(f)
    a["key_at"] = rows(np.arange(SK, dtype=f))
    a["key_last"] = rows(np.arange(SK, dtype=f) + f(LOOKBACK))

    def experts(gate, up, down):
        n = gate.shape[0]
        gu = np.stack([gate.reshape(n, C, P, I1), up.reshape(n, C, P, I1)], axis=3)
        return np.concatenate([gu.transpose(0, 2, 1, 3, 4).reshape(n, P, 2 * D), down], axis=2)

    a["f1_experts"] = experts(*(np.concatenate([inp["L1_ffn_" + k], inp["L1_ffn_s" + k][None]]) for k in ("Wg", "Wu", "Wd")))
    a["f1_router"] = chunks(inp["L1_ffn_Wr"].T)
    a["f1_bias"] = inp["L1_ffn_bias"].reshape(1, E1)
    a["below"] = rows(-np.arange(1, 9, dtype=f))
    swap = (np.arange(HD2) + HD2 // 2) % HD2
    swapped = lambda w: w.reshape(D, H2, HD2)[:, :, swap].reshape(D, D)
    wq, wk, wv, wo = (inp["L2_xattn_" + k] for k in ("Wq", "Wk", "Wv", "Wo"))
    a["l2_w"] = np.stack([chunks(w) for w in (wq, swapped(wq), wk, swapped(wk), wv, wo)], axis=1)
    freqs = np.outer(np.arange(S, dtype=f), f(1.0) / f(10000.0) ** (np.arange(0, HD2, 2, dtype=f) / f(HD2)))
    a["l2_cos"] = np.tile(np.cos(freqs).T, (P // HD2 * 2, 1)).astype(f)
    a["l2_sin"] = np.tile(np.concatenate([-np.sin(freqs).T, np.sin(freqs).T]), (P // HD2, 1)).astype(f)
    a["eight_of"] = np.tile(np.repeat(np.eye(8, dtype=f).reshape(8, 2, 4).transpose(0, 2, 1), HD2, axis=0), (2, 1, 1))
    a["l2_gate"] = rows(inp["L2_xattn_gate"].reshape(-1))
    a["mask"] = inp["mask_Bx1xSxS_fk0"].reshape(NT, P, S).transpose(1, 0, 2)
    a["l2_head_of"] = np.repeat(np.eye(P // HD2, dtype=f), HD2, axis=0)
    a["f2_gate"] = chunks(inp["L2_ffn_gate_w"].T).reshape(P, -1)
    down = np.zeros((-(-I2 // P) * P, D), f)
    down[:I2] = inp["L2_ffn_down_w"].T
    a["f2_down"] = chunks(down).reshape(P, -1)
    a["f2_norm"] = rows(inp["L2_ffn_gate_norm_w"])
    a["f2_dnorm"] = rows(inp["L2_ffn_down_norm_w"])
    a["l3_w"] = np.stack([chunks(inp["L3_xattn_" + k].T) for k in ("W_in", "W_out")], axis=1)
    a["l3_in_bias"] = inp["L3_xattn_b_in"].reshape(C, P).T
    a["l3_out_bias"] = inp["L3_xattn_b_out"].reshape(1, D)
    a["l3_affine"] = np.stack([rows(inp["L3_xattn_" + k]) for k in ("gamma", "beta")], axis=1)
    a["l3_decay"] = rows(inp["L3_xattn_decay"].reshape(1))
    gu = inp["L3_ffn_w_gate_up"]
    a["f3_experts"] = experts(gu[:, :, :I3], gu[:, :, I3:], inp["L3_ffn_w_down"])
    a["f3_router"] = chunks(inp["L3_ffn_w_cls"].T)
    a["f3_bias"] = rows(inp["L3_ffn_bias"])
    a["earlier"] = np.triu(np.ones((P, P), f), 1)
    return {k: np.ascontiguousarray(v) for k, v in a.items()}


def kernel(**inputs):
    from concourse import bacc
    from concourse.bass_utils import run_bass_kernel_spmd

    nc = bacc.Bacc("TRN2", target_bir_lowering=False, num_devices=1)
    arrays = laid_out({k: np.asarray(v) for k, v in inputs.items()})
    A = {k: nc.dram_tensor(f"in_{k}_dram", v.shape, mybir.dt.from_np(v.dtype), kind="ExternalInput").ap()
         for k, v in arrays.items()}
    out = nc.dram_tensor("out_0_dram", (P, NT, D), F32, kind="ExternalOutput").ap()
    flamingo(nc, A, out)
    r = run_bass_kernel_spmd(nc, [{f"in_{k}_dram": v for k, v in arrays.items()}], core_ids=[0])
    return r.results[0]["out_0_dram"].transpose(1, 0, 2).reshape(B, S, D)
```

```python
from contextlib import ExitStack

import numpy as np

import concourse.bass as bass
from concourse import mybir

F32 = mybir.dt.float32
BF16 = mybir.dt.bfloat16
I32 = mybir.dt.int32
ALU = mybir.AluOpType
ACT = mybir.ActivationFunctionType
AX = mybir.AxisListType.X

P = 128
D = 256
C = D // P
B = 4
S = 256
TB = S // P
NT = B * TB
T = B * S
SK = 64
CT = B * SK
BANK = 512

H0, HD0 = 16, 16
HB0 = P // HD0
I0 = 1024
H1, HD1, R1, QC1, KC1 = 16, 128, 64, 96, 64
LOOKBACK = 8
I1, E1 = 128, 16
H2, HD2 = 32, 8
I2 = 704
I3, E3, Z3, TOP3, CAP3 = 128, 32, 32, 8, 128


class Tally:

    def __init__(self, sem):
        self.sem, self.base, self.k, self.i, self.per = sem, 0, 0, 0, 0

    def loop(self, i, per):
        self.base += self.k
        self.k, self.i, self.per = 0, i, per

    def end_loop(self, trips):
        assert self.k == self.per, (self.sem, self.k, self.per)
        self.base += trips * self.per
        self.k, self.i, self.per = 0, 0, 0

    def now(self):
        return self.i * self.per + (self.base + self.k)


class Steps(Tally):

    def __init__(self, eng, sem):
        super().__init__(sem)
        self.eng = eng

    def mark(self, ins):
        self.k += 1
        return ins.then_inc(self.sem, 1)

    def wait(self):
        self.eng.wait_ge(self.sem, self.now())

    def done(self, ins):
        self.mark(ins)
        self.wait()


def tile_of(x, t):
    return x[:, bass.ds(t, 1), :].rearrange("p a n -> p (a n)")


def flat(x):
    return x.rearrange("p a n -> p (a n)")


class Region:

    def __init__(self, tensor):
        self.tensor, self.at = tensor, 0

    def restart(self):
        self.at = 0

    def take(self, shape, dt=F32):
        n = int(np.prod(shape[1:]))
        words = n if dt != BF16 else (n + 1) // 2
        v = self.tensor[0:shape[0], self.at:self.at + words]
        self.at += words
        assert self.at <= self.tensor.shape[1], (self.at, self.tensor.shape)
        if dt != F32:
            v = v.bitcast(dt)
        if len(shape) == 2:
            return v
        axes = [f"d{k}" for k in range(len(shape) - 1)]
        return v.rearrange(f"p ({' '.join(axes)}) -> p {' '.join(axes)}", **dict(zip(axes[1:], shape[2:])))


def flamingo(nc, A, out):
    ctx = ExitStack()
    with ctx:
        def sb(name, shape, dt=F32):
            return ctx.enter_context(nc.sbuf_tensor(name, shape, dt))

        def sem(name):
            return ctx.enter_context(nc.semaphore(name))

        psum = ctx.enter_context(nc.psum_tensor("psum", [P, 8, BANK], F32))

        def bank(i, n=1):
            return psum[:, i:i + n, :].rearrange("p a n -> p (a n)")

        x = sb("x", [P, NT, D])
        xn = sb("xn", [P, TB, D])
        xT = sb("xT", [P, C, S])
        ident = sb("ident", [P, P])
        ones = sb("ones", [1, P])
        gates = sb("gates", [P, 8])
        minus_half = sb("minus_half", [P, 8])
        ln_stats = sb("ln_stats", [P, TB, 6])
        ln_mv = sb("ln_mv", [P, TB, 2])
        ln_rstd = sb("ln_rstd", [P, TB, 1])
        ctxT = sb("ctxT", [P, C, CT])

        prob = sb("prob", [P, 1024])
        probT = sb("probT", [P, 8, P])
        scratch = Region(sb("scratch", [P, 11264]))
        attn_region = Region(sb("attn_region", [P, 24704]))
        ffn_region = Region(sb("ffn_region", [P, 6912]))

        turn = bank(0).rearrange("p (c s) -> p c s", c=C)

        s_load = sem("constants_loaded")
        s_x_load = sem("x_loaded")
        s_const = sem("const_set")
        s_gates = sem("gates_set")
        s_dve = sem("vector_step")
        s_pool = sem("gpsimd_step")
        s_act = sem("scalar_step")
        s_ln_var = sem("ln_var_ready")
        s_ln_rstd = sem("ln_rstd_ready")
        s_ln_norm = sem("ln_norm_ready")
        s_turned = sem("turned")
        s_turn_out = sem("turn_out")
        s_store = sem("store_out")

        def settle(eng):
            eng.sem_inc(s_settled, 1)

        s_settled = sem("settled")

        def ln_moments(dve, st, i):
            for j in range(TB):
                st.mark(dve.bn_stats(ln_stats[:, j, :], tile_of(x, i * TB + j)))
            st.wait()
            settle(dve)
            for j in range(TB):
                st.mark(dve.bn_aggr(ln_mv[:, j, :], ln_stats[:, j, :]))
            st.wait()
            dve.tensor_scalar(ln_mv[:, :, 1:2], ln_mv[:, :, 1:2], 1e-5, None, ALU.add).then_inc(s_ln_var, 1)

        def ln_vector(dve, st, i, n):
            ln_moments(dve, st, i)
            dve.wait_ge(s_ln_rstd, n + 1)

        def ln_apply(dve, i, turned_before):
            dve.wait_ge(s_turned, turned_before)
            for j in range(TB):
                ins = dve.tensor_scalar(xn[:, j, :], tile_of(x, i * TB + j), ln_mv[:, j, 0:1],
                                        ln_rstd[:, j, :], ALU.subtract, ALU.mult)
            ins.then_inc(s_ln_norm, 1)

        def ln_gpsimd(pool, n):
            pool.wait_ge(s_ln_var, n + 1)
            pool.tensor_tensor(ln_rstd[:, :, 0], ln_mv[:, :, 1], minus_half[:, 0:TB],
                               ALU.pow).then_inc(s_ln_rstd, 1)

        def turn_batch(pe, turns, src):
            pe.wait_ge(s_turn_out, turns.now())
            for c in range(C):
                for j in range(TB):
                    ins = pe.transpose(turn[:, c, j * P:(j + 1) * P], src[:, j, c * P:(c + 1) * P],
                                       ident[:, :])
            ins.then_inc(s_turned, 1)
            turns.k += 1

        def turn_evac(act, turns, dst):
            act.wait_ge(s_turned, turns.now() + 1)
            act.activation(flat(dst[:, :, :]), bank(0), ACT.Copy).then_inc(s_turn_out, 1)
            turns.k += 1

        l0_w = attn_region.take([P, 4, C, D])
        l0_rows = attn_region.take([1, 4, D])
        l0_gain = attn_region.take([P, 2, D])
        ctxT2 = attn_region.take([P, C, B, P])
        head_of = sb("head_of", [P, HB0])
        half_of = sb("half_of", [P, 2])
        l0_kT = attn_region.take([P, C, CT])
        l0_v = attn_region.take([P, B, D])
        l0_kdiag = scratch.take([P, B, C, HB0, SK])
        l0_vdiag = scratch.take([P, B, H0 // 2, 2, HD0])
        heads_out = scratch.take([P, TB, D])
        junk = scratch.take([P, TB, D])
        ssq = scratch.take([P, TB])
        rms = scratch.take([P, TB])
        qn = scratch.take([P, TB, D])
        qT = scratch.take([P, C, S])
        top = sb("top", [P, H2])
        total = sb("total", [P, H2])
        oT = scratch.take([P, C, S])

        s_l0_load = sem("l0_load")
        s_proj = sem("rows_projected")
        s_ssq = sem("squares_summed")
        s_ms = sem("mean_square_ready")
        s_rms = sem("rms_ready")
        s_scaled = sem("rows_scaled")
        s_v = sem("l0_v_projected")
        s_vout = sem("l0_v_ready")
        s_diag = sem("l0_diag_ready")
        s_score = sem("scores_ready")
        s_shift = sem("scores_shifted")
        s_exp = sem("exp_ready")
        s_ptT = sem("probs_turned")
        s_pt = sem("probs_turn_out")
        s_pv = sem("pv_ready")
        s_o = sem("heads_ready")
        s_y = sem("attn_out_ready")
        s_res = sem("residual_added")

        q_ps = bank(1).rearrange("p (j d) -> p j d", j=TB)
        sc_ps = bank(2, 2)
        pt_ps = bank(4, 2)
        pv_ps = bank(6)[:, 0:D]
        y_ps = bank(7)[:, 0:D]

        def l0_attn_sync(sp):
            for dst, name in ((ctxT[:, :, :], "ctxT"), (l0_w[:, :, :, :], "l0_w"), (l0_rows[:, :, :], "l0_rows"),
                              (l0_gain[:, :, :], "l0_gain"), (ctxT2[:, :, :, :], "ctxT2"),
                              (head_of[:, :], "head_of"), (half_of[:, :], "half_of")):
                sp.dma_start(dst, A[name]).then_inc(s_l0_load, 16)
            sp.dma_start(x[:, :, :], A["x"]).then_inc(s_x_load, 16)

        def rms_scalar(act, n):
            act.wait_ge(s_proj, n + 1)
            for j in range(TB):
                ins = act.activation(junk[:, j, :], q_ps[:, j, :], ACT.Square, accum_out=ssq[:, j:j + 1])
            ins.then_inc(s_ssq, 1)

        def rms_vector(dve, n, gain, turned_before):
            dve.wait_ge(s_ssq, n + 1)
            dve.tensor_scalar(rms[:, :], ssq[:, :], 1.0 / D, 1e-6, ALU.mult, ALU.add).then_inc(s_ms, 1)
            dve.wait_ge(s_rms, n + 1)
            dve.wait_ge(s_turned, turned_before)
            for j in range(TB):
                ins = dve.scalar_tensor_tensor(out=qn[:, j, :], in0=q_ps[:, j, :], scalar=rms[:, j:j + 1],
                                               in1=gain, op0=ALU.mult, op1=ALU.mult)
            ins.then_inc(s_scaled, 1)

        def rms_gpsimd(pool, n):
            pool.wait_ge(s_ms, n + 1)
            pool.tensor_tensor(rms[:, :], rms[:, :], minus_half[:, 0:TB], ALU.pow).then_inc(s_rms, 1)

        def l0_attn_tensor(pe, turns):
            pe.wait_ge(s_l0_load, 16 * 7)
            pe.wait_ge(s_const, 3)
            for m in range(TB):
                pe.matmul(q_ps[:, m, :], ones[:, :], l0_rows[:, 1, :], start=True, stop=False)
                for c in range(C):
                    ins = pe.matmul(q_ps[:, m, :], ctxT[:, c, m * P:(m + 1) * P], l0_w[:, 1, c, :],
                                    start=False, stop=(c == C - 1))
            ins.then_inc(s_proj, 1)
            for b in range(B):
                v_ps = sc_ps[:, b * D:(b + 1) * D]
                pe.matmul(v_ps, ones[:, :], l0_rows[:, 2, :], start=True, stop=False)
                for c in range(C):
                    ins = pe.matmul(v_ps, ctxT2[:, c, b, :], l0_w[:, 2, c, :], start=False, stop=(c == C - 1))
            ins.then_inc(s_v, 1)
            pe.wait_ge(s_scaled, 1)
            turn_batch(pe, turns, qn)
            pe.wait_ge(s_vout, 1)

            def turn(b):
                pe.wait_ge(s_ln_norm, b + 1)
                turn_batch(pe, turns, xn)

            def project(b):
                pe.wait_ge(s_turn_out, turns.now())
                for j in range(TB):
                    pe.matmul(q_ps[:, j, :], ones[:, :], l0_rows[:, 0, :], start=True, stop=False)
                    for c in range(C):
                        ins = pe.matmul(q_ps[:, j, :], xT[:, c, j * P:(j + 1) * P], l0_w[:, 0, c, :],
                                        start=False, stop=(c == C - 1))
                ins.then_inc(s_proj, 1)

            def turn_queries(b):
                pe.wait_ge(s_scaled, b + 2)
                turn_batch(pe, turns, qn)

            def scores(i, j):
                pe.wait_ge(s_shift, i * TB + j + 1)
                for c in range(C):
                    keys = l0_kdiag[:, bass.ds(i, 1), c, :, :].rearrange("p b h k -> p (b h k)")
                    ins = pe.matmul(sc_ps[:, c * BANK:(c + 1) * BANK], qT[:, c, j * P:(j + 1) * P], keys,
                                    start=True, stop=True)
                ins.then_inc(s_score, 1)

            def turn_probs(i, j):
                pe.wait_ge(s_exp, i * TB + j + 1)
                pe.wait_ge(s_pt, i * TB + j + 1)
                for g in range(8):
                    ins = pe.transpose(pt_ps[:, g * P:(g + 1) * P], prob[:, g * P:(g + 1) * P], ident[:, :])
                ins.then_inc(s_ptT, 1)

            def weigh(i, j):
                pe.wait_ge(s_pt, i * TB + j + 2)
                pe.wait_ge(s_o, i * TB + j + 1)
                for g in range(8):
                    values = l0_vdiag[:, bass.ds(i, 1), g, :, :].rearrange("p b a d -> p (b a d)")
                    ins = pe.matmul(pv_ps[:, g * 32:(g + 1) * 32], probT[:, g, :], values, start=True, stop=True)
                ins.then_inc(s_pv, 1)

            def batch(i, more):
                scores(i, 1)
                turn_probs(i, 0)
                if more:
                    turn(i + 1)
                    project(i + 1)
                weigh(i, 0)
                turn_probs(i, 1)
                if more:
                    turn_queries(i + 1)
                    pe.wait_ge(s_turn_out, turns.now())
                    pe.wait_ge(s_diag, i + 2)
                    scores(i + 1, 0)
                weigh(i, 1)
                pe.wait_ge(s_o, i * TB + TB + 1)
                turn_batch(pe, turns, heads_out)
                pe.wait_ge(s_turn_out, turns.now())
                for j in range(TB):
                    pe.wait_ge(s_res, i * TB + j + 1)
                    pe.matmul(y_ps, ones[:, :], l0_rows[:, 3, :], start=True, stop=False)
                    for c in range(C):
                        ins = pe.matmul(y_ps, oT[:, c, j * P:(j + 1) * P], l0_w[:, 3, c, :],
                                        start=False, stop=(c == C - 1))
                    ins.then_inc(s_y, 1)

            turn(0)
            project(0)
            turn_queries(0)
            pe.wait_ge(s_turn_out, turns.now())
            pe.wait_ge(s_diag, 1)
            scores(0, 0)
            with pe.Fori(0, B - 1) as i:
                turns.loop(i, 3)
                batch(i, True)
            turns.end_loop(B - 1)
            batch(B - 1, False)

        def l0_attn_scalar(act, turns):
            rms_scalar(act, 0)
            act.wait_ge(s_v, 1)
            act.activation(l0_v[:, :, :].rearrange("p b d -> p (b d)"), sc_ps, ACT.Copy).then_inc(s_vout, 1)
            turn_evac(act, turns, l0_kT)

            def exponential(i, j):
                act.wait_ge(s_shift, i * TB + j + 2)
                act.activation(prob[:, :], prob[:, :], ACT.Exp, scale=HD0 ** -0.5).then_inc(s_exp, 1)

            def turned_out(i, j):
                act.wait_ge(s_ptT, i * TB + j + 2)
                act.wait_ge(s_pv, i * TB + j + 1)
                act.activation(probT[:, :, :].rearrange("p g q -> p (g q)"), pt_ps, ACT.Copy).then_inc(s_pt, 1)

            def batch(i, more):
                if more:
                    turn_evac(act, turns, xT)
                turned_out(i, 0)
                exponential(i, 1)
                if more:
                    rms_scalar(act, i + 2)
                turned_out(i, 1)
                if more:
                    turn_evac(act, turns, qT)
                    exponential(i + 1, 0)
                turn_evac(act, turns, oT)

            turn_evac(act, turns, xT)
            rms_scalar(act, 1)
            turn_evac(act, turns, qT)
            exponential(0, 0)
            with act.Fori(0, B - 1) as i:
                turns.loop(i, 3)
                batch(i, True)
            turns.end_loop(B - 1)
            batch(B - 1, False)

        def l0_attn_gpsimd(pool):
            rms_gpsimd(pool, 0)
            ln_gpsimd(pool, 0)
            pool.wait_ge(s_l0_load, 16 * 7)
            pool.wait_ge(s_turn_out, 1)
            pool.wait_ge(s_vout, 1)
            for b in range(B):
                for c in range(C):
                    pool.tensor_tensor(l0_kdiag[:, b, c, :, :],
                                       l0_kT[:, c:c + 1, b * SK:(b + 1) * SK].to_broadcast([P, HB0, SK]),
                                       head_of[:, :].unsqueeze(2).to_broadcast([P, HB0, SK]), ALU.mult)
                pool.tensor_tensor(l0_vdiag[:, b, :, :, :],
                                   l0_v[:, b, :].rearrange("p (g a d) -> p g a d", a=2, d=HD0),
                                   half_of[:, :].unsqueeze(1).unsqueeze(3).to_broadcast([P, H0 // 2, 2, HD0]),
                                   ALU.mult).then_inc(s_diag, 1)
                if b == 0:
                    rms_gpsimd(pool, 1)
            with pool.Fori(0, B - 1) as i:
                ln_gpsimd(pool, i + 1)
                rms_gpsimd(pool, i + 2)

        def l0_attn_vector(dve, st):
            def normalise(b, turned_before):
                ln_vector(dve, st, b, b)
                ln_apply(dve, b, turned_before)

            def shift(i, j):
                dve.wait_ge(s_score, i * TB + j + 2)
                st.done(dve.tensor_reduce(top[:, 0:H0], sc_ps.rearrange("p (h k) -> p h k", h=H0), AX, ALU.max))
                dve.wait_ge(s_ptT, i * TB + j + 1)
                dve.tensor_tensor(prob[:, :].rearrange("p (h k) -> p h k", h=H0),
                                  sc_ps.rearrange("p (h k) -> p h k", h=H0),
                                  top[:, 0:H0].unsqueeze(2).to_broadcast([P, H0, SK]),
                                  ALU.subtract).then_inc(s_shift, 1)

            def norm(i, j):
                sums = total[:, j * H0:(j + 1) * H0]
                dve.wait_ge(s_exp, i * TB + j + 1)
                st.done(dve.tensor_reduce(sums, prob[:, :].rearrange("p (h k) -> p h k", h=H0), AX, ALU.add))
                st.done(dve.reciprocal(sums, sums))

            def heads(i, j):
                dve.wait_ge(s_pv, i * TB + j + 2)
                dve.wait_ge(s_turned, i * 3 + 3)
                dve.tensor_tensor(heads_out[:, j, :].rearrange("p (h d) -> p h d", h=H0),
                                  pv_ps.rearrange("p (h d) -> p h d", h=H0),
                                  total[:, j * H0:(j + 1) * H0].unsqueeze(2).to_broadcast([P, H0, HD0]),
                                  ALU.mult).then_inc(s_o, 1)

            def batch(i, more):
                if more:
                    normalise(i + 1, i * 3 + 2)
                norm(i, 0)
                shift(i, 1)
                if more:
                    rms_vector(dve, i + 2, l0_gain[:, 0, :], i * 3 + 3)
                heads(i, 0)
                norm(i, 1)
                if more:
                    shift(i + 1, 0)
                heads(i, 1)
                for j in range(TB):
                    dve.wait_ge(s_y, i * TB + j + 1)
                    dve.scalar_tensor_tensor(out=tile_of(x, i * TB + j), in0=y_ps, scalar=gates[:, 0:1],
                                             in1=tile_of(x, i * TB + j), op0=ALU.mult, op1=ALU.add).then_inc(s_res, 1)

            dve.wait_ge(s_l0_load, 16 * 7)
            rms_vector(dve, 0, l0_gain[:, 1, :], 0)
            dve.wait_ge(s_x_load, 16)
            normalise(0, 1)
            rms_vector(dve, 1, l0_gain[:, 0, :], 1)
            shift(0, 0)
            with dve.Fori(0, B - 1) as i:
                st.loop(i, 4 + TB * 3)
                batch(i, True)
            st.end_loop(B - 1)
            batch(B - 1, False)

        scratch.restart()
        f0_w = ffn_region.take([P, 2, C, I0])
        f0_down = ffn_region.take([P, I0 // P, D])
        act_f = scratch.take([P, I0])
        hid = scratch.take([P, I0])
        mag = scratch.take([P, I0])
        beats = scratch.take([P, 6, I0 // 4], BF16)
        wins = scratch.take([P, 4, I0 // 4], BF16)
        hidT = scratch.take([P, I0 // P, P])

        s_f0_load = sem("f0_load")
        s_gate = sem("gate_ready")
        s_up = sem("up_ready")
        s_act = sem("act_ready")
        s_hid = sem("hidden_ready")
        s_mag = sem("magnitude_ready")
        s_kept = sem("hidden_kept")
        s_htT = sem("hidden_turned")
        s_ht = sem("hidden_turn_out")
        s_fy = sem("ffn_out_ready")

        gate_ps = bank(1, 2)
        up_ps = bank(3, 2)
        ht_ps = bank(5, 2)

        def l0_ffn_sync(sp):
            sp.dma_start(f0_w[:, :, :, :], A["f0_w"]).then_inc(s_f0_load, 16)
            sp.dma_start(f0_down[:, :, :], A["f0_down"]).then_inc(s_f0_load, 16)

        s_gated = sem("gate_times_act")

        def l0_ffn_gpsimd(pool):
            pool.sem_inc(s_gated, 1)
            ln_gpsimd(pool, B)
            with pool.Fori(0, B - 1) as i:
                ln_gpsimd(pool, i + 1 + B)

        def l0_ffn_tensor(pe, turns):
            def product(ps, w, j, n, ready):
                for c in range(C):
                    ins = pe.matmul(ps[:, n * BANK:(n + 1) * BANK], xT[:, c, j * P:(j + 1) * P],
                                    f0_w[:, w, c, n * BANK:(n + 1) * BANK], start=(c == 0), stop=(c == C - 1))
                if n:
                    ins.then_inc(ready, 1)

            def gate(i, j):
                pe.wait_ge(s_gated, i * TB + j + 1)
                product(gate_ps, 0, j, 0, s_gate)
                product(gate_ps, 0, j, 1, s_gate)

            def up(i, j, n):
                if n == 0:
                    pe.wait_ge(s_hid, i * TB + j + 1)
                product(up_ps, 1, j, n, s_up)

            def turn_kept(i, j):
                pe.wait_ge(s_kept, i * TB + j + 2)
                pe.wait_ge(s_ht, i * TB + j + 1)
                for g in range(I0 // P):
                    ins = pe.transpose(ht_ps[:, g * P:(g + 1) * P], hid[:, g * P:(g + 1) * P], ident[:, :])
                ins.then_inc(s_htT, 1)

            def down(i, j):
                pe.wait_ge(s_ht, i * TB + j + 2)
                pe.wait_ge(s_res, i * TB + j + NT + 1)
                for g in range(I0 // P):
                    ins = pe.matmul(y_ps, hidT[:, g, :], f0_down[:, g, :], start=(g == 0), stop=(g == I0 // P - 1))
                ins.then_inc(s_fy, 1)

            def turn(b):
                pe.wait_ge(s_ln_norm, b + B + 1)
                turn_batch(pe, turns, xn)

            def batch(i, more):
                up(i, 1, 0)
                turn_kept(i, 0)
                up(i, 1, 1)
                if more:
                    turn(i + 1)
                down(i, 0)
                if more:
                    pe.wait_ge(s_turn_out, turns.now())
                    gate(i + 1, 0)
                    up(i + 1, 0, 0)
                turn_kept(i, 1)
                if more:
                    up(i + 1, 0, 1)
                down(i, 1)
                if more:
                    gate(i + 1, 1)

            pe.wait_ge(s_f0_load, 32)
            pe.wait_ge(s_res, NT + 1)
            turn(0)
            pe.wait_ge(s_turn_out, turns.now())
            gate(0, 0)
            up(0, 0, 0)
            up(0, 0, 1)
            gate(0, 1)
            with pe.Fori(0, B - 1) as i:
                turns.loop(i, 1)
                batch(i, True)
            turns.end_loop(B - 1)
            batch(B - 1, False)

        def l0_ffn_scalar(act, turns):
            def tanh(i, j):
                act.wait_ge(s_gate, i * TB + j + 1)
                act.wait_ge(s_hid, i * TB + j + 1)
                act.activation(act_f[:, :], gate_ps, ACT.Tanh, scale=0.5).then_inc(s_act, 1)

            def magnitude(i, j):
                act.wait_ge(s_hid, i * TB + j + 2)
                act.wait_ge(s_kept, i * TB + j + 1)
                act.activation(mag[:, :], hid[:, :], ACT.Abs).then_inc(s_mag, 1)

            def turned_out(i, j):
                act.wait_ge(s_htT, i * TB + j + 2)
                act.wait_ge(s_fy, i * TB + j + 1)
                act.activation(hidT[:, :, :].rearrange("p g q -> p (g q)"), ht_ps, ACT.Copy).then_inc(s_ht, 1)

            def batch(i, more):
                tanh(i, 1)
                turned_out(i, 0)
                if more:
                    turn_evac(act, turns, xT)
                magnitude(i, 1)
                if more:
                    tanh(i + 1, 0)
                turned_out(i, 1)
                if more:
                    magnitude(i + 1, 0)

            turn_evac(act, turns, xT)
            tanh(0, 0)
            magnitude(0, 0)
            with act.Fori(0, B - 1) as i:
                turns.loop(i, 1)
                batch(i, True)
            turns.end_loop(B - 1)
            batch(B - 1, False)

        def l0_ffn_vector(dve, st):
            quad = lambda v: v.rearrange("p (n f) -> p f n", f=4)

            def normalise(b):
                ln_vector(dve, st, b, b + B)
                ln_apply(dve, b, b + 13)

            def times_gate(i, j):
                dve.wait_ge(s_act, i * TB + j + 1)
                dve.scalar_tensor_tensor(out=act_f[:, :], in0=act_f[:, :], scalar=1.0, in1=gate_ps,
                                         op0=ALU.add, op1=ALU.mult).then_inc(s_gated, 1)

            def times_up(i, j):
                dve.wait_ge(s_gated, i * TB + j + 2)
                dve.wait_ge(s_up, i * TB + j + 1)
                dve.wait_ge(s_htT, i * TB + j + 1)
                dve.scalar_tensor_tensor(out=hid[:, :], in0=act_f[:, :], scalar=0.5, in1=up_ps,
                                         op0=ALU.mult, op1=ALU.mult).then_inc(s_hid, 1)

            def compare(i, j):
                dve.wait_ge(s_mag, i * TB + j + 1)
                m = quad(mag[:, :])
                for first, n, at in ((0, 3, 0), (1, 2, 3), (2, 1, 5)):
                    st.mark(dve.tensor_tensor(beats[:, at:at + n, :],
                                              m[:, first:first + 1, :].to_broadcast([P, n, I0 // 4]),
                                              m[:, first + 1:4, :], ALU.is_ge))

            def select(i, j):
                st.wait()
                for v, (a, b, op) in enumerate(((0, 1, ALU.add), (3, 4, ALU.add), (5, 1, ALU.subtract), (2, 4, ALU.add))):
                    st.mark(dve.tensor_tensor(wins[:, v, :], beats[:, a, :], beats[:, b, :], op))
                st.wait()
                for v, (c, op) in enumerate(((2, ALU.add), (0, ALU.subtract), (3, ALU.subtract), (5, ALU.add))):
                    st.mark(dve.tensor_tensor(wins[:, v, :], wins[:, v, :], beats[:, c, :], op))
                st.wait()
                h = quad(hid[:, :])
                for v, (bound, op) in enumerate(((2.0, ALU.is_ge), (1.0, ALU.is_ge), (0.0, ALU.is_ge), (1.0, ALU.is_le))):
                    ins = dve.scalar_tensor_tensor(out=h[:, v, :], in0=wins[:, v, :], scalar=bound, in1=h[:, v, :],
                                                   op0=op, op1=ALU.mult)
                ins.then_inc(s_kept, 1)

            def batch(i, more):
                select(i, 0)
                times_gate(i, 1)
                if more:
                    normalise(i + 1)
                times_up(i, 1)
                compare(i, 1)
                select(i, 1)
                add_result(dve, i, 0, 1, s_fy)
                if more:
                    times_gate(i + 1, 0)
                    times_up(i + 1, 0)
                    compare(i + 1, 0)
                add_result(dve, i, 1, 1, s_fy)

            normalise(0)
            times_gate(0, 0)
            times_up(0, 0)
            compare(0, 0)
            with dve.Fori(0, B - 1) as i:
                st.loop(i, 4 + TB * 11)
                batch(i, True)
            st.end_loop(B - 1)
            batch(B - 1, False)

        def add_result(dve, i, j, gate, ready):
            dve.wait_ge(ready, i * TB + j + 2)
            dve.scalar_tensor_tensor(out=tile_of(x, i * TB + j), in0=y_ps, scalar=gates[:, gate:gate + 1],
                                     in1=tile_of(x, i * TB + j), op0=ALU.mult, op1=ALU.add).then_inc(s_res, 1)

        scratch.restart()
        attn_region.restart()
        l1_kvc = attn_region.take([P, C, KC1])
        l1_dq = attn_region.take([P, C, QC1])
        l1_uqT = attn_region.take([P, H1, QC1])
        l1_qr = attn_region.take([QC1, 2, H1 * R1])
        l1_uk = attn_region.take([KC1, H1 * HD1])
        l1_kr = attn_region.take([KC1, 2, P])
        l1_uv = attn_region.take([KC1, H1 * HD1])
        l1_wo = attn_region.take([P, H1, D])
        l1_keys = attn_region.take([QC1, B, H1, SK])
        l1_vals = attn_region.take([P, B, H1 // 2, D])
        l1_cos_sin = scratch.take([P, 2, S])
        kvT = scratch.take([KC1, CT])
        kv_h = scratch.take([P, 4, 2, CT])
        krot = scratch.take([P, 2, CT])
        krdiag = scratch.take([P, B, 2, SK])
        qcT = scratch.take([QC1, S])
        qrot = scratch.take([P, 2, 2, 2 * P])
        qrT = scratch.take([P, H1 // 2, S])
        seg_i = sb("seg_i", [P, NT], I32)
        seg = scratch.take([P, NT])
        key_at = scratch.take([P, SK])
        key_last = scratch.take([P, SK])
        seen = scratch.take([P, NT, SK])
        unseen = scratch.take([P, NT, SK])

        s_l1_load = sem("l1_load")
        s_kvT = sem("kv_compressed")
        s_kvT_out = sem("kv_compressed_out")
        s_kr = sem("keys_to_rotate")
        s_krdiag = sem("rotated_keys_ready")
        s_kvh = sem("head_kv_ready")
        s_kvh_out = sem("head_kv_out")
        s_keys = sem("head_keys_ready")
        s_keys_out = sem("head_keys_out")
        s_vals = sem("pair_values_ready")
        s_vals_out = sem("pair_values_out")
        s_qc = sem("queries_compressed")
        s_qc_out = sem("queries_compressed_out")
        s_qr = sem("queries_to_rotate")
        s_qrot = sem("queries_multiplied")
        s_qrT = sem("queries_rotated")
        s_prob = sem("probs_ready")
        s_masked = sem("scores_masked")

        L1_LOADS = 12
        l1_names = ("l1_kvc", "l1_dq", "l1_uqT", "l1_qr", "l1_uk", "l1_kr", "l1_uv", "l1_wo")

        def l1_attn_sync(sp):
            sp.wait_ge(s_res, NT + 1)
            for dst, name in zip((l1_kvc, l1_dq, l1_uqT, l1_qr, l1_uk, l1_kr, l1_uv, l1_wo), l1_names):
                sp.dma_start(dst, A[name]).then_inc(s_l1_load, 16)
            sp.dma_start(seg_i[:, :], A["seg"]).then_inc(s_l1_load, 16)
            sp.wait_ge(s_res, 2 * NT + 1)
            for dst, name in ((l1_cos_sin, "l1_cos_sin"), (key_at, "key_at"), (key_last, "key_last")):
                sp.dma_start(dst, A[name]).then_inc(s_l1_load, 16)

        def l1_attn_gpsimd(pool):
            for signal, start in ((s_masked, 1), (s_qrot, 2), (s_qrT, 1)):
                pool.sem_inc(signal, start)

            def rotated(i, j):
                pool.wait_ge(s_score, i * TB + (NT + j))
                for k in range(4):
                    pool.wait_ge(s_qrot, i * 8 + (4 * j + k + 3))
                    pool.tensor_tensor(qrT[:, 2 * k:2 * k + 2, j * P:(j + 1) * P],
                                       qrot[:, k % 2, 0, :].rearrange("p (a q) -> p a q", a=2),
                                       qrot[:, k % 2, 1, :].rearrange("p (a q) -> p a q", a=2), ALU.add).then_inc(s_qrT, 1)

            ln_gpsimd(pool, 2 * B)
            rotated(0, 0)
            rotated(0, 1)
            with pool.Fori(0, B - 1) as i:
                ln_gpsimd(pool, i + 1 + 2 * B)
                rotated(i + 1, 0)
                rotated(i + 1, 1)

        kvh_ps = [bank(1 + k).rearrange("p (a n) -> p a n", a=2) for k in range(2)]
        keys_ps = bank(3).rearrange("p (a n) -> p a n", a=2)
        vals_ps = [bank(4, 2), bank(6, 2)]
        sc1_ps = bank(1, 2)
        pt1_ps = bank(3, 2)
        qr_ps = [bank(5), bank(6)]
        qc_ps = bank(0)[0:QC1, 0:S]

        def l1_attn_tensor(pe, turns):
            pe.wait_ge(s_l1_load, 16 * L1_LOADS)
            pe.wait_ge(s_res, 2 * NT + 1)
            for c in range(C):
                ins = pe.matmul(kvh_ps[0][0:KC1, 0, :], l1_kvc[:, c, :], ctxT[:, c, :], start=(c == 0), stop=(c == C - 1))
            ins.then_inc(s_kvT, 1)
            pe.wait_ge(s_kvT_out, 1)
            for a in range(2):
                ins = pe.matmul(keys_ps[:, a, :], l1_kr[:, a, :], kvT, start=True, stop=True)
            ins.then_inc(s_kr, 1)

            def head_kv(h):
                if h >= 2:
                    pe.wait_ge(s_kvh_out, h - 1)
                pe.matmul(kvh_ps[h % 2][:, 0, :], l1_uk[:, h * HD1:(h + 1) * HD1], kvT, start=True, stop=True)
                pe.matmul(kvh_ps[h % 2][:, 1, :], l1_uv[:, h * HD1:(h + 1) * HD1], kvT, start=True, stop=True)\
                  .then_inc(s_kvh, 1)

            head_kv(0)
            head_kv(1)
            pe.wait_ge(s_krdiag, 1)
            for g in range(H1 // 2):
                if g + 1 < H1 // 2:
                    head_kv(2 * g + 2)
                    head_kv(2 * g + 3)
                pe.wait_ge(s_kvh_out, 2 * g + 2)
                if g >= 1:
                    pe.wait_ge(s_keys_out, g)
                for a in range(2):
                    ins = pe.matmul(keys_ps[0:QC1, a, :], l1_uqT[:, 2 * g + a, :], kv_h[:, (2 * g + a) % 4, 0, :],
                                    start=True, stop=True)
                ins.then_inc(s_keys, 1)
                if g >= 2:
                    pe.wait_ge(s_vals_out, g - 1)
                for b in range(B):
                    for a in range(2):
                        ins = pe.matmul(vals_ps[g % 2][SK * a:SK * a + SK, b * D:(b + 1) * D],
                                        kv_h[:, (2 * g + a) % 4, 1, b * SK:(b + 1) * SK], l1_wo[:, 2 * g + a, :],
                                        start=True, stop=True)
                ins.then_inc(s_vals, 1)
            pe.wait_ge(s_vals_out, H1 // 2)
            pe.wait_ge(s_keys_out, H1 // 2)

            def turn(b):
                pe.wait_ge(s_ln_norm, b + 2 * B + 1)
                turn_batch(pe, turns, xn)

            def compress(b):
                pe.wait_ge(s_turn_out, turns.now())
                for c in range(C):
                    ins = pe.matmul(qc_ps, l1_dq[:, c, :], xT[:, c, :], start=(c == 0), stop=(c == C - 1))
                ins.then_inc(s_qc, 1)

            def rotary(i, j, k):
                if k == 0:
                    pe.wait_ge(s_qc_out, i + 1)
                pe.wait_ge(s_qrot, i * 8 + (4 * j + k + 1))
                for a in range(2):
                    for n in range(2):
                        h = 2 * (2 * k + n)
                        ins = pe.matmul(qr_ps[k % 2][:, (2 * a + n) * P:(2 * a + n + 1) * P], l1_qr[:, a, h * R1:(h + 2) * R1],
                                        qcT[:, j * P:(j + 1) * P], start=True, stop=True)
                ins.then_inc(s_qr, 1)

            def scores(i, j):
                pe.wait_ge(s_qrT, i * 8 + (4 * j + 6))
                pe.wait_ge(s_masked, i * TB + (j + 1))
                for n in range(2):
                    keys = l1_keys[:, bass.ds(i, 1), 8 * n:8 * n + 8, :].rearrange("p a h k -> p (a h k)")
                    pe.matmul(sc1_ps[:, n * BANK:(n + 1) * BANK], qcT[:, j * P:(j + 1) * P], keys,
                              start=True, stop=False)
                    for g in range(4 * n, 4 * n + 4):
                        ins = pe.matmul(sc1_ps[:, g * P:(g + 1) * P], qrT[:, g, j * P:(j + 1) * P],
                                        krdiag[:, bass.ds(i, 1), :, :].rearrange("p b a k -> p (b a k)"),
                                        start=False, stop=(g % 4 == 3))
                ins.then_inc(s_score, 1)

            def turn_probs(i, j):
                pe.wait_ge(s_prob, i * TB + j + 1)
                pe.wait_ge(s_pt, i * TB + j + NT + 1)
                for g in range(8):
                    ins = pe.transpose(pt1_ps[:, g * P:(g + 1) * P], prob[:, g * P:(g + 1) * P], ident[:, :])
                ins.then_inc(s_ptT, 1)

            def weigh(i, j):
                pe.wait_ge(s_pt, i * TB + j + NT + 2)
                pe.wait_ge(s_res, i * TB + j + 2 * NT + 1)
                for g in range(8):
                    ins = pe.matmul(y_ps, probT[:, g, :],
                                    l1_vals[:, bass.ds(i, 1), g, :].rearrange("p b n -> p (b n)"),
                                    start=(g == 0), stop=(g == 7))
                ins.then_inc(s_y, 1)

            def batch(i, more):
                scores(i, 1)
                if more:
                    pe.wait_ge(s_qc_out, i + 1)
                    turn(i + 1)
                turn_probs(i, 0)
                if more:
                    compress(i + 1)
                weigh(i, 0)
                if more:
                    for k in range(4):
                        rotary(i + 1, 0, k)
                    scores(i + 1, 0)
                    rotary(i + 1, 1, 0)
                turn_probs(i, 1)
                if more:
                    for k in range(1, 4):
                        rotary(i + 1, 1, k)
                weigh(i, 1)

            turn(0)
            compress(0)
            for k in range(4):
                rotary(0, 0, k)
            scores(0, 0)
            for k in range(4):
                rotary(0, 1, k)
            with pe.Fori(0, B - 1) as i:
                turns.loop(i, 1)
                batch(i, True)
            turns.end_loop(B - 1)
            batch(B - 1, False)

        def l1_attn_scalar(act, turns):
            act.wait_ge(s_kvT, 1)
            act.activation(kvT, kvh_ps[0][0:KC1, 0, :], ACT.Copy).then_inc(s_kvT_out, 1)

            def head_out(h):
                act.wait_ge(s_kvh, h + 1)
                if h >= 4:
                    act.wait_ge(s_vals, h // 2 - 1)
                act.activation(kv_h[:, h % 4, :, :], kvh_ps[h % 2], ACT.Copy).then_inc(s_kvh_out, 1)

            head_out(0)
            head_out(1)
            for g in range(H1 // 2):
                if g + 1 < H1 // 2:
                    head_out(2 * g + 2)
                    head_out(2 * g + 3)
                act.wait_ge(s_keys, g + 1)
                act.activation(l1_keys[:, :, 2 * g:2 * g + 2, :].rearrange("p b a k -> p a b k"),
                               keys_ps[0:QC1, :, :].rearrange("p a (b k) -> p a b k", b=B), ACT.Copy).then_inc(s_keys_out, 1)

            def compressed(b):
                act.wait_ge(s_qc, b + 1)
                act.activation(qcT, qc_ps, ACT.Copy).then_inc(s_qc_out, 1)

            def exponential(i, j):
                act.wait_ge(s_shift, i * TB + j + NT + 2)
                act.activation(prob[:, :], prob[:, :], ACT.Exp, scale=(HD1 + R1) ** -0.5).then_inc(s_exp, 1)

            def turned_out(i, j):
                act.wait_ge(s_ptT, i * TB + j + NT + 2)
                act.wait_ge(s_y, i * TB + j + NT)
                act.activation(probT[:, :, :].rearrange("p g q -> p (g q)"), pt1_ps, ACT.Copy).then_inc(s_pt, 1)

            def batch(i, more):
                if more:
                    turn_evac(act, turns, xT)
                turned_out(i, 0)
                if more:
                    compressed(i + 1)
                exponential(i, 1)
                turned_out(i, 1)
                if more:
                    exponential(i + 1, 0)

            turn_evac(act, turns, xT)
            compressed(0)
            exponential(0, 0)
            with act.Fori(0, B - 1) as i:
                turns.loop(i, 1)
                batch(i, True)
            turns.end_loop(B - 1)
            batch(B - 1, False)

        def l1_attn_vector(dve, st):
            dve.wait_ge(s_l1_load, 16 * L1_LOADS)
            st.done(dve.tensor_copy(seg, seg_i[:, :]))
            wide = lambda v, axis: v.unsqueeze(axis).to_broadcast([P, NT, SK])
            st.mark(dve.tensor_tensor(seen, wide(key_at, 1), wide(seg, 2), ALU.is_le))
            st.done(dve.tensor_tensor(unseen, wide(key_last, 1), wide(seg, 2), ALU.is_ge))
            st.done(dve.tensor_tensor(unseen, unseen, seen, ALU.mult))
            st.done(dve.tensor_scalar(unseen, unseen, -1.0, 1e30, ALU.add, ALU.mult))
            dve.wait_ge(s_kr, 1)
            for a in range(2):
                st.mark(dve.tensor_tensor(krot[:, a, :].rearrange("p (b k) -> p b k", b=B),
                                          keys_ps[:, a, :].rearrange("p (b k) -> p b k", b=B),
                                          l1_cos_sin[:, a, 0:SK].unsqueeze(1).to_broadcast([P, B, SK]), ALU.mult))
            st.wait()
            st.done(dve.tensor_tensor(krot[:, 0, :], krot[:, 0, :], krot[:, 1, :], ALU.add))
            for b in range(B):
                ins = st.mark(dve.tensor_tensor(krdiag[:, b, :, :],
                                                krot[:, 0:1, b * SK:(b + 1) * SK].to_broadcast([P, 2, SK]),
                                                half_of[:, :].unsqueeze(2).to_broadcast([P, 2, SK]), ALU.mult))
            st.wait()
            dve.engine_nop().then_inc(s_krdiag, 1)
            for g in range(H1 // 2):
                dve.wait_ge(s_vals, g + 1)
                dve.tensor_copy(l1_vals[:, :, g, :], vals_ps[g % 2].rearrange("p (b n) -> p b n", b=B)).then_inc(s_vals_out, 1)
            heads = lambda v: v.rearrange("p (h k) -> p h k", h=H1)
            per_head = lambda v: v[:, 0:H1].unsqueeze(2).to_broadcast([P, H1, SK])

            def normalise(b):
                ln_vector(dve, st, b, b + 2 * B)
                ln_apply(dve, b, b + 17)

            def multiply(i, j, k):
                dve.wait_ge(s_qr, i * 8 + (4 * j + k + 1))
                dve.wait_ge(s_qrT, i * 8 + (4 * j + k + 1))
                dve.tensor_tensor(qrot[:, k % 2, :, :].rearrange("p a (n q) -> p a n q", n=2),
                                  qr_ps[k % 2].rearrange("p (a n q) -> p a n q", a=2, n=2),
                                  l1_cos_sin[:, :, j * P:(j + 1) * P].unsqueeze(2).to_broadcast([P, 2, 2, P]),
                                  ALU.mult).then_inc(s_qrot, 1)

            def mask(i, j):
                dve.wait_ge(s_score, i * TB + j + NT + 2)
                dve.wait_ge(s_ptT, i * TB + j + NT + 1)
                dve.tensor_tensor(heads(prob[:, :]), heads(sc1_ps),
                                  unseen[:, bass.ds(i * TB + j, 1), :].to_broadcast([P, H1, SK]), ALU.add).then_inc(s_masked, 1)

            def shift(i, j):
                dve.wait_ge(s_masked, i * TB + (j + 2))
                st.done(dve.tensor_reduce(top[:, 0:H1], heads(prob[:, :]), AX, ALU.max))
                dve.tensor_tensor(heads(prob[:, :]), heads(prob[:, :]), per_head(top), ALU.subtract).then_inc(s_shift, 1)

            def divide(i, j):
                dve.wait_ge(s_exp, i * TB + j + NT + 1)
                st.done(dve.tensor_reduce(total[:, 0:H1], heads(prob[:, :]), AX, ALU.add))
                st.done(dve.reciprocal(total[:, 0:H1], total[:, 0:H1]))
                dve.tensor_tensor(heads(prob[:, :]), heads(prob[:, :]), per_head(total), ALU.mult).then_inc(s_prob, 1)

            def add(i, j):
                dve.wait_ge(s_y, i * TB + j + NT + 1)
                dve.scalar_tensor_tensor(out=tile_of(x, i * TB + j), in0=y_ps, scalar=gates[:, 2:3],
                                         in1=tile_of(x, i * TB + j), op0=ALU.mult, op1=ALU.add).then_inc(s_res, 1)

            def batch(i, more):
                if more:
                    normalise(i + 1)
                mask(i, 1)
                shift(i, 1)
                add(i, 0)
                if more:
                    for k in range(4):
                        multiply(i + 1, 0, k)
                divide(i, 1)
                if more:
                    multiply(i + 1, 1, 0)
                    mask(i + 1, 0)
                    for k in range(1, 4):
                        multiply(i + 1, 1, k)
                    shift(i + 1, 0)
                add(i, 1)
                if more:
                    divide(i + 1, 0)

            normalise(0)
            for k in range(4):
                multiply(0, 0, k)
            mask(0, 0)
            shift(0, 0)
            for k in range(4):
                multiply(0, 1, k)
            divide(0, 0)
            with dve.Fori(0, B - 1) as i:
                st.loop(i, 4 + TB * 3)
                batch(i, True)
            st.end_loop(B - 1)
            batch(B - 1, False)

        SLOTS = 4
        UNITS = 2 * SLOTS
        HT = T // 2
        scratch.restart()
        ffn_region.restart()
        xT_all = scratch.take([P, C, T])
        weight_of = scratch.take([P, NT, E3 + 1])
        act_u = scratch.take([P, 2, HT])
        hid_u = scratch.take([P, 2, HT])
        expert_w = ffn_region.take([P, SLOTS, 3 * D])
        r_top = scratch.take([P, NT, 1])
        r_sum = scratch.take([P, NT, 1])
        moe_mark = scratch.at

        s_xall = sem("all_transposed")
        s_expert = [sem(f"expert_loaded_{k}") for k in range(SLOTS)]
        s_ugate = sem("unit_gate_ready")
        s_uup = sem("unit_up_ready")
        s_uact = sem("unit_act_ready")
        s_uhid = sem("unit_hidden_ready")
        s_udown = sem("unit_down_ready")
        s_uadd = sem("unit_tile_added")
        s_logit = sem("logits_ready")
        s_rshift = sem("logits_shifted")
        s_rexp = sem("router_exp_ready")
        s_routed = sem("router_done")

        gate_u = [bank(1), bank(2)]
        up_u = [bank(3), bank(4)]
        down_u = [bank(5, 2), None]
        down_banks = [(5, 6), (7, 0)]

        def down_of(k, q):
            b = down_banks[k][q // 2]
            return bank(b)[:, (q % 2) * D:(q % 2 + 1) * D]

        def experts_sync(sp, name, experts, before, units_before):
            for k in range(SLOTS):
                sp.dma_start(expert_w[:, k, :], A[name][k]).then_inc(s_expert[k], 16)
            if experts > 2 * SLOTS:
                with sp.Fori(1, experts // SLOTS) as t:
                    for k in range(SLOTS):
                        sp.wait_ge(s_udown, t * UNITS + (units_before + 2 * k + 2 + 2 - UNITS))
                        sp.dma_start(expert_w[:, k, :],
                                     A[name][bass.ds(t * SLOTS + k, 1), :, :].rearrange("e p n -> p (e n)"))\
                          .then_inc(s_expert[k], 16)
            if experts % SLOTS:
                sp.wait_ge(s_udown, 2 * experts + (units_before + 2 - UNITS))
                sp.dma_start(expert_w[:, 0, :], A[name][experts - 1]).then_inc(s_expert[0], 16)

        def unit_loop(eng, experts, unit):
            turns = (experts - 1) // SLOTS
            with eng.Fori(0, turns) as t:
                for u in range(UNITS):
                    unit(t, u, True)
            left = 2 * experts - turns * UNITS
            for u in range(left):
                unit(turns, u, u + 1 < left)

        def experts_tensor(pe, experts, before, units_before):
            def gate_up(t, u):
                k = u // 2 % SLOTS
                if u % 2 == 0:
                    pe.wait_ge(s_expert[k], (t + u // UNITS) * 16 + 16 * (before[k] + 1))
                pe.wait_ge(s_uhid, t * UNITS + (units_before + u + 1))
                for a, ps, ready in ((0, gate_u, s_ugate), (1, up_u, s_uup)):
                    for c in range(C):
                        at = (2 * c + a) * I1
                        ins = pe.matmul(ps[u % 2], expert_w[:, k, at:at + I1],
                                        xT_all[:, c, (u % 2) * HT:(u % 2 + 1) * HT], start=(c == 0), stop=(c == C - 1))
                    ins.then_inc(ready, 1)

            def down(t, u):
                pe.wait_ge(s_uhid, t * UNITS + (units_before + u + 1 + 2))
                pe.wait_ge(s_uadd, t * (4 * UNITS) + 4 * (units_before + u + 1))
                for q in range(4):
                    ins = pe.matmul(down_of(u % 2, q), hid_u[:, u % 2, q * P:(q + 1) * P],
                                    expert_w[:, u // 2, 2 * D:3 * D], start=True, stop=True)
                ins.then_inc(s_udown, 1)

            def unit(t, u, more):
                if more:
                    gate_up(t, u + 1)
                down(t, u)

            gate_up(0, 0)
            unit_loop(pe, experts, unit)

        def experts_scalar(act, experts, units_before):
            def tanh(t, u):
                act.wait_ge(s_ugate, t * UNITS + (units_before + u + 1))
                act.wait_ge(s_uhid, t * UNITS + (units_before + u + 1))
                act.activation(act_u[:, u % 2, :], gate_u[u % 2], ACT.Tanh, scale=0.5).then_inc(s_uact, 1)

            tanh(0, 0)
            unit_loop(act, experts, lambda t, u, more: tanh(t, u + 1) if more else None)

        def experts_vector(dve, st, experts, units_before):
            def hidden(t, u):
                k = u % 2
                dve.wait_ge(s_uact, t * UNITS + (units_before + u + 1))
                ins = dve.scalar_tensor_tensor(out=act_u[:, k, :], in0=act_u[:, k, :], scalar=1.0, in1=gate_u[k],
                                               op0=ALU.add, op1=ALU.mult)
                ins.then_inc(s_uown, 1)
                dve.wait_ge(s_uown, t * UNITS + (units_before + u + 1))
                dve.wait_ge(s_uup, t * UNITS + (units_before + u + 1))
                dve.wait_ge(s_udown, t * UNITS + (units_before + u + 1))
                dve.scalar_tensor_tensor(out=hid_u[:, k, :], in0=act_u[:, k, :], scalar=0.5, in1=up_u[k],
                                         op0=ALU.mult, op1=ALU.mult).then_inc(s_uhid, 1)

            def add(t, u):
                dve.wait_ge(s_udown, t * UNITS + (units_before + u + 1 + 2))
                dve.wait_ge(s_uadd, t * (4 * UNITS) + 4 * (units_before + u + 1))
                for q in range(4):
                    n = (u % 2) * 4 + q
                    weight = weight_of[:, n, bass.ds(t * SLOTS + u // 2, 1)]
                    dve.scalar_tensor_tensor(out=x[:, n, :], in0=down_of(u % 2, q), scalar=weight, in1=x[:, n, :],
                                             op0=ALU.mult, op1=ALU.add).then_inc(s_uadd, 1)

            def unit(t, u, more):
                if more:
                    hidden(t, u + 1)
                add(t, u)

            hidden(0, 0)
            unit_loop(dve, experts, unit)
            dve.wait_ge(s_uadd, 4 * (units_before + 2 * experts + 2))
            dve.engine_nop().then_inc(s_res, NT)

        s_uown = sem("unit_act_times_gate")

        W1 = E1 + 8
        f1_router = scratch.take([P, C, E1])
        f1_bias = scratch.take([1, E1])
        below = scratch.take([P, 8])
        r_prob = scratch.take([P, NT, W1])
        r_rest = scratch.take([P, NT, W1])
        r_eight = scratch.take([P, NT, 8])
        r_two = scratch.take([P, NT, 8])

        s_f1_load = sem("f1_load")
        logit_ps = bank(6)

        def l1_ffn_sync(sp):
            sp.wait_ge(s_res, 3 * NT + 1)
            sp.dma_start(f1_router, A["f1_router"]).then_inc(s_f1_load, 16)
            sp.dma_start(f1_bias, A["f1_bias"]).then_inc(s_f1_load, 16)
            sp.dma_start(below, A["below"]).then_inc(s_f1_load, 16)
            experts_sync(sp, "f1_experts", E1 + 1, 0, 0)

        def router_tensor(pe, turns, normalised, r, router, experts, bias):
            for b in range(B):
                pe.wait_ge(s_ln_norm, b + normalised + 1)
                pe.wait_ge(s_xall, b + r + 1)
                turn_batch(pe, turns, xn)
                pe.wait_ge(s_turn_out, turns.now())
                for j in range(TB):
                    t = b * TB + j
                    ps = logit_ps[:, t * experts:(t + 1) * experts]
                    if bias is not None:
                        pe.matmul(ps, ones[:, :], bias, start=True, stop=False)
                    for c in range(C):
                        ins = pe.matmul(ps, xT[:, c, j * P:(j + 1) * P], router[:, c, :],
                                        start=(bias is None and c == 0), stop=(c == C - 1))
                ins.then_inc(s_logit, 1)

        def router_scalar(act, turns, r, n, probs):
            for b in range(B):
                act.wait_ge(s_logit, b + r + 1)
                turn_evac(act, turns, xT)
                act.activation(xT_all[:, :, b * S:(b + 1) * S], turn, ACT.Copy).then_inc(s_xall, 1)
            act.wait_ge(s_rshift, n + 2)
            act.activation(probs, probs, ACT.Exp).then_inc(s_rexp, 1)

        def router_gpsimd(pool, n):
            with pool.Fori(0, B) as i:
                ln_gpsimd(pool, i + n)

        def router_vector(dve, st, ln_before, turned_before, r, n, probs, experts):
            for b in range(B):
                ln_vector(dve, st, b, b + ln_before)
                ln_apply(dve, b, b + turned_before)
            logits = logit_ps[:, 0:NT * experts].rearrange("p (t e) -> p t e", t=NT)
            spread = lambda v: v.to_broadcast([P, NT, experts])
            dve.wait_ge(s_logit, r + B + 1)
            st.done(dve.tensor_reduce(r_top[:, :, 0], logits, AX, ALU.max))
            dve.tensor_tensor(probs, logits, spread(r_top), ALU.subtract).then_inc(s_rshift, 1)
            dve.wait_ge(s_rexp, n + 1)
            st.done(dve.tensor_reduce(r_sum[:, :, 0], probs, AX, ALU.add))
            st.done(dve.reciprocal(r_sum, r_sum))
            st.done(dve.tensor_tensor(probs, probs, spread(r_sum), ALU.mult))

        def l1_ffn_tensor(pe, turns):
            pe.wait_ge(s_f1_load, 48)
            router_tensor(pe, turns, 3 * B, 0, f1_router, E1, f1_bias)
            pe.wait_ge(s_xall, B + 1)
            pe.wait_ge(s_rshift, 2)
            experts_tensor(pe, E1 + 1, [0] * SLOTS, 0)

        def l1_ffn_scalar(act, turns):
            router_scalar(act, turns, 0, 0, r_prob[:, :, 0:E1])
            experts_scalar(act, E1 + 1, 0)

        def l1_ffn_gpsimd(pool):
            router_gpsimd(pool, 3 * B)

        def l1_ffn_vector(dve, st):
            dve.engine_nop().then_inc(s_uhid, 2)
            dve.engine_nop().then_inc(s_udown, 2)
            dve.engine_nop().then_inc(s_uadd, 8)
            dve.wait_ge(s_f1_load, 48)
            st.mark(dve.memset(weight_of[:, :, E1:E1 + 1], 1.0))
            wide_below = below.unsqueeze(1).to_broadcast([P, NT, 8])
            st.mark(dve.tensor_copy(r_prob[:, :, E1:W1], wide_below))
            st.done(dve.tensor_copy(r_two, wide_below))
            probs = r_prob[:, :, 0:E1]
            router_vector(dve, st, 3 * B, 21, 0, 0, probs, E1)
            for t in range(NT):
                st.mark(dve.max(r_eight[:, t, :], r_prob[:, t, 0:E1]))
            st.wait()
            st.done(dve.tensor_copy(r_two[:, :, 0:2], r_eight[:, :, 0:2]))
            for t in range(NT):
                st.mark(dve.match_replace(out=r_rest[:, t, :], in_to_replace=r_two[:, t, :],
                                          in_values=r_prob[:, t, :], imm_value=-9.0))
            st.wait()
            chosen = r_rest[:, :, 0:E1]
            st.done(dve.tensor_tensor(chosen, chosen, probs, ALU.not_equal))
            st.done(dve.tensor_tensor(chosen, chosen, probs, ALU.mult))
            st.done(dve.tensor_reduce(r_sum[:, :, 0], chosen, AX, ALU.add))
            st.done(dve.tensor_scalar(r_sum, r_sum, 1e-9, None, ALU.add))
            st.done(dve.reciprocal(r_sum, r_sum))
            st.done(dve.tensor_tensor(weight_of[:, :, 0:E1], chosen, r_sum.to_broadcast([P, NT, E1]), ALU.mult))
            st.done(dve.tensor_scalar(weight_of[:, :, 0:E1 + 1], weight_of[:, :, 0:E1 + 1], gates[:, 3:4], None, ALU.mult))
            dve.wait_ge(s_turned, 25)
            experts_vector(dve, st, E1 + 1, 0)

        scratch.restart()
        scratch.at = 1280
        attn_region.restart()
        HQ = 4
        QC = P // (HQ * HD2)
        NQ = H2 // HQ
        W = HQ * HD2
        SELF = C * HQ
        CROSS = C
        TU = SELF + CROSS
        BU = TB * TU
        LAG = 4
        l2_w = attn_region.take([P, 6, C, D])
        l2_ctxT2 = attn_region.take([P, C, B, P])
        l2_cos = attn_region.take([P, S])
        l2_sin = attn_region.take([P, S])
        eight_of = attn_region.take([P, HQ, 2])
        l2_head_of = attn_region.take([P, H2 // C])
        l2_gate = attn_region.take([P, H2])
        l2_kT = attn_region.take([P, C, S])
        l2_akT = attn_region.take([P, C, CT])
        l2_av = attn_region.take([P, B, D])
        l2_kdiag = attn_region.take([P, C, HQ, 2, S])
        l2_akdiag = attn_region.take([P, C, H2 // C, SK])
        l2_vwide = attn_region.take([P, W + TB * H2 * W])
        l2_avwide = attn_region.take([P, W + H2 // 2 * W])
        l2_v_at = l2_vwide[:, W:].rearrange("p (n w) -> p n w", w=W)
        l2_av_at = l2_avwide[:, W:].rearrange("p (n w) -> p n w", w=W)
        l2_mask = attn_region.take([P, TB, S])
        l2_qT = attn_region.take([P, C, S])
        l2_rot = scratch.take([P, 2, 2, C * S])
        l2_rep = scratch.take([P, 2, D])
        l2_raw = scratch.take([P, 2, C, P])
        l2_oT = scratch.take([P, C, S])
        l2_prob = attn_region.take([P, LAG, 1024])
        l2_probT = scratch.take([P, 2, 8, P])
        l2_halves = scratch.take([P, H2 // 2, SK // 2])
        l2_max = attn_region.take([P, LAG, HQ])
        l2_neg = attn_region.take([P, LAG, HQ])
        l2_cmax = attn_region.take([P, LAG, H2 // 2])
        l2_sum = attn_region.take([P, TB, H2])
        l2_csum = attn_region.take([P, TB, H2])

        s_l2_load = sem("l2_load")
        s_mask = sem("mask_loaded")
        s_mask_ok = sem("mask_clamped")
        s_l2_ctx = sem("l2_context_projected")
        s_l2_ctx_out = sem("l2_context_out")
        s_l2_qk = sem("l2_qk_projected")
        s_l2_v = sem("l2_v_projected")
        s_l2_v_out = sem("l2_v_out")
        s_l2_mul = sem("l2_qk_multiplied")
        s_l2_rot = sem("l2_qk_rotated")
        s_l2_diag = sem("l2_diag_ready")
        s_l2_zero = sem("l2_zeros_set")
        s_ptT_b = sem("probs_turned_second_half")
        s_pt_b = sem("probs_turn_out_second_half")
        s_csum = sem("l2_context_sums_ready")
        s_rep = sem("l2_inverse_sums_ready")
        s_repT = sem("l2_inverse_sums_turned")
        s_oT = sem("l2_heads_ready")

        l2_sc = [bank(1, 2), bank(3, 2)]
        l2_pt_ps = [bank(5), bank(6)]
        l2_o_ps = bank(7).rearrange("p (a c q) -> p a c q", a=2, c=C)
        l2_repT_ps = bank(0)
        l2_y_ps = bank(0)[:, 0:D]
        U0 = 2 * NT
        PV0 = NT
        O0 = NT
        V0 = 2 * NT
        HALF = BANK // P

        L2_LOADS = 7

        def l2_attn_sync(sp):
            sp.wait_ge(s_res, 3 * NT + 1)
            for dst, name in ((l2_w, "l2_w"), (l2_ctxT2, "ctxT2"), (l2_cos, "l2_cos"), (l2_sin, "l2_sin"),
                              (eight_of, "eight_of"), (l2_head_of, "l2_head_of"), (l2_gate, "l2_gate")):
                sp.dma_start(dst, A[name]).then_inc(s_l2_load, 16)
            f2_weights_sync(sp)
            l3_context_sync(sp)
            with sp.Fori(0, B) as i:
                sp.wait_ge(s_shift, i * BU + (U0 - CROSS + 1))
                sp.dma_start(l2_mask, A["mask"][:, bass.ds(i * TB, TB), :]).then_inc(s_mask, 16)

        def l2_attn_gpsimd(pool):
            for signal, start in ((s_ptT_b, LAG), (s_pt_b, 1), (s_csum, 1), (s_repT, 1), (s_oT, 1),
                                  (s_l2_mul, 1)):
                pool.sem_inc(signal, start)
            pool.wait_ge(s_res, 3 * NT + 1)
            pool.memset(l2_vwide, 0.0).then_inc(s_l2_zero, 1)
            pool.memset(l2_avwide, 0.0).then_inc(s_l2_zero, 1)
            pool.wait_ge(s_l2_load, 16 * L2_LOADS)
            pool.wait_ge(s_l2_ctx_out, 2)
            pool.wait_ge(s_l2_zero, 2)
            st = Steps(pool, s_pool)

            def clamp_mask(b):
                pool.wait_ge(s_mask, b * 16 + 16)
                settle(pool)
                pool.tensor_scalar(l2_mask, l2_mask, float(np.finfo(np.float32).min), None, ALU.max).then_inc(s_mask_ok, 1)

            def rotated(b, a, dst):
                pool.tensor_tensor(flat(dst), l2_rot[:, a, 0, :], l2_rot[:, a, 1, :], ALU.add).then_inc(s_l2_rot, 1)

            def prepare(b, first):
                if first:
                    rotated(b, 0, l2_qT)
                pool.wait_ge(s_l2_mul, b * 4 + 5)
                rotated(b, 1, l2_kT)
                pool.wait_ge(s_l2_rot, b * 2 + (3 if first else 2))
                for c in range(C):
                    for h in range(HQ):
                        pool.wait_ge(s_score, b * BU + (U0 - TU + HQ * c + h + 2))
                        pool.tensor_tensor(l2_kdiag[:, c, h, :, :], l2_kT[:, c:c + 1, :].to_broadcast([P, 2, S]),
                                           eight_of[:, h, :].unsqueeze(2).to_broadcast([P, 2, S]), ALU.mult).then_inc(s_l2_diag, 1)
                pool.wait_ge(s_score, b * BU + (U0 + 1))
                if not first:
                    rotated(b, 0, l2_qT)
                    clamp_mask(b)
                for c in range(C):
                    pool.tensor_tensor(l2_akdiag[:, c, :, :],
                                       l2_akT[:, c:c + 1, bass.ds(b * SK, SK)].to_broadcast([P, H2 // C, SK]),
                                       l2_head_of.unsqueeze(2).to_broadcast([P, H2 // C, SK]), ALU.mult).then_inc(s_l2_diag, 1)

            def context_sums(i, j):
                for c in range(CROSS):
                    u = TU * j + SELF + c
                    pool.wait_ge(s_exp, i * BU + (U0 + u + 1))
                    pool.wait_ge(s_csum, i * TB * CROSS + (1 + CROSS * j + c))
                    part = l2_prob[:, u % LAG, :].rearrange("p (h k) -> p h k", k=SK)
                    width = SK // 2
                    while width > 1:
                        half = l2_halves[:, :, 0:width]
                        st.done(pool.tensor_tensor(half, part[:, :, 0:width], part[:, :, width:2 * width], ALU.add))
                        part, width = half, width // 2
                    pool.tensor_tensor(l2_csum[:, j, 16 * c:16 * c + 16].unsqueeze(2), part[:, :, 0:1], part[:, :, 1:2],
                                       ALU.add).then_inc(s_csum, 1)

            def batch(i, more):
                if more:
                    ln_gpsimd(pool, i + 1 + 4 * B)
                context_sums(i, 0)
                if more:
                    prepare(i + 1, False)
                context_sums(i, 1)

            ln_gpsimd(pool, 4 * B)
            f2_weights_gpsimd(pool)
            clamp_mask(0)
            pool.wait_ge(s_l2_mul, 3)
            prepare(0, True)
            with pool.Fori(0, B - 1) as i:
                st.loop(i, TB * CROSS * 5)
                batch(i, True)
            st.end_loop(B - 1)
            batch(B - 1, False)

        def l2_attn_tensor(pe, turns):
            pe.wait_ge(s_l2_load, 16 * L2_LOADS)
            pe.wait_ge(s_res, 4 * NT + 1)
            for m in range(C):
                for c in range(C):
                    ins = pe.matmul(bank(1)[:, m * CT:(m + 1) * CT], l2_w[:, 2, c, m * P:(m + 1) * P], ctxT[:, c, :],
                                    start=(c == 0), stop=(c == C - 1))
            ins.then_inc(s_l2_ctx, 1)
            for b in range(B):
                for c in range(C):
                    ins = pe.matmul(bank(3, 2)[:, b * D:(b + 1) * D], l2_ctxT2[:, c, b, :], l2_w[:, 4, c, :],
                                    start=(c == 0), stop=(c == C - 1))
            ins.then_inc(s_l2_ctx, 1)
            pe.wait_ge(s_l2_ctx_out, 2)

            def turn(b):
                pe.wait_ge(s_ln_norm, b + 4 * B + 1)
                turn_batch(pe, turns, xn)

            def project(b, a):
                pe.wait_ge(s_turn_out, turns.now())
                pe.wait_ge(s_l2_mul, b * 4 + a + 1)
                for m in range(C):
                    for c in range(C):
                        ins = pe.matmul(bank(0)[:, m * S:(m + 1) * S], l2_w[:, a, c, m * P:(m + 1) * P],
                                        xT[:, c, :], start=(c == 0), stop=(c == C - 1))
                ins.then_inc(s_l2_qk, 1)

            def project_values(b):
                for m in range(TB):
                    for c in range(C):
                        ins = pe.matmul(bank(5)[:, m * D:(m + 1) * D], xT[:, c, m * P:(m + 1) * P], l2_w[:, 4, c, :],
                                        start=(c == 0), stop=(c == C - 1))
                ins.then_inc(s_l2_v, 1)

            def batch(i, more):
                def scores(u):
                    j, k = u % BU // TU, u % TU
                    pe.wait_ge(s_shift, i * BU + (U0 + u))
                    c = k // HQ if k < SELF else k - SELF
                    if j == 0:
                        pe.wait_ge(s_l2_diag, i * TU + (u // BU * TU + k + 1))
                        pe.wait_ge(s_l2_rot, i * 2 + (u // BU * 2 + 3))
                    for n in range(2):
                        if k < SELF:
                            rows = slice(2 * W * n, 2 * W * n + 2 * W)
                            keys = l2_kdiag[rows, c, k % HQ, :, :].rearrange("p a k -> p (a k)")
                        else:
                            rows = slice(0, P)
                            keys = l2_akdiag[:, c, 8 * n:8 * n + 8, :].rearrange("p h k -> p (h k)")
                        ins = pe.matmul(l2_sc[u % 2][:, n * BANK:(n + 1) * BANK], l2_qT[rows, c, j * P:(j + 1) * P], keys,
                                        start=True, stop=True)
                    ins.then_inc(s_score, 1)

                def turn_probs(u):
                    pe.wait_ge(s_exp, i * BU + (U0 + u + 1))
                    pe.wait_ge(s_pt, i * BU + (U0 + u) + 1)
                    for g in range(HALF):
                        ins = pe.transpose(l2_pt_ps[0][:, g * P:(g + 1) * P], l2_prob[:, u % LAG, g * P:(g + 1) * P], ident[:, :])
                    ins.then_inc(s_ptT, 1)
                    pe.wait_ge(s_pt_b, i * BU + (u + 1))
                    for g in range(HALF):
                        ins = pe.transpose(l2_pt_ps[1][:, g * P:(g + 1) * P], l2_prob[:, u % LAG, (HALF + g) * P:(HALF + g + 1) * P],
                                           ident[:, :])
                    ins.then_inc(s_ptT_b, 1)

                def weigh(u):
                    j, k = u // TU, u % TU
                    pe.wait_ge(s_pt, i * BU + (U0 + u + 2))
                    pe.wait_ge(s_pt_b, i * BU + (u + 2))
                    if k == 0:
                        pe.wait_ge(s_o, i * TB + (O0 + j) + 1)
                    for e in range(2):
                        for g in range(QC):
                            rows = slice(W * g, W * g + W)
                            if k < SELF:
                                c, h = k // HQ, k % HQ
                                at = W * (1 + e * H2 + 16 * c + HQ * g + h) - HD2 * h
                                ins = pe.matmul(l2_o_ps[rows, 0, c, :], l2_vwide[:, at:at + W], l2_probT[:, u % 2, 2 * g + e, :],
                                          start=(h == 0 and e == 0), stop=(h == HQ - 1 and e == 1))
                            else:
                                c = k - SELF
                                at = W * (1 + 8 * c + 2 * g + e) - 2 * HD2 * e
                                ins = pe.matmul(l2_o_ps[rows, 1, c, :], l2_avwide[:, at:at + W], l2_probT[:, u % 2, 2 * g + e, :],
                                          start=(e == 0), stop=(e == 1))
                    ins.then_inc(s_pv, 1)

                def turn_sums(j):
                    pe.wait_ge(s_rep, i * TB + (j + 1))
                    if j:
                        pe.wait_ge(s_res, i * TB + (4 * NT + j) + 1)
                    for g in range(2 * C):
                        ins = pe.transpose(l2_repT_ps[:, g * P:(g + 1) * P], flat(l2_rep)[:, g * P:(g + 1) * P], ident[:, :])
                    ins.then_inc(s_repT, 1)

                def result(j):
                    pe.wait_ge(s_oT, i * TB + (j + 2))
                    for c in range(C):
                        ins = pe.matmul(l2_y_ps, l2_oT[:, c, j * P:(j + 1) * P], l2_w[:, 5, c, :],
                                        start=(c == 0), stop=(c == C - 1))
                    ins.then_inc(s_y, 1)

                if i is None:
                    i = 0
                    scores(0)
                    scores(1)
                    return
                pe.wait_ge(s_l2_v_out, i + 1)
                for u in range(BU + 1):
                    if u < BU and (more or u + 2 < BU):
                        scores(u + 2)
                    if u < BU:
                        turn_probs(u)
                    if u >= 1:
                        weigh(u - 1)
                    if more and u == 2:
                        pe.wait_ge(s_res, i * TB + 4 * NT + 1)
                        turn(i + 1)
                    if more and 4 <= u < 8:
                        project(i + 1, u - 4)
                    if not more and u == 0:
                        pe.wait_ge(s_res, i * TB + 4 * NT + 1)
                        f2_weights_tensor(pe, bank(0)[:, 0:2])
                    if u == TU + 1:
                        turn_sums(0)
                    if u == TU + 3:
                        result(0)
                if more:
                    project_values(i + 1)
                turn_sums(1)
                result(1)

            turn(0)
            for a in range(4):
                project(0, a)
            project_values(0)
            batch(None, True)
            with pe.Fori(0, B - 1) as i:
                turns.loop(i, 1)
                batch(i, True)
            turns.end_loop(B - 1)
            batch(B - 1, False)

        def l2_attn_scalar(act, turns):
            act.wait_ge(s_l2_load, 16 * L2_LOADS)
            act.activation(l2_gate, l2_gate, ACT.Tanh).then_inc(s_act_own, 1)
            act.wait_ge(s_l2_ctx, 1)
            act.activation(flat(l2_akT), bank(1), ACT.Copy).then_inc(s_l2_ctx_out, 1)
            act.wait_ge(s_l2_ctx, 2)
            act.activation(flat(l2_av), bank(3, 2), ACT.Copy).then_inc(s_l2_ctx_out, 1)
            act.wait_ge(s_l2_zero, 2)
            act.wait_ge(s_l2_ctx_out, 2)

            def values_out(b):
                act.wait_ge(s_l2_v, b + 1)
                act.activation(l2_v_at[:, :, 0:HD2], bank(5).rearrange("p (n d) -> p n d", d=HD2), ACT.Copy)
                for half in range(2):
                    rows = slice(half * SK, half * SK + SK)
                    ins = act.activation(l2_av_at[rows, :, half * HD2:half * HD2 + HD2],
                                         tile_of(l2_av, b)[rows, :].rearrange("p (n a d) -> p n a d", a=2, d=HD2)[:, :, half, :], ACT.Copy)
                ins.then_inc(s_l2_v_out, 1)

            def batch(i, more):
                def exps(u):
                    j, k = u % BU // TU, u % TU
                    act.wait_ge(s_shift, i * BU + (U0 + u + 2))
                    if k < SELF:
                        for g in range(QC):
                            h = 16 * (k // HQ) + HQ * g + k % HQ
                            ins = act.activation(l2_prob[:, u % LAG, g * S:(g + 1) * S], l2_prob[:, u % LAG, g * S:(g + 1) * S],
                                                 ACT.Exp, bias=l2_neg[:, u % LAG, g:g + 1],
                                                 accum_out=l2_sum[:, j, h:h + 1])
                    else:
                        ins = act.activation(l2_prob[:, u % LAG, :], l2_prob[:, u % LAG, :], ACT.Exp)
                    ins.then_inc(s_exp, 1)

                def evac(u):
                    act.wait_ge(s_ptT, i * BU + (U0 + u + 2))
                    act.wait_ge(s_pv, i * BU + (PV0 + u))
                    act.activation(l2_probT[:, u % 2, 0:HALF, :].rearrange("p g q -> p (g q)"), l2_pt_ps[0], ACT.Copy).then_inc(s_pt, 1)
                    if u % TU >= SELF:
                        act.wait_ge(s_ptT_b, i * BU + (u + 1 + LAG))
                        act.activation(l2_probT[:, u % 2, HALF:, :].rearrange("p g q -> p (g q)"), l2_pt_ps[1],
                                       ACT.Copy).then_inc(s_pt_b, 1)

                def products_out(j):
                    act.wait_ge(s_pv, i * BU + (PV0 + TU * (j + 1)) + 1)
                    act.wait_ge(s_oT, i * TB + (j + 1))
                    act.activation(l2_raw.rearrange("p a c q -> p (a c q)"), bank(7), ACT.Copy).then_inc(s_o, 1)

                if i is None:
                    i = 0
                    exps(0)
                    exps(1)
                    return
                for u in range(BU):
                    evac(u)
                    if more or u + 2 < BU:
                        exps(u + 2)
                    if more and u == 2:
                        turn_evac(act, turns, xT)
                    if u == TU:
                        products_out(0)
                products_out(1)
                if more:
                    values_out(i + 1)

            turn_evac(act, turns, xT)
            f2_weights_scalar(act)
            values_out(0)
            batch(None, True)
            with act.Fori(0, B - 1) as i:
                turns.loop(i, 1)
                batch(i, True)
            turns.end_loop(B - 1)
            batch(B - 1, False)

        s_act_own = sem("l2_gate_set")

        def l2_attn_vector(dve, st):
            dve.wait_ge(s_l2_load, 16 * L2_LOADS)
            dve.wait_ge(s_act_own, 1)

            def normalise(b):
                ln_vector(dve, st, b, b + 4 * B)
                ln_apply(dve, b, b + 25)

            def multiply(b, a):
                if a == 0:
                    dve.wait_ge(s_l2_rot, b * 2 + 1)
                dve.wait_ge(s_l2_qk, b * 4 + a + 1)
                dve.scalar_tensor_tensor(out=l2_rot[:, a // 2, a % 2, :].rearrange("p (c s) -> p c s", c=C),
                                         in0=bank(0).rearrange("p (c s) -> p c s", c=C), scalar=HD2 ** -0.5 if a < 2 else 1.0,
                                         in1=(l2_cos, l2_sin)[a % 2].unsqueeze(1).to_broadcast([P, C, S]),
                                         op0=ALU.mult, op1=ALU.mult).then_inc(s_l2_mul, 1)

            def batch(i, more):
                def shift(u):
                    j, k = u % BU // TU, u % TU
                    if u % BU == 0:
                        dve.wait_ge(s_mask_ok, i + (u // BU + 1))
                    dve.wait_ge(s_score, i * BU + (U0 + u + 2))
                    dve.wait_ge(s_ptT_b, i * BU + (u + 1))
                    if u in (2, TU + 2, TU + 3):
                        dve.wait_ge(s_csum, i * TB * CROSS + (1 if u == 2 else u - TU))
                    if k < SELF:
                        settle(dve)
                        for g in range(QC):
                            st.mark(dve.tensor_tensor_reduce(out=l2_prob[:, u % LAG, g * S:(g + 1) * S],
                                                             in0=l2_sc[u % 2][:, g * S:(g + 1) * S], in1=l2_mask[:, j, :],
                                                             scale=1.0, scalar=float(np.finfo(np.float32).min),
                                                             op0=ALU.add, op1=ALU.max, accum_out=l2_max[:, u % LAG, g:g + 1]))
                        st.wait()
                        dve.tensor_scalar(l2_neg[:, u % LAG, :], l2_max[:, u % LAG, :], -1.0, None, ALU.mult).then_inc(s_shift, 1)
                    else:
                        heads = lambda v: v.rearrange("p (h k) -> p h k", k=SK)
                        st.done(dve.tensor_reduce(l2_cmax[:, u % LAG, :], heads(l2_sc[u % 2]), AX, ALU.max))
                        dve.tensor_tensor(heads(l2_prob[:, u % LAG, :]), heads(l2_sc[u % 2]),
                                          l2_cmax[:, u % LAG, :].unsqueeze(2).to_broadcast([P, H2 // 2, SK]), ALU.subtract).then_inc(s_shift, 1)

                def evac_second(u):
                    if u % TU < SELF:
                        dve.wait_ge(s_ptT_b, i * BU + (u + 1 + LAG))
                        dve.wait_ge(s_pv, i * BU + (PV0 + u))
                        dve.tensor_copy(l2_probT[:, u % 2, HALF:, :].rearrange("p g q -> p (g q)"), l2_pt_ps[1]).then_inc(s_pt_b, 1)

                def inverse_sums(j):
                    wide = lambda v: v[:, j, :].unsqueeze(2).to_broadcast([P, H2, HD2])
                    dve.wait_ge(s_exp, i * BU + (U0 + TU * (j + 1)))
                    dve.wait_ge(s_csum, i * TB * CROSS + (1 + CROSS * (j + 1)))
                    st.mark(dve.reciprocal(l2_sum[:, j, :], l2_sum[:, j, :]))
                    st.done(dve.reciprocal(l2_csum[:, j, :], l2_csum[:, j, :]))
                    st.done(dve.tensor_tensor(l2_csum[:, j, :], l2_csum[:, j, :], l2_gate, ALU.mult))
                    dve.wait_ge(s_repT, i * TB + (j + 1))
                    dve.tensor_copy(l2_rep[:, 0, :].rearrange("p (h d) -> p h d", h=H2), wide(l2_sum))
                    dve.tensor_copy(l2_rep[:, 1, :].rearrange("p (h d) -> p h d", h=H2), wide(l2_csum)).then_inc(s_rep, 1)

                def scale_products(j):
                    dve.wait_ge(s_o, i * TB + (O0 + j + 2))
                    dve.wait_ge(s_repT, i * TB + (j + 2))
                    st.done(dve.tensor_tensor(l2_raw.rearrange("p a c q -> p (a c q)"), l2_raw.rearrange("p a c q -> p (a c q)"),
                                              l2_repT_ps, ALU.mult))
                    dve.tensor_tensor(l2_oT[:, :, j * P:(j + 1) * P], l2_raw[:, 0, :, :], l2_raw[:, 1, :, :],
                                      ALU.add).then_inc(s_oT, 1)

                def add_result(j):
                    dve.wait_ge(s_y, i * TB + (V0 + j + 1))
                    dve.scalar_tensor_tensor(out=tile_of(x, i * TB + j), in0=l2_y_ps, scalar=gates[:, 4:5],
                                             in1=tile_of(x, i * TB + j), op0=ALU.mult, op1=ALU.add).then_inc(s_res, 1)

                if i is None:
                    i = 0
                    shift(0)
                    shift(1)
                    return
                for u in range(BU):
                    if more or u + 2 < BU:
                        shift(u + 2)
                    evac_second(u)
                    if more and u == 0:
                        normalise(i + 1)
                    if more and 4 <= u < 8:
                        multiply(i + 1, u - 4)
                    if not more and 1 <= u <= F2_WEIGHT_STEPS:
                        f2_weights_vector(dve, st, u - 1, bank(0))
                    if u == TU:
                        inverse_sums(0)
                    if u == TU + 2:
                        scale_products(0)
                    if u == TU + 4:
                        add_result(0)
                inverse_sums(1)
                scale_products(1)
                add_result(1)

            normalise(0)
            for a in range(4):
                multiply(0, a)
            batch(None, True)
            with dve.Fori(0, B - 1) as i:
                st.loop(i, 4 + TB * (SELF * QC + CROSS + 4))
                batch(i, True)
            st.end_loop(B - 1)
            batch(B - 1, False)

        scratch.restart()
        ffn_region.restart()
        K2 = (I2 + P - 1) // P
        ROUND = 1.5 * 2.0 ** 23
        f2_gate = ffn_region.take([P, C * 2 * I2])
        f2_down = ffn_region.take([P, K2 * D])
        f2_gate_q = ffn_region.take([P, C, 2 * I2], BF16)
        f2_down_q = ffn_region.take([P, K2, D], BF16)
        f2_norm = scratch.take([P, D])
        f2_dnorm = scratch.take([P, I2])
        ident_b = scratch.take([P, P], BF16)
        ones_sq = scratch.take([P, P])
        w_sum = scratch.take([P, 2])
        w_mean = scratch.take([P, 2])
        w_scale = scratch.take([P, 2])
        f2_junk = scratch.take([P, TB, I2])
        f2_xjunk = scratch.take([P, TB, D])
        row_ss = scratch.take([P, TB])
        row_rms = scratch.take([P, TB])
        row_max = scratch.take([P, TB])
        row_q = scratch.take([P, TB])
        row_y = scratch.take([P, TB])
        row_half = scratch.take([P, TB])
        row_sq = scratch.take([P, TB])
        hrow_ss = scratch.take([P, TB])
        hrow_rms = scratch.take([P, TB])
        hrow_max = scratch.take([P, TB])
        hrow_q = scratch.take([P, TB])
        hrow_y = scratch.take([P, TB])
        f2_xq = scratch.take([P, TB, D], BF16)
        f2_xqT = scratch.take([P, C, S], BF16)
        f2_act = scratch.take([P, TB, I2])
        f2_hq = scratch.take([P, TB, I2], BF16)
        f2_hqT = scratch.take([P, K2, P], BF16)

        s_f2_load = sem("f2_load")
        s_wsum = sem("weights_summed")
        s_wmean = sem("weight_sums_spread")
        s_xrow_ss = sem("x_row_squares_summed")
        s_xrow_ms = sem("x_row_mean_square_ready")
        s_xrow_rms = sem("x_row_rms_ready")
        s_row_ss = sem("row_squares_summed")
        s_row_ms = sem("row_mean_square_ready")
        s_row_rms = sem("row_rms_ready")
        s_row_norm = sem("rows_normalised")
        s_xq = sem("rows_quantised")
        s_h2 = sem("f2_hidden_ready")
        s_hq = sem("hidden_quantised")

        turn_b = bank(0).bitcast(BF16)
        hq_ps = bank(5).bitcast(BF16)

        def f2_weights_sync(sp):
            sp.wait_ge(s_res, 4 * NT + 1)
            sp.dma_start(f2_gate, A["f2_gate"]).then_inc(s_f2_load, 16)
            sp.dma_start(f2_down, A["f2_down"]).then_inc(s_f2_load, 16)
            sp.dma_start(f2_norm, A["f2_norm"]).then_inc(s_f2_load, 16)
            sp.dma_start(f2_dnorm, A["f2_dnorm"]).then_inc(s_f2_load, 16)

        def f2_weights_gpsimd(pool):
            pool.wait_ge(s_res, 4 * NT + 1)
            pool.memset(ones_sq, 1.0).then_inc(s_wsum, 1)

        def f2_weights_scalar(act):
            act.wait_ge(s_f2_load, 64)
            act.activation(f2_gate_q.rearrange("p c n -> p (c n)"), f2_gate, ACT.Abs, accum_out=w_sum[:, 0:1])
            act.activation(f2_down_q.rearrange("p c n -> p (c n)"), f2_down, ACT.Abs, accum_out=w_sum[:, 1:2]).then_inc(s_wsum, 1)
            act.activation(ident_b, ident[:, :], ACT.Copy).then_inc(s_wsum, 1)

        def f2_weights_tensor(pe, ps):
            pe.wait_ge(s_wsum, 3)
            pe.matmul(ps, ones_sq, w_sum, start=True, stop=True).then_inc(s_wmean, 1)

        F2_WEIGHT_STEPS = 7

        def f2_weights_vector(dve, st, step, ps):
            if step == 0:
                dve.wait_ge(s_wmean, 1)
                for k, size in enumerate((2 * I2 * D, I2 * D)):
                    st.mark(dve.tensor_scalar(w_mean[:, k:k + 1], ps[:, k:k + 1], 1.0 / size, 1e-5, ALU.mult, ALU.max))
                st.wait()
                st.done(dve.reciprocal(w_scale, w_mean))
                return
            k, op = (step - 1) // 3, (step - 1) % 3
            w, whole = ((f2_gate, f2_gate_q), (f2_down, f2_down_q))[k]
            if op == 0:
                ins = dve.tensor_scalar(w, w, w_scale[:, k:k + 1], ROUND, ALU.mult, ALU.add)
            elif op == 1:
                ins = dve.tensor_scalar(w, w, ROUND, 1.0, ALU.subtract, ALU.min)
            else:
                ins = dve.tensor_scalar(whole.rearrange("p c n -> p (c n)"), w, -1.0, None, ALU.max)
            st.done(ins)

        def l2_ffn_sync(sp):
            pass

        def l2_ffn_gpsimd(pool):
            def power(v, ready, made, n):
                pool.wait_ge(ready, n)
                pool.tensor_tensor(v, v, minus_half[:, 0:v.shape[1]], ALU.pow).then_inc(made, 1)

            def batch(i, more):
                if more:
                    ln_gpsimd(pool, i + 1 + 5 * B)
                power(hrow_rms[:, 0:1], s_row_ms, s_row_rms, i * TB + 1)
                if more:
                    power(row_rms, s_xrow_ms, s_xrow_rms, i + 2)
                power(hrow_rms[:, 1:2], s_row_ms, s_row_rms, i * TB + 2)

            ln_gpsimd(pool, 5 * B)
            power(row_rms, s_xrow_ms, s_xrow_rms, 1)
            with pool.Fori(0, B - 1) as i:
                batch(i, True)
            batch(B - 1, False)

        def l2_ffn_tensor(pe, turns):
            pe.wait_ge(s_res, 5 * NT + 1)
            l3_context_tensor(pe)

            def turn_rows(b):
                pe.wait_ge(s_xq, b + 2)
                pe.wait_ge(s_turn_out, turns.now())
                for c in range(C):
                    for j in range(TB):
                        ins = pe.transpose(turn_b[:, c * S + j * P:c * S + (j + 1) * P], f2_xq[:, j, c * P:(c + 1) * P], ident_b)
                ins.then_inc(s_turned, 1)
                turns.k += 1
                pe.wait_ge(s_turn_out, turns.now())

            def gate_up(i, j):
                pe.wait_ge(s_h2, i * TB + j + 1)
                for a, ps, ready in ((0, gate_ps, s_gate), (1, up_ps, s_up)):
                    for n0, n1 in ((0, BANK), (BANK, I2)):
                        for c in range(C):
                            ins = pe.matmul(ps[:, n0:n1], f2_xqT[:, c, j * P:(j + 1) * P],
                                            f2_gate_q[:, c, a * I2 + n0:a * I2 + n1], start=(c == 0), stop=(c == C - 1))
                    ins.then_inc(ready, 1)

            def down(i, j):
                pe.wait_ge(s_hq, i * TB + j + 1)
                pe.wait_ge(s_ht, i * TB + (NT + j) + 1)
                for k in range(K2):
                    w = min(P, I2 - k * P)
                    ins = pe.transpose(hq_ps[0:w, k * P:(k + 1) * P], f2_hq[:, j, k * P:k * P + w], ident_b)
                ins.then_inc(s_htT, 1)
                pe.wait_ge(s_ht, i * TB + (NT + j + 2))
                pe.wait_ge(s_res, i * TB + (5 * NT + j) + 1)
                for k in range(K2):
                    w = min(P, I2 - k * P)
                    ins = pe.matmul(y_ps, f2_hqT[0:w, k, :], f2_down_q[0:w, k, :], start=(k == 0), stop=(k == K2 - 1))
                ins.then_inc(s_fy, 1)

            def batch(i, more):
                gate_up(i, 1)
                down(i, 0)
                if more:
                    turn_rows(i + 1)
                    gate_up(i + 1, 0)
                down(i, 1)

            turn_rows(0)
            gate_up(0, 0)
            with pe.Fori(0, B - 1) as i:
                turns.loop(i, 1)
                batch(i, True)
            turns.end_loop(B - 1)
            batch(B - 1, False)

        def l2_ffn_scalar(act, turns):
            act.wait_ge(s_res, 5 * NT + 1)
            l3_context_scalar(act)

            def row_squares(b):
                act.wait_ge(s_ln_norm, b + 5 * B + 1)
                for j in range(TB):
                    ins = act.activation(f2_xjunk[:, j, :], xn[:, j, :], ACT.Square, accum_out=row_ss[:, j:j + 1])
                ins.then_inc(s_xrow_ss, 1)

            def rows_turned():
                act.wait_ge(s_turned, turns.now() + 1)
                act.activation(f2_xqT.rearrange("p c s -> p (c s)"), turn_b[:, 0:C * S], ACT.Copy).then_inc(s_turn_out, 1)
                turns.k += 1

            def tanh(i, j):
                act.wait_ge(s_gate, i * TB + (NT + j + 1))
                act.activation(f2_act[:, j, :], gate_ps[:, 0:I2], ACT.Tanh, scale=row_half[:, j:j + 1]).then_inc(s_act, 1)

            def hidden_squares(i, j):
                act.wait_ge(s_h2, i * TB + j + 2)
                act.activation(f2_junk[:, j, :], f2_act[:, j, :], ACT.Square, accum_out=hrow_ss[:, j:j + 1]).then_inc(s_row_ss, 1)

            def hidden_turned(i, j):
                act.wait_ge(s_htT, i * TB + (NT + j + 2))
                act.wait_ge(s_fy, i * TB + (NT + j) + 1)
                act.activation(f2_hqT[:, 0:K2 - 1, :].rearrange("p k q -> p (k q)"), hq_ps[:, 0:(K2 - 1) * P], ACT.Copy)
                act.activation(f2_hqT[0:I2 % P, K2 - 1, :], hq_ps[0:I2 % P, (K2 - 1) * P:K2 * P], ACT.Copy).then_inc(s_ht, 1)

            def batch(i, more):
                hidden_squares(i, 0)
                tanh(i, 1)
                if more:
                    row_squares(i + 1)
                hidden_turned(i, 0)
                hidden_squares(i, 1)
                if more:
                    rows_turned()
                    tanh(i + 1, 0)
                hidden_turned(i, 1)

            row_squares(0)
            rows_turned()
            tanh(0, 0)
            with act.Fori(0, B - 1) as i:
                turns.loop(i, 1)
                batch(i, True)
            turns.end_loop(B - 1)
            batch(B - 1, False)

        def quantise(dve, st, v, whole, scales, low, high):
            for j, scale in enumerate(scales):
                st.mark(dve.tensor_scalar(v[j], v[j], scale, ROUND, ALU.mult, ALU.add))
            st.wait()
            for j in range(len(scales)):
                st.mark(dve.tensor_scalar(v[j], v[j], ROUND, high, ALU.subtract, ALU.min))
            st.wait()
            return [dve.tensor_scalar(whole[j], v[j], low, None, ALU.max) for j in range(len(scales))][-1]

        def l2_ffn_vector(dve, st):
            dve.engine_nop().then_inc(s_xq, 1)
            l3_context_vector(dve, st)

            def normalise(b):
                dve.wait_ge(s_ln_rstd, b + 5 * B + 1)
                ln_apply(dve, b, b + 29)

            def quantise_rows(b):
                dve.wait_ge(s_xrow_ss, b + 1)
                dve.tensor_scalar(row_rms, row_ss, 1.0 / D, 1e-5, ALU.mult, ALU.add).then_inc(s_xrow_ms, 1)
                dve.wait_ge(s_xrow_rms, b + 1)
                for j in range(TB):
                    st.mark(dve.scalar_tensor_tensor(out=xn[:, j, :], in0=xn[:, j, :], scalar=row_rms[:, j:j + 1],
                                                     in1=f2_norm, op0=ALU.mult, op1=ALU.mult))
                st.wait()
                st.done(dve.tensor_reduce(row_max, xn[:, :, :], AX, ALU.max, apply_absolute_value=True))
                st.done(dve.tensor_scalar(row_max, row_max, 1e-5, None, ALU.max))
                st.mark(dve.reciprocal(row_q, row_max))
                st.done(dve.tensor_scalar(row_y, row_max, 1.0 / 127.0, w_mean[:, 0:1], ALU.mult, ALU.mult))
                st.mark(dve.tensor_scalar(row_q, row_q, 127.0, None, ALU.mult))
                st.mark(dve.tensor_scalar(row_half, row_y, 0.5, None, ALU.mult))
                st.done(dve.scalar_tensor_tensor(out=row_sq, in0=row_y, scalar=0.5, in1=row_y, op0=ALU.mult, op1=ALU.mult))
                quantise(dve, st, [xn[:, j, :] for j in range(TB)], [f2_xq[:, j, :] for j in range(TB)],
                         [row_q[:, j:j + 1] for j in range(TB)], -128.0, 127.0).then_inc(s_xq, 1)

            def hidden(i, j):
                h = f2_act[:, j, :]
                dve.wait_ge(s_act, i * TB + (NT + j + 1))
                st.done(dve.scalar_tensor_tensor(out=h, in0=h, scalar=1.0, in1=gate_ps[:, 0:I2], op0=ALU.add, op1=ALU.mult))
                dve.wait_ge(s_up, i * TB + (NT + j + 1))
                dve.scalar_tensor_tensor(out=h, in0=h, scalar=row_sq[:, j:j + 1], in1=up_ps[:, 0:I2],
                                         op0=ALU.mult, op1=ALU.mult).then_inc(s_h2, 1)

            def quantise_hidden(i, j):
                h = f2_act[:, j, :]
                dve.wait_ge(s_row_ss, i * TB + j + 1)
                dve.tensor_scalar(hrow_rms[:, j:j + 1], hrow_ss[:, j:j + 1], 1.0 / I2, 1e-5, ALU.mult, ALU.add).then_inc(s_row_ms, 1)
                dve.wait_ge(s_row_rms, i * TB + j + 1)
                st.done(dve.scalar_tensor_tensor(out=h, in0=h, scalar=hrow_rms[:, j:j + 1], in1=f2_dnorm,
                                                 op0=ALU.mult, op1=ALU.mult))
                top1, q1, y1 = hrow_max[:, j:j + 1], hrow_q[:, j:j + 1], hrow_y[:, j:j + 1]
                st.done(dve.tensor_reduce(top1, h, AX, ALU.max, apply_absolute_value=True))
                st.done(dve.tensor_scalar(top1, top1, 1e-5, None, ALU.max))
                st.mark(dve.reciprocal(q1, top1))
                st.done(dve.tensor_scalar(y1, top1, 1.0 / 127.0, w_mean[:, 1:2], ALU.mult, ALU.mult))
                st.mark(dve.tensor_scalar(y1, y1, gates[:, 5:6], None, ALU.mult))
                st.done(dve.tensor_scalar(q1, q1, 127.0, None, ALU.mult))
                quantise(dve, st, [h], [f2_hq[:, j, :]], [q1], -128.0, 127.0).then_inc(s_hq, 1)

            def batch(i, more):
                hidden(i, 0)
                if more:
                    ln_moments(dve, st, i + 1)
                quantise_hidden(i, 0)
                if more:
                    normalise(i + 1)
                hidden(i, 1)
                if more:
                    quantise_rows(i + 1)
                quantise_hidden(i, 1)
                for j in range(TB):
                    dve.wait_ge(s_fy, i * TB + (NT + j + 2))
                    dve.scalar_tensor_tensor(out=tile_of(x, i * TB + j), in0=y_ps, scalar=hrow_y[:, j:j + 1],
                                             in1=tile_of(x, i * TB + j), op0=ALU.mult, op1=ALU.add).then_inc(s_res, 1)

            ln_moments(dve, st, 0)
            normalise(0)
            quantise_rows(0)
            with dve.Fori(0, B - 1) as i:
                st.loop(i, 4 + 9 + 4 + TB * 10)
                batch(i, True)
            st.end_loop(B - 1)
            batch(B - 1, False)

        attn_region.restart()
        l3_region = Region(sb("l3_region", [P, 3 * 1024]))
        l3_w = l3_region.take([P, 2, C, D])
        l3_in_bias = l3_region.take([P, C])
        l3_out_bias = l3_region.take([1, D])
        l3_affine = l3_region.take([P, 2, D])
        l3_decay = l3_region.take([P, 1])
        l3_in = attn_region.take([P, C, CT])
        l3_state = attn_region.take([P, C, CT])
        l3_decays = attn_region.take([P, SK])
        l3_mean = attn_region.take([P, C, B])
        l3_mean_wide = attn_region.take([P, C, B, P])
        l3_summary = attn_region.take([P, B, D])
        l3_y = attn_region.take([P, 2, TB, D])
        l3_stats = attn_region.take([P, 2, TB, 6])
        l3_mv = attn_region.take([P, 2, TB, 2])
        l3_rstd = attn_region.take([P, 2, TB, 1])

        s_l3_load = sem("l3_load")
        s_l3_in = sem("l3_context_projected")
        s_l3_in_out = sem("l3_context_out")
        s_l3_mean = sem("l3_means_ready")
        s_l3_sum = sem("l3_summary_ready")
        s_l3_sum_out = sem("l3_summary_out")

        def l3_context_sync(sp):
            for dst, name in ((l3_w, "l3_w"), (l3_in_bias, "l3_in_bias"), (l3_out_bias, "l3_out_bias"),
                              (l3_affine, "l3_affine"), (l3_decay, "l3_decay")):
                sp.dma_start(dst, A[name]).then_inc(s_l3_load, 16)

        def l3_context_tensor(pe):
            pe.wait_ge(s_l3_load, 16 * 5)
            for m in range(C):
                for c in range(C):
                    ins = pe.matmul(bank(6)[:, m * CT:(m + 1) * CT], l3_w[:, 0, c, m * P:(m + 1) * P], ctxT[:, c, :],
                                    start=(c == 0), stop=(c == C - 1))
            ins.then_inc(s_l3_in, 1)
            pe.wait_ge(s_l3_mean, 1)
            for b in range(B):
                ps = bank(1, 2)[:, b * D:(b + 1) * D]
                pe.matmul(ps, ones[:, :], l3_out_bias, start=True, stop=False)
                for c in range(C):
                    ins = pe.matmul(ps, l3_mean_wide[:, c, b, :], l3_w[:, 1, c, :], start=False, stop=(c == C - 1))
            ins.then_inc(s_l3_sum, 1)
            pe.wait_ge(s_l3_sum_out, 1)

        def l3_context_scalar(act):
            act.wait_ge(s_l3_load, 16 * 5)
            act.activation(l3_decay, l3_decay, ACT.Tanh, scale=0.5).then_inc(s_l3_in_out, 1)
            act.wait_ge(s_l3_in, 1)
            for c in range(C):
                ins = act.activation(l3_in[:, c, :], bank(6)[:, c * CT:(c + 1) * CT], ACT.Identity, bias=l3_in_bias[:, c:c + 1])
            ins.then_inc(s_l3_in_out, 1)
            act.wait_ge(s_l3_sum, 1)
            act.activation(flat(l3_summary), bank(1, 2), ACT.Copy).then_inc(s_l3_sum_out, 1)

        def l3_context_vector(dve, st):
            dve.wait_ge(s_l3_in_out, 2)
            st.done(dve.tensor_scalar(l3_decay, l3_decay, 1.0, 0.5, ALU.add, ALU.mult))
            st.done(dve.tensor_copy(l3_decays, l3_decay.to_broadcast([P, SK])))
            for c in range(C):
                for b in range(B):
                    at = slice(b * SK, (b + 1) * SK)
                    st.mark(dve.tensor_tensor_scan(l3_state[:, c, at], l3_decays, l3_in[:, c, at], 0.0, ALU.mult, ALU.add))
            st.wait()
            st.done(dve.tensor_reduce(l3_mean, l3_state.rearrange("p c (b k) -> p c b k", b=B), AX, ALU.add))
            st.done(dve.tensor_scalar(l3_mean, l3_mean, 1.0 / SK, None, ALU.mult))
            dve.tensor_copy(l3_mean_wide, l3_mean.unsqueeze(3).to_broadcast([P, C, B, P])).then_inc(s_l3_mean, 1)

        def l3_attn_sync(sp):
            pass

        def l3_attn_tensor(pe, turns):
            pass

        def l3_attn_scalar(act, turns):
            pass

        def l3_attn_gpsimd(pool):
            with pool.Fori(0, B // 2) as i:
                for k in range(4):
                    n = k % 2
                    pool.wait_ge(s_ln_var, i * 4 + (6 * B + k + 1))
                    pool.tensor_tensor(l3_rstd[:, n, :, 0], l3_mv[:, n, :, 1], minus_half[:, 0:TB], ALU.pow).then_inc(s_ln_rstd, 1)

        def l3_attn_vector(dve, st):
            def moments(n, tile):
                for j in range(TB):
                    st.mark(dve.bn_stats(l3_stats[:, n, j, :], tile(j)))
                st.wait()
                settle(dve)
                for j in range(TB):
                    st.mark(dve.bn_aggr(l3_mv[:, n, j, :], l3_stats[:, n, j, :]))
                st.wait()
                dve.tensor_scalar(l3_mv[:, n, :, 1:2], l3_mv[:, n, :, 1:2], 1e-5, None, ALU.add).then_inc(s_ln_var, 1)

            def normalised(i, k, n, tile):
                dve.wait_ge(s_ln_rstd, i * 4 + (6 * B + k + 1))
                for j in range(TB):
                    st.mark(dve.tensor_scalar(l3_y[:, n, j, :], tile(j), l3_mv[:, n, j, 0:1], l3_rstd[:, n, j, :],
                                              ALU.subtract, ALU.mult))
                st.wait()

            dve.wait_ge(s_l3_sum_out, 1)
            with dve.Fori(0, B // 2) as i:
                st.loop(i, 2 * (4 + 2 + 1 + 4 + 2 + 2))
                for n in range(2):
                    moments(n, lambda j: tile_of(x, i * (2 * TB) + (n * TB + j)))
                for n in range(2):
                    normalised(i, n, n, lambda j: tile_of(x, i * (2 * TB) + (n * TB + j)))
                    summary = l3_summary[:, bass.ds(i * 2 + n, 1), :].to_broadcast([P, TB, D])
                    st.done(dve.tensor_tensor(l3_y[:, n, :, :], l3_y[:, n, :, :], summary, ALU.add))
                    moments(n, lambda j: l3_y[:, n, j, :])
                for n in range(2):
                    normalised(i, 2 + n, n, lambda j: l3_y[:, n, j, :])
                    for k, op in enumerate((ALU.mult, ALU.add)):
                        st.done(dve.tensor_tensor(l3_y[:, n, :, :], l3_y[:, n, :, :],
                                                  l3_affine[:, k:k + 1, :].to_broadcast([P, TB, D]), op))
                    for j in range(TB):
                        t = i * (2 * TB) + (n * TB + j)
                        dve.scalar_tensor_tensor(out=tile_of(x, t), in0=l3_y[:, n, j, :], scalar=gates[:, 6:7],
                                                 in1=tile_of(x, t), op0=ALU.mult, op1=ALU.add).then_inc(s_res, 1)
                dve.wait_ge(s_res, i * (2 * TB) + (6 * NT + 2 * TB) + 1)
            st.end_loop(B // 2)

        scratch.restart()
        scratch.at = moe_mark
        ffn_region.restart()
        f3_expert_w = ffn_region.take([P, SLOTS, 3 * D])
        EZ = E3 + Z3
        f3_router = scratch.take([P, C, EZ])
        f3_bias = scratch.take([P, EZ])
        earlier = scratch.take([P, P])
        all_ones = scratch.take([P, P])
        c_prob = scratch.take([P, NT, EZ])
        c_biased = scratch.take([P, NT, EZ])
        c_rest = scratch.take([P, NT, EZ])
        c_eight = scratch.take([P, NT, 8])
        c_sum = scratch.take([P, NT, 1])
        c_idle = scratch.take([P, NT, 1])
        taken = scratch.take([P, NT, E3])
        taken_before = scratch.take([P, NT, E3])
        c_keep = scratch.take([P, NT, E3])

        s_f3_load = sem("f3_load")
        s_taken = sem("experts_taken")
        s_place = sem("places_counted")
        place_ps = bank(7)[:, 0:NT * E3]

        def l3_ffn_sync(sp):
            sp.wait_ge(s_res, 7 * NT + 1)
            for dst, name in ((f3_router, "f3_router"), (f3_bias, "f3_bias"), (earlier, "earlier")):
                sp.dma_start(dst, A[name]).then_inc(s_f3_load, 16)
            experts_sync(sp, "f3_experts", E3, 0, 2 * (E1 + 1))

        def l3_ffn_gpsimd(pool):
            pool.wait_ge(s_res, 7 * NT + 1)
            pool.memset(all_ones, 1.0).then_inc(s_const, 1)
            router_gpsimd(pool, 8 * B)

        def l3_ffn_scalar(act, turns):
            router_scalar(act, turns, B, 1, c_prob)
            experts_scalar(act, E3, 2 * (E1 + 1))

        def l3_ffn_tensor(pe, turns):
            pe.wait_ge(s_f3_load, 48)
            pe.wait_ge(s_const, 4)
            router_tensor(pe, turns, 6 * B, B, f3_router, EZ, None)
            pe.wait_ge(s_taken, 1)
            pe.matmul(place_ps, all_ones, flat(taken_before), start=True, stop=False)
            pe.matmul(place_ps, earlier, flat(taken), start=False, stop=True).then_inc(s_place, 1)
            pe.wait_ge(s_xall, 2 * B + 1)
            pe.wait_ge(s_kept_places, 1)
            experts_tensor(pe, E3, [5, 4, 4, 4], 2 * (E1 + 1))

        def l3_ffn_vector(dve, st):
            spread = lambda v, n: v.to_broadcast([P, NT, n])
            router_vector(dve, st, 8 * B, 33, B, 1, c_prob, EZ)
            dve.wait_ge(s_f3_load, 48)
            st.done(dve.tensor_tensor(c_biased, c_prob, f3_bias.unsqueeze(1).to_broadcast([P, NT, EZ]), ALU.add))
            for t in range(NT):
                st.mark(dve.max(c_eight[:, t, :], c_biased[:, t, :]))
            st.wait()
            for t in range(NT):
                st.mark(dve.match_replace(out=c_rest[:, t, :], in_to_replace=c_eight[:, t, :],
                                          in_values=c_biased[:, t, :], imm_value=-3e38))
            st.wait()
            st.done(dve.tensor_tensor(c_rest, c_rest, c_biased, ALU.not_equal))
            st.mark(dve.tensor_copy(taken, c_rest[:, :, 0:E3]))
            st.done(dve.memset(taken_before[:, 0, :], 0.0))
            for t in range(NT - 1):
                st.done(dve.tensor_tensor(taken_before[:, t + 1, :], taken_before[:, t, :], taken[:, t, :], ALU.add))
            dve.engine_nop().then_inc(s_taken, 1)
            st.done(dve.tensor_tensor(c_rest, c_rest, c_prob, ALU.mult))
            st.done(dve.tensor_reduce(c_sum[:, :, 0], c_rest, AX, ALU.add))
            st.done(dve.tensor_scalar(c_sum, c_sum, 1e-20, None, ALU.add))
            st.done(dve.reciprocal(c_sum, c_sum))
            st.done(dve.scalar_tensor_tensor(out=c_rest, in0=c_rest, scalar=1.5, in1=spread(c_sum, EZ),
                                             op0=ALU.mult, op1=ALU.mult))
            st.mark(dve.tensor_reduce(c_idle[:, :, 0], c_rest[:, :, E3:EZ], AX, ALU.add))
            dve.wait_ge(s_place, 1)
            dve.tensor_scalar(flat(c_keep), place_ps, float(CAP3), None, ALU.is_lt).then_inc(s_kept_places, 1)
            dve.wait_ge(s_kept_places, 1)
            st.done(dve.tensor_tensor(c_keep, c_keep, c_rest[:, :, 0:E3], ALU.mult))
            st.done(dve.scalar_tensor_tensor(out=weight_of[:, :, 0:E3], in0=spread(c_idle, E3), scalar=1.0,
                                             in1=c_keep, op0=ALU.add, op1=ALU.mult))
            st.done(dve.tensor_scalar(weight_of[:, :, 0:E3], weight_of[:, :, 0:E3], gates[:, 7:8], None, ALU.mult))
            experts_vector(dve, st, E3, 2 * (E1 + 1))

        s_kept_places = sem("places_in_capacity")

        stage_list = [
            dict(sync=l0_attn_sync, gpsimd=l0_attn_gpsimd, scalar=l0_attn_scalar, vector=l0_attn_vector, tensor=l0_attn_tensor),
            dict(sync=l0_ffn_sync, gpsimd=l0_ffn_gpsimd, scalar=l0_ffn_scalar, vector=l0_ffn_vector, tensor=l0_ffn_tensor),
            dict(sync=l1_attn_sync, gpsimd=l1_attn_gpsimd, scalar=l1_attn_scalar, vector=l1_attn_vector, tensor=l1_attn_tensor),
            dict(sync=l1_ffn_sync, gpsimd=l1_ffn_gpsimd, scalar=l1_ffn_scalar, vector=l1_ffn_vector, tensor=l1_ffn_tensor),
            dict(sync=l2_attn_sync, gpsimd=l2_attn_gpsimd, scalar=l2_attn_scalar, vector=l2_attn_vector, tensor=l2_attn_tensor),
            dict(sync=l2_ffn_sync, gpsimd=l2_ffn_gpsimd, scalar=l2_ffn_scalar, vector=l2_ffn_vector, tensor=l2_ffn_tensor),
            dict(sync=l3_attn_sync, gpsimd=l3_attn_gpsimd, scalar=l3_attn_scalar, vector=l3_attn_vector, tensor=l3_attn_tensor),
            dict(sync=l3_ffn_sync, gpsimd=l3_ffn_gpsimd, scalar=l3_ffn_scalar, vector=l3_ffn_vector, tensor=l3_ffn_tensor),
        ]

        block = ctx.enter_context(nc.Block())

        @block.sync
        def _(sp):
            sp.dma_start(gates[:, :], A["gates"]).then_inc(s_load, 16)
            sp.dma_start(ident[:, :], A["ident"]).then_inc(s_load, 16)
            for stage in stage_list:
                stage["sync"](sp)
            sp.wait_ge(s_res, len(stage_list) * NT + 1)
            sp.dma_start(out, x[:, :, :]).then_inc(s_store, 16)
            sp.wait_ge(s_store, 16)

        @block.gpsimd
        def _(pool):
            for signal in (s_shift, s_pt, s_o, s_res, s_pv, s_score, s_ptT, s_hid, s_ht, s_kept, s_fy, s_htT, s_qrT,
                           s_rshift, s_logit, s_xall, s_l2_rot, s_h2):
                pool.sem_inc(signal, 1)
            pool.memset(ones[:, :], 1.0).then_inc(s_const, 1)
            pool.memset(minus_half[:, :], -0.5).then_inc(s_const, 1)
            pool.wait_ge(s_const, 2)
            for stage in stage_list:
                stage["gpsimd"](pool)

        @block.scalar
        def _(act):
            turns = Tally(s_turned)
            act.wait_ge(s_load, 32)
            act.activation(gates[:, :], gates[:, :], ACT.Tanh).then_inc(s_const, 1)
            for stage in stage_list:
                stage["scalar"](act, turns)

        @block.vector
        def _(dve):
            st = Steps(dve, s_dve)
            dve.wait_ge(s_load, 32)
            dve.wait_ge(s_const, 3)
            for n, stage in enumerate(stage_list):
                stage["vector"](dve, st)
                dve.wait_ge(s_res, (n + 1) * NT + 1)

        @block.tensor
        def _(pe):
            turns = Tally(s_turned)
            pe.wait_ge(s_load, 32)
            for stage in stage_list:
                stage["tensor"](pe, turns)


def laid_out(inp):
    f = np.float32

    def chunks(w):
        return w.reshape(-1, P, w.shape[-1]).transpose(1, 0, 2)

    def rows(v):
        return np.broadcast_to(v.reshape(1, -1), (P, v.size))

    a = {}
    a["x"] = inp["x"].reshape(NT, P, D).transpose(1, 0, 2)
    a["gates"] = rows(np.stack([inp["g_xattn"], inp["g_ffn"]], axis=1).reshape(-1))
    a["ident"] = np.eye(P, dtype=f)
    context = inp["ctx_2048"].reshape(CT, D).T
    a["ctxT"] = chunks(context)
    a["ctxT2"] = np.repeat(chunks(context).reshape(P, C, B, 1, SK), 2, axis=3).reshape(P, C, B, P)
    a["l0_w"] = np.stack([chunks(inp["L0_xattn_" + k]) for k in ("Wq", "Wk_img", "Wv_img", "Wo")], axis=1)
    a["l0_rows"] = np.stack([inp["L0_xattn_" + k] for k in ("bq", "bk_img", "bv_img", "bo")])[None]
    a["l0_gain"] = np.stack([rows(inp["L0_xattn_" + k]) for k in ("gq", "gk_img")], axis=1)
    a["head_of"] = np.repeat(np.eye(HB0, dtype=f), HD0, axis=0)
    a["half_of"] = np.repeat(np.eye(2, dtype=f), SK, axis=0)
    a["f0_w"] = np.stack([chunks(inp["L0_ffn_w_gate"]), chunks(inp["L0_ffn_w_up"])], axis=1)
    a["f0_down"] = chunks(inp["L0_ffn_w_down"])
    a["l1_kvc"] = chunks(inp["L1_xattn_W_kvc"])
    a["l1_dq"] = chunks(inp["L1_xattn_W_dq"])
    a["l1_uqT"] = inp["L1_xattn_W_uq"].reshape(QC1, H1, HD1).transpose(2, 1, 0)
    swap = (np.arange(R1) + R1 // 2) % R1
    qr = inp["L1_xattn_W_qr"].reshape(QC1, H1, R1)
    a["l1_qr"] = np.stack([qr, qr[:, :, swap]], axis=1).reshape(QC1, 2, H1 * R1)
    a["l1_uk"] = inp["L1_xattn_W_uk"]
    kr = inp["L1_xattn_W_kr"]
    a["l1_kr"] = np.stack([np.concatenate([w, w], axis=1) for w in (kr, kr[:, swap])], axis=1)
    a["l1_uv"] = inp["L1_xattn_W_uv"]
    a["l1_wo"] = inp["L1_xattn_W_o"].reshape(H1, HD1, D).transpose(1, 0, 2)
    a["seg"] = inp["itok_BxS_0_1023"].reshape(NT, P).T
    half = R1 // 2
    angle = np.arange(S, dtype=f)[:, None] * (f(1.0) / f(10000.0) ** (np.arange(half, dtype=f) / f(half)))
    a["l1_cos_sin"] = np.stack([np.tile(np.cos(angle).T, (4, 1)),
                                np.tile(np.concatenate([-np.sin(angle).T, np.sin(angle).T]), (2, 1))], axis=1).astype(f)
    a["key_at"] = rows(np.arange(SK, dtype=f))
    a["key_last"] = rows(np.arange(SK, dtype=f) + f(LOOKBACK))

    def experts(gate, up, down):
        n = gate.shape[0]
        gu = np.stack([gate.reshape(n, C, P, I1), up.reshape(n, C, P, I1)], axis=3)
        return np.concatenate([gu.transpose(0, 2, 1, 3, 4).reshape(n, P, 2 * D), down], axis=2)

    a["f1_experts"] = experts(*(np.concatenate([inp["L1_ffn_" + k], inp["L1_ffn_s" + k][None]]) for k in ("Wg", "Wu", "Wd")))
    a["f1_router"] = chunks(inp["L1_ffn_Wr"].T)
    a["f1_bias"] = inp["L1_ffn_bias"].reshape(1, E1)
    a["below"] = rows(-np.arange(1, 9, dtype=f))
    swap = (np.arange(HD2) + HD2 // 2) % HD2
    swapped = lambda w: w.reshape(D, H2, HD2)[:, :, swap].reshape(D, D)
    wq, wk, wv, wo = (inp["L2_xattn_" + k] for k in ("Wq", "Wk", "Wv", "Wo"))
    a["l2_w"] = np.stack([chunks(w) for w in (wq, swapped(wq), wk, swapped(wk), wv, wo)], axis=1)
    freqs = np.outer(np.arange(S, dtype=f), f(1.0) / f(10000.0) ** (np.arange(0, HD2, 2, dtype=f) / f(HD2)))
    a["l2_cos"] = np.tile(np.cos(freqs).T, (P // HD2 * 2, 1)).astype(f)
    a["l2_sin"] = np.tile(np.concatenate([-np.sin(freqs).T, np.sin(freqs).T]), (P // HD2, 1)).astype(f)
    a["eight_of"] = np.tile(np.repeat(np.eye(8, dtype=f).reshape(8, 2, 4).transpose(0, 2, 1), HD2, axis=0), (2, 1, 1))
    a["l2_gate"] = rows(inp["L2_xattn_gate"].reshape(-1))
    a["mask"] = inp["mask_Bx1xSxS_fk0"].reshape(NT, P, S).transpose(1, 0, 2)
    a["l2_head_of"] = np.repeat(np.eye(P // HD2, dtype=f), HD2, axis=0)
    a["f2_gate"] = chunks(inp["L2_ffn_gate_w"].T).reshape(P, -1)
    down = np.zeros((-(-I2 // P) * P, D), f)
    down[:I2] = inp["L2_ffn_down_w"].T
    a["f2_down"] = chunks(down).reshape(P, -1)
    a["f2_norm"] = rows(inp["L2_ffn_gate_norm_w"])
    a["f2_dnorm"] = rows(inp["L2_ffn_down_norm_w"])
    a["l3_w"] = np.stack([chunks(inp["L3_xattn_" + k].T) for k in ("W_in", "W_out")], axis=1)
    a["l3_in_bias"] = inp["L3_xattn_b_in"].reshape(C, P).T
    a["l3_out_bias"] = inp["L3_xattn_b_out"].reshape(1, D)
    a["l3_affine"] = np.stack([rows(inp["L3_xattn_" + k]) for k in ("gamma", "beta")], axis=1)
    a["l3_decay"] = rows(inp["L3_xattn_decay"].reshape(1))
    gu = inp["L3_ffn_w_gate_up"]
    a["f3_experts"] = experts(gu[:, :, :I3], gu[:, :, I3:], inp["L3_ffn_w_down"])
    a["f3_router"] = chunks(inp["L3_ffn_w_cls"].T)
    a["f3_bias"] = rows(inp["L3_ffn_bias"])
    a["earlier"] = np.triu(np.ones((P, P), f), 1)
    return {k: np.ascontiguousarray(v) for k, v in a.items()}


def kernel(**inputs):
    from concourse import bacc
    from concourse.bass_utils import run_bass_kernel_spmd

    nc = bacc.Bacc("TRN2", target_bir_lowering=False, num_devices=1)
    arrays = laid_out({k: np.asarray(v) for k, v in inputs.items()})
    A = {k: nc.dram_tensor(f"in_{k}_dram", v.shape, mybir.dt.from_np(v.dtype), kind="ExternalInput").ap()
         for k, v in arrays.items()}
    out = nc.dram_tensor("out_0_dram", (P, NT, D), F32, kind="ExternalOutput").ap()
    flamingo(nc, A, out)
    r = run_bass_kernel_spmd(nc, [{f"in_{k}_dram": v for k, v in arrays.items()}], core_ids=[0])
    return r.results[0]["out_0_dram"].transpose(1, 0, 2).reshape(B, S, D)
```
